# Optimizing a Trainium2 kernel written in Bass

```python
import numpy as np
import jax
import jax.numpy as jnp

def _softmax(x, axis=-1):
    return jax.nn.softmax(x, axis=axis)

def _gelu(x):
    return jax.nn.gelu(x, approximate=True)

def _silu(x):
    return jax.nn.silu(x)

def _sigmoid(x):
    return jax.nn.sigmoid(x)

def _layernorm(x, axis=-1, eps=1e-05):
    m = jnp.mean(x, axis=axis, keepdims=True)
    v = jnp.var(x, axis=axis, keepdims=True)
    return (x - m) / jnp.sqrt(v + eps)

def _scatter_add(tgt, idx, src, axis=0):
    return tgt.at[idx].add(src)

def _segment_sum(src, seg, n):
    return jax.ops.segment_sum(src, seg, n)
kernel_name = 'mk_lm_tower_d2_tok_ids1024_r4_3d9edf'

def setup_inputs(seed: int=0):
    np.random.seed(seed)
    _w = jnp.asarray

    def _rec_inputs():
        import jax
        import jax.numpy as jnp
        _rk = jax.random.key(seed)
        x = jax.random.randint(jax.random.fold_in(_rk, 1), (16, 256), 0, 12564, jnp.int32)
        return x
    x = _rec_inputs()

    def _L0_tok_setup():
        import jax, jax.numpy as jnp
        import numpy as np
        VOCAB = 50257
        NUM_DIM = 256
        BATCH = 4
        SEQ = 1024
        key = jax.random.key(seed)
        k_tok, k_w, k_b = jax.random.split(key, 3)
        tokens = jax.random.randint(k_tok, (BATCH, SEQ), 0, VOCAB)
        weight = jax.random.normal(k_w, (NUM_DIM, VOCAB), dtype=jnp.float32) * 0.02
        bias = jax.random.normal(k_b, (NUM_DIM,), dtype=jnp.float32) * 0.02
        return {'tokens': tokens, 'weight': weight, 'bias': bias}
    _L0_tok_all = _L0_tok_setup()
    _L0_tok_in = {k: v for k, v in _L0_tok_all.items() if k in ('weight', 'bias')}
    del _L0_tok_all

    def _L0_attn_setup():
        import jax, jax.numpy as jnp
        import numpy as np
        import math
        NUM_HEADS = 16
        WINDOW = 128
        EPS = 1e-06

        def _telephone_block(x, g, Wqkv, Wo):
            B, S, D = x.shape
            H, dh, W = (NUM_HEADS, D // NUM_HEADS, WINDOW)
            nb = S // W
            xn = x * jax.lax.rsqrt(jnp.mean(x * x, axis=-1, keepdims=True) + EPS) * g
            qkv = xn @ Wqkv
            q, k, v = jnp.split(qkv, 3, axis=-1)

            def split_heads(t):
                return t.reshape(B, nb, W, H, dh).transpose(0, 3, 1, 2, 4)
            q, k, v = (split_heads(q), split_heads(k), split_heads(v))

            def shift_prev(t):
                return jnp.pad(t[:, :, :-1], ((0, 0), (0, 0), (1, 0), (0, 0), (0, 0)))
            k_ext = jnp.concatenate([shift_prev(k), k], axis=3)
            v_ext = jnp.concatenate([shift_prev(v), v], axis=3)
            scale = 1.0 / math.sqrt(dh)
            scores = jnp.einsum('bhnqd,bhnkd->bhnqk', q, k_ext) * scale
            i = jnp.arange(W)[:, None]
            j = jnp.arange(2 * W)[None, :]
            base = (j > i) & (j <= i + W)
            first = base & (j >= W)
            blk0 = (jnp.arange(nb) == 0)[:, None, None]
            mask = jnp.where(blk0, first[None], base[None])
            scores = jnp.where(mask[None, None], scores, jnp.finfo(scores.dtype).min)
            p = jax.nn.softmax(scores, axis=-1)
            o = jnp.einsum('bhnqk,bhnkd->bhnqd', p, v_ext)
            o = o.transpose(0, 2, 3, 1, 4).reshape(B, S, D)
            h = o @ Wo
            return x + h
        key = jax.random.key(seed)
        k1, k2, k3, k4 = jax.random.split(key, 4)
        B, S, D = (4, 1024, 256)
        x = jax.random.normal(k1, (B, S, D), dtype=jnp.float32)
        g = jnp.ones((D,), dtype=jnp.float32)
        Wqkv = jax.random.normal(k2, (D, 3 * D), dtype=jnp.float32) * 0.02
        Wo = jax.random.normal(k3, (D, D), dtype=jnp.float32) * 0.02
        return {'x': x, 'g': g, 'Wqkv': Wqkv, 'Wo': Wo}
    _L0_attn_all = _L0_attn_setup()
    _L0_attn_in = {k: v for k, v in _L0_attn_all.items() if k in ('g', 'Wqkv', 'Wo')}
    del _L0_attn_all

    def _L0_ffn_setup():
        import jax, jax.numpy as jnp
        import numpy as np
        D_MODEL = 256
        M = 64
        INNER = 16
        key = jax.random.key(seed)
        ks = jax.random.split(key, 9)

        def init(k, shape, fan_in):
            bound = 1.0 / np.sqrt(fan_in)
            return jax.random.uniform(k, shape, jnp.float32, -bound, bound)
        x = jax.random.normal(ks[0], (16, 1024, D_MODEL), dtype=jnp.float32)
        Win = init(ks[1], (D_MODEL, M), D_MODEL)
        bin_ = init(ks[2], (M,), D_MODEL)
        W1 = init(ks[3], (M, INNER), 1)
        b1 = init(ks[4], (M, INNER), 1)
        W2 = init(ks[5], (M, INNER), INNER)
        b2 = init(ks[6], (M,), INNER)
        Wout = init(ks[7], (M, D_MODEL), M)
        bout = init(ks[8], (D_MODEL,), M)
        return {'x': x, 'Win': Win, 'bin_': bin_, 'W1': W1, 'b1': b1, 'W2': W2, 'b2': b2, 'Wout': Wout, 'bout': bout}
    _L0_ffn_all = _L0_ffn_setup()
    _L0_ffn_in = {k: v for k, v in _L0_ffn_all.items() if k in ('Win', 'bin_', 'W1', 'b1', 'W2', 'b2', 'Wout', 'bout')}
    del _L0_ffn_all

    def _L1_attn_setup():
        import jax, jax.numpy as jnp
        import numpy as np
        HEADS = 16
        TILE = 32
        QMAX = 127.0

        def _build_pla(num_intervals=12, dmin=-10.0, dmax=0.0):
            xs = np.linspace(dmin, dmax, 1001)
            ys = np.exp(xs)
            edges = np.linspace(dmin, dmax, num_intervals + 1)
            ms, cs = ([], [])
            for i in range(num_intervals):
                msk = (xs >= edges[i]) & (xs <= edges[i + 1])
                m, c = np.polyfit(xs[msk], ys[msk], 1)
                ms.append(m)
                cs.append(c)
            return (np.asarray(ms, np.float32), np.asarray(cs, np.float32), np.asarray(edges[:-1], np.float32))
        _PLA_M, _PLA_C, _PLA_A = _build_pla()

        def _quant(x, axis=None):
            mx = jnp.max(jnp.abs(x)) if axis is None else jnp.max(jnp.abs(x), axis=axis, keepdims=True)
            scale = mx / QMAX
            scale = jnp.where(scale == 0, jnp.ones_like(scale), scale)
            q = jnp.clip(jnp.round(x / scale), -QMAX, QMAX) * scale
            return x + jax.lax.stop_gradient(q - x)

        def _quant_seq_blocks(x, tile):
            B, H, S, D = x.shape
            xr = x.reshape(B, H, S // tile, tile, D)
            mx = jnp.max(jnp.abs(xr), axis=(0, 1, 3, 4), keepdims=True)
            scale = mx / QMAX
            scale = jnp.where(scale == 0, jnp.ones_like(scale), scale)
            q = jnp.clip(jnp.round(xr / scale), -QMAX, QMAX) * scale
            q = xr + jax.lax.stop_gradient(q - xr)
            return q.reshape(B, H, S, D)

        def _pla_softmax(scores):
            m = jnp.asarray(_PLA_M)
            c = jnp.asarray(_PLA_C)
            a = jnp.asarray(_PLA_A)
            shifted = scores - jnp.max(scores, axis=-1, keepdims=True)
            fscale = 2.0 ** 26
            fx = jnp.clip(jnp.round(shifted * fscale), -2.0 ** 31, 2.0 ** 31 - 1) / fscale
            xc = jnp.clip(fx, -10.0, 0.0)
            idx = jnp.clip(jnp.searchsorted(a, xc, side='right') - 1, 0, a.shape[0] - 1)
            exps = m[idx] * xc + c[idx]
            sm = exps / (jnp.sum(exps, axis=-1, keepdims=True) + 1e-09)
            return _quant(sm)

        def _qlinear(x, W, b):
            return _quant(x) @ _quant(W, axis=1).T + b
        key = jax.random.key(seed)
        ks = jax.random.split(key, 9)
        B, S, H = (16, 128, 256)
        w = lambda k: jax.random.normal(k, (H, H), jnp.float32) * H ** (-0.5)
        bb = lambda k: jax.random.normal(k, (H,), jnp.float32) * 0.01
        return {'hidden_states': jax.random.normal(ks[0], (B, S, H), jnp.float32), 'Wq': w(ks[1]), 'bq': bb(ks[2]), 'Wk': w(ks[3]), 'bk': bb(ks[4]), 'Wv': w(ks[5]), 'bv': bb(ks[6]), 'Wo': w(ks[7]), 'bo': bb(ks[8])}
    _L1_attn_all = _L1_attn_setup()
    _L1_attn_in = {k: v for k, v in _L1_attn_all.items() if k in ('Wq', 'bq', 'Wk', 'bk', 'Wv', 'bv', 'Wo', 'bo')}
    del _L1_attn_all

    def _L1_ffn_setup():
        import jax, jax.numpy as jnp
        import numpy as np
        B, S, D, F, E = (4, 512, 256, 1024, 8)
        LN_EPS = 1e-05
        key = jax.random.key(seed)
        ks = jax.random.split(key, 6)
        sc = 0.02
        return {'x': jax.random.normal(ks[0], (B, S, D), dtype=jnp.float32), 'Wr': jax.random.normal(ks[1], (D, E), dtype=jnp.float32) * sc, 'br': jnp.zeros((E,), jnp.float32), 'ln_g': jnp.ones((D,), jnp.float32), 'ln_b': jnp.zeros((D,), jnp.float32), 'W1': jax.random.normal(ks[2], (E, D, F), dtype=jnp.float32) * sc, 'b1': jnp.zeros((E, F), jnp.float32), 'W2': jax.random.normal(ks[3], (E, F, D), dtype=jnp.float32) * sc, 'b2': jnp.zeros((E, D), jnp.float32)}
    _L1_ffn_all = _L1_ffn_setup()
    _L1_ffn_in = {k: v for k, v in _L1_ffn_all.items() if k in ('Wr', 'br', 'ln_g', 'ln_b', 'W1', 'b1', 'W2', 'b2')}
    del _L1_ffn_all
    return {'x': x, 'L0_tok_weight': _L0_tok_in['weight'], 'L0_tok_bias': _L0_tok_in['bias'], 'L0_attn_g': _L0_attn_in['g'], 'L0_attn_Wqkv': _L0_attn_in['Wqkv'], 'L0_attn_Wo': _L0_attn_in['Wo'], 'L0_ffn_Win': _L0_ffn_in['Win'], 'L0_ffn_bin_': _L0_ffn_in['bin_'], 'L0_ffn_W1': _L0_ffn_in['W1'], 'L0_ffn_b1': _L0_ffn_in['b1'], 'L0_ffn_W2': _L0_ffn_in['W2'], 'L0_ffn_b2': _L0_ffn_in['b2'], 'L0_ffn_Wout': _L0_ffn_in['Wout'], 'L0_ffn_bout': _L0_ffn_in['bout'], 'L1_attn_Wq': _L1_attn_in['Wq'], 'L1_attn_bq': _L1_attn_in['bq'], 'L1_attn_Wk': _L1_attn_in['Wk'], 'L1_attn_bk': _L1_attn_in['bk'], 'L1_attn_Wv': _L1_attn_in['Wv'], 'L1_attn_bv': _L1_attn_in['bv'], 'L1_attn_Wo': _L1_attn_in['Wo'], 'L1_attn_bo': _L1_attn_in['bo'], 'L1_ffn_Wr': _L1_ffn_in['Wr'], 'L1_ffn_br': _L1_ffn_in['br'], 'L1_ffn_ln_g': _L1_ffn_in['ln_g'], 'L1_ffn_ln_b': _L1_ffn_in['ln_b'], 'L1_ffn_W1': _L1_ffn_in['W1'], 'L1_ffn_b1': _L1_ffn_in['b1'], 'L1_ffn_W2': _L1_ffn_in['W2'], 'L1_ffn_b2': _L1_ffn_in['b2']}

def reference(x, L0_tok_weight, L0_tok_bias, L0_attn_g, L0_attn_Wqkv, L0_attn_Wo, L0_ffn_Win, L0_ffn_bin_, L0_ffn_W1, L0_ffn_b1, L0_ffn_W2, L0_ffn_b2, L0_ffn_Wout, L0_ffn_bout, L1_attn_Wq, L1_attn_bq, L1_attn_Wk, L1_attn_bk, L1_attn_Wv, L1_attn_bv, L1_attn_Wo, L1_attn_bo, L1_ffn_Wr, L1_ffn_br, L1_ffn_ln_g, L1_ffn_ln_b, L1_ffn_W1, L1_ffn_b1, L1_ffn_W2, L1_ffn_b2):
    import jax
    import jax.numpy as jnp

    def _L0_tok_ref(tokens, weight, bias):
        import jax, jax.numpy as jnp
        import numpy as np
        VOCAB = 50257
        NUM_DIM = 256
        BATCH = 4
        SEQ = 1024
        table = weight.T
        return jnp.take(table, tokens, axis=0) + bias

    def _L0_attn_ref(x, g, Wqkv, Wo):
        import jax, jax.numpy as jnp
        import numpy as np
        import math
        NUM_HEADS = 16
        WINDOW = 128
        EPS = 1e-06

        def _telephone_block(x, g, Wqkv, Wo):
            B, S, D = x.shape
            H, dh, W = (NUM_HEADS, D // NUM_HEADS, WINDOW)
            nb = S // W
            xn = x * jax.lax.rsqrt(jnp.mean(x * x, axis=-1, keepdims=True) + EPS) * g
            qkv = xn @ Wqkv
            q, k, v = jnp.split(qkv, 3, axis=-1)

            def split_heads(t):
                return t.reshape(B, nb, W, H, dh).transpose(0, 3, 1, 2, 4)
            q, k, v = (split_heads(q), split_heads(k), split_heads(v))

            def shift_prev(t):
                return jnp.pad(t[:, :, :-1], ((0, 0), (0, 0), (1, 0), (0, 0), (0, 0)))
            k_ext = jnp.concatenate([shift_prev(k), k], axis=3)
            v_ext = jnp.concatenate([shift_prev(v), v], axis=3)
            scale = 1.0 / math.sqrt(dh)
            scores = jnp.einsum('bhnqd,bhnkd->bhnqk', q, k_ext) * scale
            i = jnp.arange(W)[:, None]
            j = jnp.arange(2 * W)[None, :]
            base = (j > i) & (j <= i + W)
            first = base & (j >= W)
            blk0 = (jnp.arange(nb) == 0)[:, None, None]
            mask = jnp.where(blk0, first[None], base[None])
            scores = jnp.where(mask[None, None], scores, jnp.finfo(scores.dtype).min)
            p = jax.nn.softmax(scores, axis=-1)
            o = jnp.einsum('bhnqk,bhnkd->bhnqd', p, v_ext)
            o = o.transpose(0, 2, 3, 1, 4).reshape(B, S, D)
            h = o @ Wo
            return x + h
        return _telephone_block(x, g, Wqkv, Wo)

    def _L0_ffn_ref(x, Win, bin_, W1, b1, W2, b2, Wout, bout):
        import jax, jax.numpy as jnp
        import numpy as np
        D_MODEL = 256
        M = 64
        INNER = 16
        s = jnp.einsum('btd,dm->btm', x, Win) + bin_
        h = jax.nn.relu(s[..., None] * W1 + b1)
        g = jnp.einsum('btmh,mh->btm', h, W2) + b2
        out = jnp.einsum('btm,md->btd', g, Wout) + bout
        return out

    def _L1_attn_ref(hidden_states, Wq, bq, Wk, bk, Wv, bv, Wo, bo):
        import jax, jax.numpy as jnp
        import numpy as np
        HEADS = 16
        TILE = 32
        QMAX = 127.0

        def _build_pla(num_intervals=12, dmin=-10.0, dmax=0.0):
            xs = np.linspace(dmin, dmax, 1001)
            ys = np.exp(xs)
            edges = np.linspace(dmin, dmax, num_intervals + 1)
            ms, cs = ([], [])
            for i in range(num_intervals):
                msk = (xs >= edges[i]) & (xs <= edges[i + 1])
                m, c = np.polyfit(xs[msk], ys[msk], 1)
                ms.append(m)
                cs.append(c)
            return (np.asarray(ms, np.float32), np.asarray(cs, np.float32), np.asarray(edges[:-1], np.float32))
        _PLA_M, _PLA_C, _PLA_A = _build_pla()

        def _quant(x, axis=None):
            mx = jnp.max(jnp.abs(x)) if axis is None else jnp.max(jnp.abs(x), axis=axis, keepdims=True)
            scale = mx / QMAX
            scale = jnp.where(scale == 0, jnp.ones_like(scale), scale)
            q = jnp.clip(jnp.round(x / scale), -QMAX, QMAX) * scale
            return x + jax.lax.stop_gradient(q - x)

        def _quant_seq_blocks(x, tile):
            B, H, S, D = x.shape
            xr = x.reshape(B, H, S // tile, tile, D)
            mx = jnp.max(jnp.abs(xr), axis=(0, 1, 3, 4), keepdims=True)
            scale = mx / QMAX
            scale = jnp.where(scale == 0, jnp.ones_like(scale), scale)
            q = jnp.clip(jnp.round(xr / scale), -QMAX, QMAX) * scale
            q = xr + jax.lax.stop_gradient(q - xr)
            return q.reshape(B, H, S, D)

        def _pla_softmax(scores):
            m = jnp.asarray(_PLA_M)
            c = jnp.asarray(_PLA_C)
            a = jnp.asarray(_PLA_A)
            shifted = scores - jnp.max(scores, axis=-1, keepdims=True)
            fscale = 2.0 ** 26
            fx = jnp.clip(jnp.round(shifted * fscale), -2.0 ** 31, 2.0 ** 31 - 1) / fscale
            xc = jnp.clip(fx, -10.0, 0.0)
            idx = jnp.clip(jnp.searchsorted(a, xc, side='right') - 1, 0, a.shape[0] - 1)
            exps = m[idx] * xc + c[idx]
            sm = exps / (jnp.sum(exps, axis=-1, keepdims=True) + 1e-09)
            return _quant(sm)

        def _qlinear(x, W, b):
            return _quant(x) @ _quant(W, axis=1).T + b
        B, S, Hd = hidden_states.shape
        d = Hd // HEADS
        split = lambda t: t.reshape(B, S, HEADS, d).transpose(0, 2, 1, 3)
        q = split(_qlinear(hidden_states, Wq, bq))
        k = split(_qlinear(hidden_states, Wk, bk))
        v = split(_qlinear(hidden_states, Wv, bv))
        qb = _quant_seq_blocks(q, TILE)
        kb = _quant_seq_blocks(k, TILE)
        scores = jnp.einsum('bhqd,bhkd->bhqk', qb, kb) * d ** (-0.5)
        probs = _pla_softmax(scores)
        ctx = jnp.einsum('bhqk,bhkd->bhqd', probs, _quant(v))
        ctx = ctx.transpose(0, 2, 1, 3).reshape(B, S, Hd)
        return _qlinear(ctx, Wo, bo)

    def _L1_ffn_ref(x, Wr, br, ln_g, ln_b, W1, b1, W2, b2):
        import jax, jax.numpy as jnp
        import numpy as np
        B, S, D, F, E = (4, 512, 256, 1024, 8)
        LN_EPS = 1e-05
        tokens_shape = x.shape[:-1]
        xt = x.reshape(-1, x.shape[-1])
        router_logits = xt @ Wr + br
        router_probs = jax.nn.softmax(router_logits, axis=-1)
        gates = jnp.max(router_probs, axis=-1, keepdims=True)
        idx = jnp.argmax(router_probs, axis=-1)
        onehot = jax.nn.one_hot(idx, E, dtype=xt.dtype)
        mu = jnp.mean(xt, axis=-1, keepdims=True)
        var = jnp.mean(jnp.square(xt - mu), axis=-1, keepdims=True)
        xn = (xt - mu) * jax.lax.rsqrt(var + LN_EPS) * ln_g + ln_b
        h = jnp.einsum('te,td,edf->tf', onehot, xn, W1) + b1[idx]
        h = jax.nn.relu(h)
        y = jnp.einsum('te,tf,efd->td', onehot, h, W2) + b2[idx]
        y = y * gates
        return y.reshape(tokens_shape + (y.shape[-1],))
    h = _L0_tok_ref(x, L0_tok_weight, L0_tok_bias)
    h = h + _L0_attn_ref(_layernorm(h, axis=-1), L0_attn_g, L0_attn_Wqkv, L0_attn_Wo)
    h = h + _L0_ffn_ref(_layernorm(h, axis=-1), L0_ffn_Win, L0_ffn_bin_, L0_ffn_W1, L0_ffn_b1, L0_ffn_W2, L0_ffn_b2, L0_ffn_Wout, L0_ffn_bout)
    h = h + _L1_attn_ref(_layernorm(h, axis=-1), L1_attn_Wq, L1_attn_bq, L1_attn_Wk, L1_attn_bk, L1_attn_Wv, L1_attn_bv, L1_attn_Wo, L1_attn_bo)
    h = h + _L1_ffn_ref(_layernorm(h, axis=-1), L1_ffn_Wr, L1_ffn_br, L1_ffn_ln_g, L1_ffn_ln_b, L1_ffn_W1, L1_ffn_b1, L1_ffn_W2, L1_ffn_b2)
    return h

_drawn_inputs = setup_inputs


def setup_inputs(seed=0):
    import zlib

    import numpy as np

    out = dict(_drawn_inputs(seed))
    spreads = {'L0_attn_g': (1.0, 0.6),
     'L1_ffn_br': (0.0, 0.561),
     'L1_ffn_ln_g': (1.0, 0.6),
     'L1_ffn_ln_b': (0.0, 0.8),
     'L1_ffn_b1': (0.0, 0.8),
     'L1_ffn_b2': (0.0, 0.48)}
    factors = {'L0_ffn_bin_': 5.616,
     'L1_attn_bq': 32.623,
     'L1_attn_bk': 44.843,
     'L1_attn_bv': 5.785,
     'L1_attn_bo': 6.976,
     'L1_ffn_W1': 2.743}
    for name, (base, spread) in spreads.items():
        noise = np.random.default_rng([zlib.crc32(name.encode()), seed]).standard_normal(out[name].shape)
        drawn = base * np.exp(spread * noise) if base else spread * noise
        out[name] = jnp.asarray(drawn.astype(out[name].dtype))
    for name, factor in factors.items():
        out[name] = (out[name] * factor).astype(out[name].dtype)
    return out
```

```python
from contextlib import ExitStack

import numpy as np

import concourse.bass as bass
from concourse import mybir

F32 = mybir.dt.float32
BF16 = mybir.dt.bfloat16
I32 = mybir.dt.int32
U32 = mybir.dt.uint32
I16 = mybir.dt.int16
ALU = mybir.AluOpType
ACT = mybir.ActivationFunctionType
AX = mybir.AxisListType
RMAX = bass.bass_isa.ReduceOp.max
ds = bass.ds

P = 128
NB, S, D = 16, 256, 256
NT = NB * S // P
KD = D // P
H, DH = 16, 16
NBLK = 8
M_UNITS, INNER = 64, 16
NE, FF = 8, 1024
QMAX = 127.0
NEG = -1e30
VA = DH + 1
XT = NT + NE - 1
SPLIT_Q = (0, 0, 1, 0, 2, 1)
SPLIT_K = (0, 1, 0, 2, 0, 1)


def pla_table():
    xs = np.linspace(-10.0, 0.0, 1001)
    ys = np.exp(xs)
    edges = np.linspace(-10.0, 0.0, 13)
    ms, cs = [], []
    for i in range(12):
        inside = (xs >= edges[i]) & (xs <= edges[i + 1])
        a, b = np.polyfit(xs[inside], ys[inside], 1)
        ms.append(float(a))
        cs.append(float(b))
    return ms, cs


def stage_semaphores(nc, ctx):
    taken = []

    def give_back():
        nc.clear_and_free_semaphores(taken)
        nc.all_engine_barrier()

    def sem(name):
        taken.append(nc.alloc_semaphore(name))
        return taken[-1]

    ctx.callback(give_back)
    return sem


class Link:

    def __init__(self, eng, sem):
        self.eng, self.sem, self.n, self.base = eng, sem, 0, None

    def loop(self, turn, per_turn):
        self.start, self.per_turn = self.n, per_turn
        self.base = turn * per_turn + self.n
        self.n = 0

    def end(self, turns):
        assert self.n == self.per_turn, self.n
        self.n = self.start + turns * self.per_turn
        self.base = None

    def __call__(self, ins):
        ins.then_inc(self.sem, 1)
        self.n += 1
        self.eng.wait_ge(self.sem, self.n if self.base is None else self.base + self.n)


class Core:
    pass


def rstd_vector(dve, link, c, eps, sqrt_asked, sqrt_done, asks):
    st, a, b = c.stats, c.small[:, 0, :], c.small[:, 1, :]
    link(dve.tensor_tensor(a, st[:, :, 1], st[:, :, 4], ALU.add))
    link(dve.tensor_scalar(c.mean[:, :], a, 0.5, None, ALU.mult))
    link(dve.tensor_tensor(a, st[:, :, 1], st[:, :, 4], ALU.subtract))
    link(dve.tensor_tensor(a, a, a, ALU.mult))
    link(dve.tensor_tensor(b, st[:, :, 2], st[:, :, 5], ALU.add))
    link(dve.tensor_scalar(b, b, 1.0 / D, None, ALU.mult))
    link(dve.scalar_tensor_tensor(out=c.var[:, :], in0=a, scalar=0.25, in1=b, op0=ALU.mult, op1=ALU.add))
    link(dve.tensor_scalar(c.veps[:, :], c.var[:, :], eps, None, ALU.add))
    root(dve, link, c, c.rstd, sqrt_asked, sqrt_done, asks)


def root(dve, link, c, out, sqrt_asked, sqrt_done, asks):
    b = c.small[:, 1, :]
    dve.sem_inc(sqrt_asked, 1)
    dve.wait_ge(sqrt_done, asks)
    link(dve.reciprocal(out[:, :], c.sd[:, :]))
    link(dve.tensor_tensor(b, out[:, :], out[:, :], ALU.mult))
    link(dve.tensor_tensor(b, b, c.veps[:, :], ALU.mult))
    link(dve.tensor_scalar(b, b, -0.5, 1.5, ALU.mult, ALU.add))
    link(dve.tensor_tensor(out[:, :], out[:, :], b, ALU.mult))


def root_scalar(act, c, sqrt_asked, sqrt_done, asks):
    act.wait_ge(sqrt_asked, asks)
    act.activation(c.sd[:, :], c.veps[:, :], ACT.Sqrt).then_inc(sqrt_done, 1)


def stage_setup(nc, c):
    with ExitStack() as ctx:
        sb = lambda name, shape, dt: ctx.enter_context(nc.sbuf_tensor(name, shape, dt))
        sem = stage_semaphores(nc, ctx)
        idx = sb("idx", [P, NT], I32)
        tok_bias = sb("tok_bias", [P, D], F32)
        gcol = sb("gcol", [P, KD], F32)
        ones = sb("ones_tmp", [P, 2048], F32)
        onesb = sb("onesb_tmp", [P, 256], BF16)
        w2col = sb("w2col", [P, NBLK], F32)
        wl1 = sb("wl1", [P, 4, KD, D], F32)
        wi = sb("wi", [P, 4, KD, D], I16)
        wb = sb("wb", [P, 4, KD, D], BF16)
        wa = sb("wa", [P, 8], F32)
        wz = sb("wz", [P, 8], F32)
        winv = sb("winv", [P, 8], F32)
        wrow = sb("wrow", [P, 4, P], F32)
        zero = sb("zero", [P, D], F32)
        pw = ctx.enter_context(nc.psum_tensor("pw", [P, 4, KD, 2 * D], BF16))
        pr = ctx.enter_context(nc.psum_tensor("pr", [P, 2, D], F32))
        idx_in, bias_in, g_in, w1_in, w_in = (sem(n) for n in ("idx_in", "bias_in", "g_in", "lw_in", "w_in"))
        rows_in = [sem(f"rows_in{i}") for i in range(4)]
        zero_set, zero_out = sem("zero_set"), sem("zero_out")
        pool_own, dve_own = sem("pool_own0"), sem("dve_own0")
        consts_set, wq_ready, wT, wT_out, wr_ready, wr, masked = (
            sem(n) for n in ("consts_set", "wq_ready", "wT", "wT_out", "wr_ready", "wr", "w2_masked"))
        block = ctx.enter_context(nc.Block())
        i = c.ins

        @block.sync
        def _(sp):
            sp.dma_start(idx[:, :], i["x"]).then_inc(idx_in, 16)
            sp.dma_start(tok_bias[:, :], i["L0_tok_bias"].partition_broadcast(P)).then_inc(bias_in, 16)
            for n, w in enumerate(("Wq", "Wk", "Wv", "Wo")):
                sp.dma_start(wl1[:, n], i[f"L1_attn_{w}"].rearrange("(m p) i -> p m i", p=P)).then_inc(w1_in, 16)
            sp.dma_start(gcol[:, :], i["L0_attn_g"]).then_inc(g_in, 16)
            sp.dma_start(c.wqkv[:, :, :], i["L0_attn_Wqkv"].rearrange("(k p) n -> p k n", p=P)).then_inc(g_in, 16)
            sp.dma_start(w2col[:, :], i["L0_ffn_W2"]).then_inc(g_in, 16)
            sp.dma_start(c.wo0[:, :, :], i["L0_attn_Wo"].rearrange("(k p) n -> p k n", p=P)).then_inc(w_in, 16)
            sp.dma_start(c.win[:, :, :], i["L0_ffn_Win"].rearrange("(k p) n -> p k n", p=P)).then_inc(w_in, 16)
            sp.dma_start(c.w1col[:, :], i["L0_ffn_W1"]).then_inc(w_in, 16)
            sp.dma_start(c.b1col[:, :], i["L0_ffn_b1"]).then_inc(w_in, 16)
            sp.dma_start(c.bin[:, :], i["L0_ffn_bin_"].rearrange("(p a) -> p a", a=1)).then_inc(w_in, 16)
            sp.dma_start(c.b2u[:, :], i["L0_ffn_b2"].rearrange("(p a) -> p a", a=1)).then_inc(w_in, 16)
            sp.dma_start(c.wout[0:M_UNITS, :], i["L0_ffn_Wout"]).then_inc(w_in, 16)
            sp.dma_start(c.wout[M_UNITS:M_UNITS + 1, :], i["L0_ffn_bout"].rearrange("(a n) -> a n", a=1))\
                .then_inc(w_in, 16)
            sp.dma_start(c.bqk[:, 0:2], i["L1_attn_bq"]).then_inc(w_in, 16)
            sp.dma_start(c.bqk[:, 2:4], i["L1_attn_bk"]).then_inc(w_in, 16)
            sp.dma_start(c.bv[:, :], i["L1_attn_bv"].partition_broadcast(P)).then_inc(w_in, 16)
            sp.dma_start(c.bo[:, :], i["L1_attn_bo"].partition_broadcast(P)).then_inc(w_in, 16)
            sp.dma_start(c.wr[:, :, :], i["L1_ffn_Wr"].rearrange("(k p) n -> p k n", p=P)).then_inc(w_in, 16)
            sp.dma_start(c.br[:, :], i["L1_ffn_br"].partition_broadcast(P)).then_inc(w_in, 16)
            sp.dma_start(c.ln_g[:, :], i["L1_ffn_ln_g"].partition_broadcast(P)).then_inc(w_in, 16)
            sp.dma_start(c.ln_b[:, :], i["L1_ffn_ln_b"].partition_broadcast(P)).then_inc(w_in, 16)
            sp.wait_ge(zero_set, 1)
            for t in range(XT):
                sp.dma_start(c.sorted_x[t * P:(t + 1) * P, :], zero[:, :]).then_inc(zero_out, 16)
            sp.wait_ge(w_in, 16 * 16)
            sp.wait_ge(zero_out, 16 * XT)

        @block.gpsimd
        def _(pool):
            link = Link(pool, pool_own)
            pool.wait_ge(idx_in, 16)
            for t in range(NT):
                pool.indirect_dma_start(
                    out=c.h[:, t, :], out_offset=None, in_=i["table"],
                    in_offset=bass.IndirectOffsetOnAxis(ap=idx[:, t:t + 1], axis=0)).then_inc(rows_in[t // 8], 16)
            link(pool.memset(ones[:, :], 1.0))
            link(pool.memset(onesb[:, :], 0.0))
            link(pool.memset(c.ident[:, :], 0.0))
            link(pool.memset(c.sel[:, :, :], 0.0))
            pick = lambda out, in_, op, fill, base, cm, pattern: link(pool.affine_select(
                out=out, in_=in_, compare_op=op, fill=fill, base=base, channel_multiplier=cm, pattern=pattern))
            pick(c.ident[:, :], c.ident[:, :], ALU.not_equal, 1.0, 0, 1, [[-1, P]])
            link(pool.tensor_copy(c.identb[:, :], c.ident[:, :]))
            zb = onesb[:, 0:P]
            pick(c.mask_qk[:, 0, :], zb, ALU.is_ge, NEG, 0, 1, [[-1, P]])
            pick(c.mask_qk[:, 1, :], zb, ALU.is_gt, NEG, 0, -1, [[1, P]])
            pick(c.mask_qk[:, 2, :], zb, ALU.is_ge, NEG, 0, 1, [[-1, P]])
            pick(c.mask_kq[:, 0, :], zb, ALU.is_ge, NEG, 0, -1, [[1, P]])
            pick(c.mask_kq[:, 1, :], zb, ALU.is_gt, NEG, 0, 1, [[-1, P]])
            for x in range(4):
                cut = slice(x * P, (x + 1) * P)
                pool.tensor_copy(c.mask4[:, 0, cut], c.mask_qk[:, 0, :])
                pool.tensor_copy(c.mask4[:, 1, cut], c.mask_qk[:, 1 + x % 2, :])
                pool.tensor_copy(c.mask4[:, 2, cut], c.mask_kq[:, x % 2, :])
                link(pool.tensor_copy(c.mask4[:, 3, cut], c.mask_kq[:, 0, :]))
            for part in range(3):
                pick(c.sel[:, :, :], c.sel[:, :, :], ALU.not_equal, 1.0, -H * part, 1, [[-1, H], [0, P]])
            sp_, on = c.spread[:, :, :], ones[0:M_UNITS, 0:1024].rearrange("p (j q) -> p j q", j=NBLK)
            pick(sp_, on, ALU.is_ge, 0.0, 0, -INNER, [[P, NBLK], [1, P]])
            pick(sp_, sp_, ALU.is_ge, 0.0, INNER - 1, INNER, [[-P, NBLK], [-1, P]])
            wm, on = c.w2m[:, :, :], ones[:, 0:512].rearrange("p (j m) -> p j m", j=NBLK)
            pick(wm, on, ALU.is_ge, 0.0, 0, 1, [[P, NBLK], [-INNER, M_UNITS]])
            pick(wm, wm, ALU.is_ge, 0.0, INNER - 1, -1, [[-P, NBLK], [INNER, M_UNITS]])
            pool.sem_inc(consts_set, 1)

        @block.vector
        def _(dve):
            link = Link(dve, dve_own)
            dve.memset(zero[:, :], 0.0).then_inc(zero_set, 1)
            dve.wait_ge(w1_in, 64)
            w8 = wl1[:, :, :, :].rearrange("p n m i -> p (n m) i")
            link(dve.tensor_reduce(wa[:, :], w8, AX.X, ALU.max, apply_absolute_value=True))
            link(dve.tensor_scalar(wa[:, :], wa[:, :], 1.0 / QMAX, None, ALU.mult))
            link(dve.tensor_scalar(wz[:, :], wa[:, :], 0.0, None, ALU.is_equal))
            link(dve.tensor_tensor(c.wscale[:, :], wa[:, :], wz[:, :], ALU.add))
            link(dve.reciprocal(winv[:, :], c.wscale[:, :]))
            for n in range(8):
                link(dve.tensor_scalar(wi[:, n // 2, n % 2, :], wl1[:, n // 2, n % 2, :], winv[:, n:n + 1], None,
                                       ALU.mult))
            dve.tensor_copy(wb[:, :, :, :], wi[:, :, :, :]).then_inc(wq_ready, 1)
            dve.wait_ge(consts_set, 1)
            for n in range(4):
                t = dve.tensor_scalar(wrow[:, n, :], ones[:, 0:P], c.wscale[:, 4 + n:5 + n], None, ALU.mult)
            t.then_inc(wr_ready, 1)
            dve.wait_ge(g_in, 48)
            for k in range(KD):
                link(dve.tensor_scalar(c.wqkv[:, k, :], c.wqkv[:, k, :], gcol[:, k:k + 1], None, ALU.mult))
            for j in range(NBLK):
                link(dve.tensor_scalar(c.w2m[:, j, :], c.w2m[:, j, :], w2col[:, j:j + 1], None, ALU.mult))
            dve.wait_ge(bias_in, 16)
            for t in range(NT):
                if t % 8 == 0:
                    dve.wait_ge(rows_in[t // 8], 16 * 8)
                link(dve.tensor_tensor(c.h[:, t, :], c.h[:, t, :], tok_bias[:, :], ALU.add))
                dve.bn_stats(c.stats[:, t, :], c.h[:, t, :])
            dve.wait_ge(wT, 1)
            dve.tensor_copy(c.wT[:, :, :, :], pw[:, :, :, 0:D])
            dve.wait_ge(wr, 1)
            dve.tensor_copy(c.wvo[:, :, :], pr[:, :, :])

        @block.tensor
        def _(pe):
            pe.wait_ge(wq_ready, 1)
            pe.wait_ge(consts_set, 1)
            for n in range(4):
                for m in range(KD):
                    for k in range(KD):
                        t = pe.transpose(pw[:, n, k, m * P:(m + 1) * P], wb[:, n, m, k * P:(k + 1) * P],
                                         c.identb[:, :])
            t.then_inc(wT, 1)
            pe.wait_ge(wr_ready, 1)
            for n in range(4):
                t = pe.matmul(pr[:, n // 2, (n % 2) * P:(n % 2 + 1) * P], wrow[:, n, :], c.ident[:, :],
                              start=True, stop=True)
            t.then_inc(wr, 1)


def last(pair, par, turn):
    return pair[1 - par], turn + par


def stage_l0_project(nc, c):
    with ExitStack() as ctx:
        sb = lambda name, shape, dt: ctx.enter_context(nc.sbuf_tensor(name, shape, dt))
        sem = stage_semaphores(nc, ctx)
        pair = lambda name: [sem(name + "_a"), sem(name + "_b")]
        xn = sb("xn", [P, 2, 2, D], F32)
        xT = sb("xT", [P, 2, KD, S], F32)
        rest = sb("rest", [P, 2, 4, S], F32)
        parts = sb("parts", [P, 2, 3, 4, S], BF16)
        rall, rp1, mr = sb("rall", [P, NT], F32), sb("rp1", [P, NT], F32), sb("mr", [P, NT], F32)
        pT = ctx.enter_context(nc.psum_tensor("pT", [P, 2, KD, S], F32))
        pqk = ctx.enter_context(nc.psum_tensor("pqk", [P, 2, 4, S], F32))
        pv = ctx.enter_context(nc.psum_tensor("pv", [P, 2, 2, D], F32))
        own, sqa, sqd = sem("own1"), sem("sqa1"), sem("sqd1")
        x_ready, xT_done, xT_out, qk_done, v_done, v_out, hi_out, mid_in, mid_out, low_out, stored = (
            pair(n) for n in ("x_ready", "xT_done", "xT_out", "qk_done", "v_done", "v_out", "hi_out", "mid_in",
                              "mid_out", "low_out", "stored"))
        block = ctx.enter_context(nc.Block())

        @block.vector
        def _(dve):
            link = Link(dve, own)
            rstd_vector(dve, link, c, 1e-5, sqa, sqd, 1)
            link(dve.tensor_tensor(c.veps[:, :], c.rstd[:, :], c.rstd[:, :], ALU.mult))
            link(dve.tensor_tensor(c.veps[:, :], c.veps[:, :], c.var[:, :], ALU.mult))
            link(dve.tensor_scalar(c.veps[:, :], c.veps[:, :], 1e-6, None, ALU.add))
            root(dve, link, c, rall, sqa, sqd, 2)
            link(dve.tensor_tensor(rall[:, :], rall[:, :], c.rstd[:, :], ALU.mult))
            link(dve.tensor_scalar(rp1[:, :], c.rstd[:, :], 1.0, None, ALU.add))
            link(dve.tensor_tensor(mr[:, :], c.mean[:, :], c.rstd[:, :], ALU.mult))

            def normalise(b, par, turn):
                dve.wait_ge(xT_done[par], turn)
                for j in range(2):
                    t = b * 2 + j
                    ins = dve.tensor_scalar(xn[:, par, j, :], c.h[:, ds(t, 1), :], c.mean[:, ds(t, 1)],
                                            rall[:, ds(t, 1)], ALU.subtract, ALU.mult)
                ins.then_inc(x_ready[par], 1)
                for j in range(2):
                    t = b * 2 + j
                    dve.tensor_scalar(c.h[:, ds(t, 1), :], c.h[:, ds(t, 1), :], rp1[:, ds(t, 1)],
                                      mr[:, ds(t, 1)], ALU.mult, ALU.subtract)

            with dve.Fori(0, NB // 2) as turn:
                for par in range(2):
                    normalise(turn * 2 + par, par, turn)
                for par in range(2):
                    dve.wait_ge(hi_out[par], turn + 1)
                    dve.tensor_tensor(rest[:, par], pqk[:, par], parts[:, par, 0], ALU.subtract)\
                        .then_inc(mid_in[par], 1)
                    dve.wait_ge(mid_out[par], turn + 1)
                    dve.tensor_tensor(parts[:, par, 2], rest[:, par], parts[:, par, 1], ALU.subtract)\
                        .then_inc(low_out[par], 1)

        @block.scalar
        def _(act):
            root_scalar(act, c, sqa, sqd, 1)
            root_scalar(act, c, sqa, sqd, 2)
            with act.Fori(0, NB // 2) as turn:
                for par in range(2):
                    act.wait_ge(xT_done[par], turn + 1)
                    act.activation(xT[:, par], pT[:, par], ACT.Copy).then_inc(xT_out[par], 1)
                for par in range(2):
                    act.wait_ge(qk_done[par], turn + 1)
                    act.wait_ge(stored[par], turn * 16)
                    act.activation(parts[:, par, 0], pqk[:, par], ACT.Copy).then_inc(hi_out[par], 1)
                    act.wait_ge(v_done[par], turn + 1)
                    for j in range(2):
                        t = turn * 4 + par * 2 + j
                        ins = act.activation(c.vaug[:, ds(t, 1), :, 0:DH],
                                             pv[:, par, j, :].rearrange("p (a h d) -> p a h d", a=1, h=H), ACT.Copy)
                    ins.then_inc(v_out[par], 1)
                    act.wait_ge(mid_in[par], turn + 1)
                    act.activation(parts[:, par, 1], rest[:, par], ACT.Copy).then_inc(mid_out[par], 1)

        @block.gpsimd
        def _(pool):
            pool.memset(c.vaug[:, :, :, DH:VA], 1.0)

        @block.tensor
        def _(pe):
            with pe.Fori(0, NB // 2) as turn:
                for par in range(2):
                    pe.wait_ge(x_ready[par], turn + 1)
                    pe.wait_ge(xT_out[par], turn)
                    for j in range(2):
                        for k in range(KD):
                            ins = pe.transpose(pT[:, par, k, j * P:(j + 1) * P], xn[:, par, j, k * P:(k + 1) * P],
                                               c.ident[:, :])
                    ins.then_inc(xT_done[par], 1)
                for par in range(2):
                    pe.wait_ge(xT_out[par], turn + 1)
                    pe.wait_ge(mid_in[par], turn)
                    for m in range(4):
                        for k in range(KD):
                            ins = pe.matmul(pqk[:, par, m, :], c.wqkv[:, k, m * P:(m + 1) * P], xT[:, par, k, :],
                                            start=(k == 0), stop=(k == KD - 1))
                    ins.then_inc(qk_done[par], 1)
                    pe.wait_ge(v_out[par], turn)
                    for j in range(2):
                        for k in range(KD):
                            ins = pe.matmul(pv[:, par, j, :], xT[:, par, k, j * P:(j + 1) * P],
                                            c.wqkv[:, k, 2 * D:3 * D], start=(k == 0), stop=(k == KD - 1))
                    ins.then_inc(v_done[par], 1)

        @block.sync
        def _(sp):
            with sp.Fori(0, NB // 2) as turn:
                for par in range(2):
                    sp.wait_ge(low_out[par], turn + 1)
                    sp.dma_start(c.qk_dram[ds(turn * 2 + par, 1)].rearrange("b q (m p) t -> p (b q m) t", p=P),
                                 parts[:, par].rearrange("p q m t -> p (q m) t")).then_inc(stored[par], 16)
            for par in range(2):
                sp.wait_ge(stored[par], 16 * NB // 2)


def load_stacks(sp, c, st, part_of, base, b, heads, sem_):
    lo, hi = heads
    for g, part in enumerate(part_of):
        rows = c.qk_dram[ds(b, 1), part, base + lo * DH:base + hi * DH, :]
        sp.dma_start(st[g * DH:(g + 1) * DH, lo:hi, :], rows.rearrange("a (h d) t -> d (a h) t", d=DH))\
            .then_inc(sem_, 16)


def stage_l0_attention(nc, c):
    G = 4
    with ExitStack() as ctx:
        sb = lambda name, shape, dt: ctx.enter_context(nc.sbuf_tensor(name, shape, dt))
        sem = stage_semaphores(nc, ctx)
        psum = lambda name, shape, dt: ctx.enter_context(nc.psum_tensor(name, shape, dt))
        q_st = [sb(f"q_st{i}", [6 * DH, H, S], BF16) for i in range(2)]
        k_st = [sb(f"k_st{i}", [6 * DH, H, S], BF16) for i in range(2)]
        nmax = sb("nmax", [P, 2, H], F32)
        nparts = sb("nparts", [P, 2, 2, H], BF16)
        nrow = sb("nrow", [2 * H, S], BF16)
        prob = sb("prob", [P, 2, 3 * G * P], F32)
        rsum = sb("rsum", [P, 2, H], F32)
        on = sb("on", [P, 2, D], F32)
        oT = sb("oT", [P, KD, S], F32)
        ring = [psum(f"ring{i}", [P, 3, 512], F32) for i in range(2)]
        po = psum("po", [P, 2, 512], F32)
        pnm = po[0:2 * H, 1, 384:512].bitcast(BF16)
        loaded = [sem("ld_a"), sem("ld_b")]
        names = ("s_done", "maxed", "nm_ready", "nmT", "nrow_out", "t_done", "exped", "pv_done", "o_ready", "oT_done",
                 "oT_out", "wo_done", "h_done", "own2")
        (s_done, maxed, nm_ready, nmT, nrow_out, t_done, exped, pv_done, o_ready, oT_done, oT_out, wo_done, h_done,
         own) = (sem(n) for n in names)
        block = ctx.enter_context(nc.Block())

        def batches(eng, body, tail):
            body(0, 0, 0, True)
            with eng.Fori(0, NB // 2 - 1) as turn:
                body(turn * 2 + 1, 1, turn, False)
                body(turn * 2 + 2, 0, turn + 1, False)
            body(NB - 1, 1, NB // 2 - 1, False)
            tail()

        @block.sync
        def _(sp):
            def load(b, par):
                load_stacks(sp, c, q_st[par], SPLIT_Q, 0, b, (0, H), loaded[par])
                load_stacks(sp, c, k_st[par], SPLIT_K, 2 * P, b, (0, H), loaded[par])
            load(0, 0)
            load(1, 1)
            with sp.Fori(0, NB // 2 - 1) as turn:
                for par in range(2):
                    sp.wait_ge(t_done, turn * 8 + 4 * par + 4)
                    load(turn * 2 + 2 + par, par)

        @block.tensor
        def _(pe):
            def scores(b, g):
                slot = ring[g % 2]
                for bank in range(3):
                    pe.matmul(slot[:, bank, :], c.identb[:, :], c.mask4[:, bank if bank < 2 else 1, :],
                              start=True, stop=False, skip_group_check=True)
                for x in range(G):
                    h = G * g + x
                    q, k = stacks[0], stacks[1]
                    pe.matmul(slot[:, 0, x * P:(x + 1) * P], q[:, h, 0:P], k[:, h, 0:P], start=False, stop=True,
                              skip_group_check=True)
                    ins = pe.matmul(slot[:, 1 + x // 2, (x % 2) * S:(x % 2 + 1) * S], q[:, h, P:S], k[:, h, :],
                                    start=False, stop=True, skip_group_check=True)
                ins.then_inc(s_done, 1)

            def turned(b, g):
                slot = ring[g % 2]
                q, k = stacks
                for bank in range(3):
                    pe.matmul(slot[:, bank, :], c.identb[:, :], c.mask4[:, 2 if bank < 2 else 3, :],
                              start=True, stop=False, skip_group_check=True)
                for x in range(G):
                    h = G * g + x
                    both, own_ = slot[:, x // 2, (x % 2) * S:(x % 2 + 1) * S], slot[:, 2, x * P:(x + 1) * P]
                    pe.matmul(both, c.sel[0:2 * H, h, :], nrow[:, :], start=False, stop=False, skip_group_check=True)
                    pe.matmul(both, k[:, h, 0:P], q[:, h, :], start=False, stop=True, skip_group_check=True)
                    pe.matmul(own_, c.sel[0:2 * H, h, :], nrow[:, P:S], start=False, stop=False,
                              skip_group_check=True)
                    ins = pe.matmul(own_, k[:, h, P:S], q[:, h, P:S], start=False, stop=True, skip_group_check=True)
                ins.then_inc(t_done, 1)

            def values(b, g):
                pt = prob[:, g % 2, :]
                for x in range(G):
                    h = G * g + x
                    o = slice(h * VA, (h + 1) * VA)
                    pe.matmul(po[:, 0, o], pt[:, x * S:x * S + P], c.vaug[:, ds(b * 2, 1), h, :], start=True,
                              stop=True, skip_group_check=True)
                    pe.matmul(po[:, 1, o], pt[:, x * S + P:(x + 1) * S], c.vaug[:, ds(b * 2, 1), h, :], start=True,
                              stop=False, skip_group_check=True)
                    ins = pe.matmul(po[:, 1, o], pt[:, 2 * 512 + x * P:2 * 512 + (x + 1) * P],
                                    c.vaug[:, ds(b * 2 + 1, 1), h, :], start=False, stop=True, skip_group_check=True)
                ins.then_inc(pv_done, 1)

            def out_turn(b):
                pe.wait_ge(o_ready, b + 1)
                slot = ring[0]
                for j in range(2):
                    for k in range(KD):
                        ins = pe.transpose(slot[:, 0, k * S + j * P:k * S + (j + 1) * P],
                                           on[:, j, k * P:(k + 1) * P], c.ident[:, :])
                ins.then_inc(oT_done, 1)

            def out_project(b):
                pe.wait_ge(oT_out, b + 1)
                slot = ring[1]
                for j in range(2):
                    for k in range(KD):
                        ins = pe.matmul(slot[:, 0, j * D:(j + 1) * D], oT[:, k, j * P:(j + 1) * P], c.wo0[:, k, :],
                                        start=(k == 0), stop=(k == KD - 1), skip_group_check=True)
                ins.then_inc(wo_done, 1)

            stacks = [None, None]

            def body(b, par, n, first):
                stacks[:] = [q_st[par], k_st[par]]
                pe.wait_ge(loaded[par], 12 * 16 * (n + 1))
                if not first:
                    pe.wait_ge(exped, b * 4 - 1)
                scores(b, 0)
                if not first:
                    pe.wait_ge(exped, b * 4)
                    values(b - 1, 3)
                scores(b, 1)
                pe.wait_ge(maxed, b * 4 + 1)
                scores(b, 2)
                pe.wait_ge(maxed, b * 4 + 2)
                scores(b, 3)
                if not first:
                    pe.wait_ge(maxed, b * 4 + 3)
                    out_turn(b - 1)
                pe.wait_ge(nm_ready, b + 1)
                for j in range(2):
                    ins = pe.transpose(pnm[:, j * P:(j + 1) * P], nparts[:, j].rearrange("p a h -> p (a h)"),
                                       c.identb[:, :])
                ins.then_inc(nmT, 1)
                if not first:
                    pe.wait_ge(maxed, b * 4 + 4)
                    out_project(b - 1)
                    pe.wait_ge(oT_out, b)
                pe.wait_ge(nrow_out, b + 1)
                turned(b, 0)
                if first:
                    pe.wait_ge(maxed, 4)
                else:
                    pe.wait_ge(h_done, b)
                turned(b, 1)
                for g in range(3):
                    pe.wait_ge(exped, b * 4 + g + 1)
                    if g == 0 and not first:
                        pe.wait_ge(o_ready, b)
                    if g + 2 < 4 and g < 2:
                        turned(b, g + 2)
                    values(b, g)

            def tail():
                b = NB - 1
                pe.wait_ge(exped, b * 4 + 4)
                values(b, 3)
                out_turn(b)
                out_project(b)

            batches(pe, body, tail)

        @block.scalar
        def _(act):
            def body(b, par, n, first):
                if not first:
                    act.wait_ge(oT_done, b)
                    act.activation(oT[:, :, :], ring[0][:, 0, :].rearrange("p (k t) -> p k t", k=KD), ACT.Copy)\
                        .then_inc(oT_out, 1)
                act.wait_ge(nmT, b + 1)
                if not first:
                    act.wait_ge(t_done, b * 4)
                act.activation(nrow[:, :], pnm[:, :], ACT.Copy).then_inc(nrow_out, 1)
                for g in range(4):
                    act.wait_ge(t_done, b * 4 + g + 1)
                    if not first:
                        act.wait_ge(pv_done, b * 4 + g - 1)
                    elif g >= 2:
                        act.wait_ge(pv_done, g - 1)
                    act.activation(prob[:, g % 2, :], ring[g % 2][:, :, :].rearrange("p a n -> p (a n)"), ACT.Exp,
                                   scale=DH ** -0.5).then_inc(exped, 1)

            def tail():
                act.wait_ge(oT_done, NB)
                act.activation(oT[:, :, :], ring[0][:, 0, :].rearrange("p (k t) -> p k t", k=KD), ACT.Copy)\
                    .then_inc(oT_out, 1)

            batches(act, body, tail)

        @block.vector
        def _(dve):
            def outputs(b):
                dve.wait_ge(pv_done, b * 4 + 4)
                o = po[:, :, 0:H * VA].rearrange("p j (h v) -> p j h v", v=VA)
                dve.reciprocal(rsum[:, :, :], o[:, :, :, DH]).then_inc(own, 1)
                dve.wait_ge(own, b * 2 + 2)
                for j in range(2):
                    ins = dve.tensor_tensor(on[:, j, :].rearrange("p (h d) -> p h d", h=H), o[:, j, :, 0:DH],
                                            rsum[:, j, :].unsqueeze(2).broadcast_to([P, H, DH]), ALU.mult)
                ins.then_inc(o_ready, 1)

            def residual(b):
                dve.wait_ge(wo_done, b + 1)
                for j in range(2):
                    ins = dve.tensor_tensor(c.h[:, ds(b * 2 + j, 1), :], c.h[:, ds(b * 2 + j, 1), :],
                                            ring[1][:, 0, j * D:(j + 1) * D].unsqueeze(1), ALU.add)
                ins.then_inc(h_done, 1)
                dve.wait_ge(h_done, b + 1)
                for j in range(2):
                    dve.bn_stats(c.stats[:, ds(b * 2 + j, 1), :], c.h[:, ds(b * 2 + j, 1), :])

            def body(b, par, n, first):
                for g in range(4):
                    dve.wait_ge(s_done, b * 4 + g + 1)
                    hs = slice(G * g, G * g + G)
                    dve.tensor_reduce(nmax[:, 0, hs], ring[g % 2][:, 0, :].rearrange("p (h k) -> p h k", h=G), AX.X,
                                      ALU.max, negate=True)
                    dve.tensor_reduce(nmax[:, 1, hs],
                                      ring[g % 2][:, 1:3, :].rearrange("p a (h k) -> p (a h) k", h=2), AX.X,
                                      ALU.max, negate=True).then_inc(maxed, 1)
                    if g == 0 and not first:
                        outputs(b - 1)
                dve.wait_ge(maxed, b * 4 + 4)
                if not first:
                    dve.wait_ge(nmT, b)
                dve.tensor_copy(nparts[:, :, 0, :], nmax[:, :, :]).then_inc(own, 1)
                dve.wait_ge(own, b * 2 + 1)
                dve.tensor_tensor(nparts[:, :, 1, :], nmax[:, :, :], nparts[:, :, 0, :], ALU.subtract)\
                    .then_inc(nm_ready, 1)
                if not first:
                    residual(b - 1)

            def tail():
                outputs(NB - 1)
                residual(NB - 1)

            batches(dve, body, tail)


def stage_l0_ffn(nc, c):
    W = 512
    TW = W // P
    STEPS = NB * S // W
    with ExitStack() as ctx:
        sb = lambda name, shape, dt: ctx.enter_context(nc.sbuf_tensor(name, shape, dt))
        sem = stage_semaphores(nc, ctx)
        pair = lambda name: [sem(name + "_a"), sem(name + "_b")]
        psum = lambda name, shape, dt: ctx.enter_context(nc.psum_tensor(name, shape, dt))
        xn = sb("xn3", [P, 2, TW, D], F32)
        xT = sb("xT3", [P, 2, KD, W], F32)
        s_in = sb("s_in", [M_UNITS, 2, W], F32)
        unit = sb("unit", [P, 2, W], F32)
        g_out = sb("g_out", [M_UNITS + 1, 2, W], F32)
        pT = psum("pT3", [P, KD, W], F32)
        ps = psum("ps3", [M_UNITS, W], F32)
        pb = [psum(f"pb3{i}", [P, W], F32) for i in range(2)]
        pg = psum("pg3", [M_UNITS, W], F32)
        po = psum("po3", [P, TW, D], F32)
        own, sqa, sqd, row_set = sem("own3"), sem("sqa3"), sem("sqd3"), sem("row_set")
        x_ready, xT_done, xT_out, s_done, s_out, g_done, g_ready, o_done, o_added = (
            pair(n) for n in ("x_ready3", "xT_done3", "xT_out3", "s_done3", "s_out3", "g_done3", "g_ready3",
                              "o_done3", "o_added3"))
        spread, unit_out, summed = pair("spread3"), pair("unit_out3"), pair("summed3")
        own_h = pair("own_h3")
        block = ctx.enter_context(nc.Block())

        @block.gpsimd
        def _(pool):
            pool.memset(g_out[M_UNITS:M_UNITS + 1, :, :], 1.0).then_inc(row_set, 1)

        @block.vector
        def _(dve):
            link = Link(dve, own)
            rstd_vector(dve, link, c, 1e-5, sqa, sqd, 1)

            def normalise(par, turn):
                dve.wait_ge(xT_done[par], turn)
                for x in range(TW):
                    t = (turn * 2 + par) * TW + x
                    ins = dve.tensor_scalar(xn[:, par, x, :], c.h[:, ds(t, 1), :], c.mean[:, ds(t, 1)],
                                            c.rstd[:, ds(t, 1)], ALU.subtract, ALU.mult)
                ins.then_inc(x_ready[par], 1)

            def residual(par, turn):
                dve.wait_ge(o_done[par], turn + 1)
                t = (turn * 2 + par) * TW
                dve.tensor_tensor(c.h[:, ds(t, TW), :], c.h[:, ds(t, TW), :], po[:, :, :], ALU.add)\
                    .then_inc(o_added[par], 1)
                dve.wait_ge(o_added[par], turn + 1)
                for x in range(TW):
                    dve.bn_stats(c.stats[:, ds(t + x, 1), :], c.h[:, ds(t + x, 1), :])

            with dve.Fori(0, STEPS // 2) as turn:
                for par in range(2):
                    normalise(par, turn)
                for par in range(2):
                    residual(par, turn)

        @block.scalar
        def _(act):
            root_scalar(act, c, sqa, sqd, 1)
            with act.Fori(0, STEPS // 2) as turn:
                for par in range(2):
                    act.wait_ge(xT_done[par], turn + 1)
                    act.activation(xT[:, par], pT[:, :, :], ACT.Copy).then_inc(xT_out[par], 1)
                    act.wait_ge(s_done[par], turn + 1)
                    act.activation(s_in[:, par], ps[:, :], ACT.Identity, bias=c.bin[:, :]).then_inc(s_out[par], 1)
                    for j in range(NBLK):
                        u, count = j % 2, turn * 8 + par * 4 + j // 2
                        act.wait_ge(spread[u], count + 1)
                        act.wait_ge(summed[u], count)
                        act.activation(unit[:, u], pb[u][:, :], ACT.Relu, bias=c.b1col[:, j:j + 1],
                                       scale=c.w1col[:, j:j + 1]).then_inc(unit_out[u], 1)
                    act.wait_ge(g_done[par], turn + 1)
                    act.activation(g_out[0:M_UNITS, par], pg[:, :], ACT.Identity, bias=c.b2u[:, :])\
                        .then_inc(g_ready[par], 1)

        @block.tensor
        def _(pe):
            pe.wait_ge(row_set, 1)
            with pe.Fori(0, STEPS // 2) as turn:
                for par in range(2):
                    pe.wait_ge(x_ready[par], turn + 1)
                    pe.wait_ge(*last(xT_out, par, turn))
                    for x in range(TW):
                        for k in range(KD):
                            ins = pe.transpose(pT[:, k, x * P:(x + 1) * P], xn[:, par, x, k * P:(k + 1) * P],
                                               c.ident[:, :])
                    ins.then_inc(xT_done[par], 1)
                    pe.wait_ge(xT_out[par], turn + 1)
                    pe.wait_ge(*last(s_out, par, turn))
                    for k in range(KD):
                        ins = pe.matmul(ps[:, :], c.win[:, k, :], xT[:, par, k, :], start=(k == 0),
                                        stop=(k == KD - 1))
                    ins.then_inc(s_done[par], 1)
                    pe.wait_ge(s_out[par], turn + 1)
                    for j in range(NBLK + 1):
                        if j < NBLK:
                            u, count = j % 2, turn * 8 + par * 4 + j // 2
                            pe.wait_ge(unit_out[u], count)
                            pe.matmul(pb[u][:, :], c.spread[:, j, :], s_in[:, par], start=True, stop=True)\
                                .then_inc(spread[u], 1)
                        if j > 0:
                            u, count = (j - 1) % 2, turn * 8 + par * 4 + (j - 1) // 2
                            pe.wait_ge(unit_out[u], count + 1)
                            if j == 1:
                                pe.wait_ge(*last(g_ready, par, turn))
                            ins = pe.matmul(pg[:, :], c.w2m[:, j - 1, :], unit[:, u], start=(j == 1),
                                            stop=(j == NBLK))
                            ins.then_inc(summed[u], 1)
                    pe.wait_ge(summed[1], turn * 8 + par * 4 + 4)
                    pe.sem_inc(g_done[par], 1)
                    pe.wait_ge(g_ready[par], turn + 1)
                    pe.wait_ge(*last(o_added, par, turn))
                    for x in range(TW):
                        ins = pe.matmul(po[:, x, :], g_out[:, par, x * P:(x + 1) * P], c.wout[:, :], start=True,
                                        stop=True)
                    ins.then_inc(o_done[par], 1)


def scale_of(dve, link, scale, inverse, tmp):
    link(dve.tensor_scalar(scale, scale, 1.0 / QMAX, None, ALU.mult))
    link(dve.tensor_scalar(tmp, scale, 0.0, None, ALU.is_equal))
    link(dve.tensor_tensor(scale, scale, tmp, ALU.add))
    link(dve.reciprocal(inverse, scale))


def stage_l1_project(nc, c):
    with ExitStack() as ctx:
        sb = lambda name, shape, dt: ctx.enter_context(nc.sbuf_tensor(name, shape, dt))
        sem = stage_semaphores(nc, ctx)
        pair = lambda name: [sem(name + "_a"), sem(name + "_b")]
        psum = lambda name, shape, dt: ctx.enter_context(nc.psum_tensor(name, shape, dt))
        xl = sb("xl", [P, 2, 4, D], F32)
        xmax = sb("xmax", [P, 8], F32)
        xm, xs, xinv, xtmp = (sb(n, [P, 1], F32) for n in ("xm", "xs", "xinv", "xtmp"))
        rinv = sb("rinv", [P, NT], F32)
        qks = sb("qks", [P, 4], F32)
        wvs = sb("wvs", [P, D], F32)
        xi = sb("xi", [P, 2, 2, D], I16)
        xb = sb("xb", [P, 2, 2, D], BF16)
        xT = sb("xT5", [P, 2, KD, S], BF16)
        vt = sb("vt", [P, 2, 2, D], F32)
        bmax = sb("bmax", [P, NB, 4 * NBLK], F32)
        vmax = sb("vmax", [P, NB], F32)
        m1 = sb("m1", [P, 4 * NBLK], F32)
        qm = sb("qm", [P, 2 * NBLK + 1], F32)
        qinv, qtmp = sb("qinv", [P, 2 * NBLK + 1], F32), sb("qtmp", [P, 2 * NBLK + 1], F32)
        pT = [psum(f"pT5{i}", [P, KD, S], BF16) for i in range(2)]
        pqk = psum("pqk5", [P, 2, 4, S], F32)
        pv = psum("pv5", [P, 2, 2, D], F32)
        own, sqa, sqd, asked, reduced = (sem(n) for n in ("own5", "sqa5", "sqd5", "asked5", "reduced5"))
        own_loop = sem("own5l")
        xi_ready, xb_ready, xT_done, xT_out, qk_done, v_done, qk_out, v_out, q_maxed = (
            pair(n) for n in ("xi_ready", "xb_ready", "xT_done5", "xT_out5", "qk_done5", "v_done5", "qk_out5",
                              "v_out5", "q_maxed"))
        block = ctx.enter_context(nc.Block())

        @block.vector
        def _(dve):
            link = Link(dve, own)
            rstd_vector(dve, link, c, 1e-5, sqa, sqd, 1)
            llink = Link(dve, own_loop)
            with dve.Fori(0, 4) as turn:
                llink.loop(turn, 2)
                for par in range(2):
                    g = turn * 2 + par
                    for x in range(4):
                        t = g * 4 + x
                        ins = dve.tensor_scalar(xl[:, par, x, :], c.h[:, ds(t, 1), :], c.mean[:, ds(t, 1)],
                                                c.rstd[:, ds(t, 1)], ALU.subtract, ALU.mult)
                    llink(ins)
                    dve.tensor_reduce(xmax[:, ds(g, 1)], xl[:, par].rearrange("p x d -> p (x d)"), AX.X, ALU.max,
                                      apply_absolute_value=True)
                llink.end(4)
            link(dve.memset(qtmp[:, :], 0.0))
            link(dve.tensor_reduce(xm[:, :], xmax[:, :], AX.X, ALU.max))
            dve.sem_inc(asked, 1)
            dve.wait_ge(reduced, 1)
            scale_of(dve, link, xs[:, :], xinv[:, :], xtmp[:, :])
            link(dve.tensor_scalar(rinv[:, :], c.rstd[:, :], xinv[:, :], None, ALU.mult))
            link(dve.tensor_scalar(qks[:, :], c.wscale[:, 0:4], xs[:, :], None, ALU.mult))
            link(dve.tensor_scalar(wvs[:, :], c.wvo[:, 0, :], xs[:, :], None, ALU.mult))

            def quantise(par, turn):
                dve.wait_ge(xb_ready[par], turn)
                for j in range(2):
                    t = (turn * 2 + par) * 2 + j
                    ins = dve.tensor_scalar(xi[:, par, j, :], c.h[:, ds(t, 1), :], c.mean[:, ds(t, 1)],
                                            rinv[:, ds(t, 1)], ALU.subtract, ALU.mult)
                ins.then_inc(xi_ready[par], 1)

            def results(par, turn):
                b = turn * 2 + par
                dve.wait_ge(v_done[par], turn + 1)
                dve.tensor_tensor(vt[:, par], pv[:, par], wvs[:, :].unsqueeze(1).broadcast_to([P, 2, D]), ALU.mult)\
                    .then_inc(v_out[par], 1)
                dve.wait_ge(v_out[par], turn * 2 + 1)
                dve.tensor_tensor(c.v32[:, ds(b * 2, 2), :], vt[:, par],
                                  c.bv[:, :].unsqueeze(1).broadcast_to([P, 2, D]), ALU.add).then_inc(v_out[par], 1)
                dve.wait_ge(qk_out[par], turn * 4 + 4)
                dve.tensor_reduce(bmax[:, ds(b, 1), :],
                                  c.qk32[:, :, ds(b * S, S)].rearrange("p m (k t) -> p m k t", t=32), AX.X, ALU.max,
                                  apply_absolute_value=True)
                dve.wait_ge(v_out[par], turn * 2 + 2)
                dve.tensor_reduce(vmax[:, ds(b, 1)], c.v32[:, ds(b * 2, 2), :].rearrange("p j d -> p (j d)"), AX.X,
                                  ALU.max, apply_absolute_value=True)

            with dve.Fori(0, NB // 2) as turn:
                for par in range(2):
                    quantise(par, turn)
                for par in range(2):
                    results(par, turn)
            link(dve.memset(qtmp[:, :], 0.0))
            link(dve.tensor_reduce(m1[:, :], bmax[:, :, :].rearrange("p b k -> p k b"), AX.X, ALU.max))
            link(dve.tensor_tensor(qm[:, 0:NBLK], m1[:, 0:NBLK], m1[:, NBLK:2 * NBLK], ALU.max))
            link(dve.tensor_tensor(qm[:, NBLK:2 * NBLK], m1[:, 2 * NBLK:3 * NBLK], m1[:, 3 * NBLK:], ALU.max))
            link(dve.tensor_reduce(qm[:, 2 * NBLK:], vmax[:, :], AX.X, ALU.max))
            dve.sem_inc(asked, 1)
            dve.wait_ge(reduced, 2)
            scale_of(dve, link, c.qscale[:, :], qinv[:, :], qtmp[:, :])
            for out, src in ((c.qs_row, c.qscale), (c.qi_row, qinv)):
                link(dve.tensor_copy(out[:, :, :].rearrange("p a (k t) -> p (a k) t", t=32),
                                     src[:, 0:2 * NBLK].unsqueeze(2).broadcast_to([P, 2 * NBLK, 32])))
            link(dve.tensor_copy(c.vinv[:, :], qinv[:, 2 * NBLK:]))

        @block.gpsimd
        def _(pool):
            pool.wait_ge(asked, 1)
            pool.partition_all_reduce(xs[:, :], xm[:, :], P, RMAX).then_inc(reduced, 1)
            pool.wait_ge(asked, 2)
            pool.partition_all_reduce(c.qscale[:, :], qm[:, :], P, RMAX).then_inc(reduced, 1)

        @block.scalar
        def _(act):
            root_scalar(act, c, sqa, sqd, 1)
            with act.Fori(0, NB // 2) as turn:
                for par in range(2):
                    act.wait_ge(xi_ready[par], turn + 1)
                    act.wait_ge(xT_done[par], turn)
                    act.activation(xb[:, par], xi[:, par], ACT.Copy).then_inc(xb_ready[par], 1)
                for par in range(2):
                    act.wait_ge(xT_done[par], turn + 1)
                    act.activation(xT[:, par], pT[par][:, :, :], ACT.Copy).then_inc(xT_out[par], 1)
                for par in range(2):
                    b = turn * 2 + par
                    act.wait_ge(qk_done[par], turn + 1)
                    for m in range(4):
                        act.activation(c.qk32[:, m, ds(b * S, S)], pqk[:, par, m, :], ACT.Identity,
                                       bias=c.bqk[:, m:m + 1], scale=qks[:, m:m + 1]).then_inc(qk_out[par], 1)

        @block.tensor
        def _(pe):
            with pe.Fori(0, NB // 2) as turn:
                for par in range(2):
                    pe.wait_ge(xb_ready[par], turn + 1)
                    pe.wait_ge(xT_out[par], turn)
                    for j in range(2):
                        for k in range(KD):
                            ins = pe.transpose(pT[par][:, k, j * P:(j + 1) * P], xb[:, par, j, k * P:(k + 1) * P],
                                               c.identb[:, :])
                    ins.then_inc(xT_done[par], 1)
                for par in range(2):
                    pe.wait_ge(xT_out[par], turn + 1)
                    pe.wait_ge(qk_out[par], turn * 4)
                    for m in range(4):
                        for k in range(KD):
                            ins = pe.matmul(pqk[:, par, m, :], c.wT[:, m // 2, k, (m % 2) * P:(m % 2 + 1) * P],
                                            xT[:, par, k, :], start=(k == 0), stop=(k == KD - 1))
                    ins.then_inc(qk_done[par], 1)
                    pe.wait_ge(v_out[par], turn * 2)
                    for j in range(2):
                        for k in range(KD):
                            ins = pe.matmul(pv[:, par, j, :], xT[:, par, k, j * P:(j + 1) * P], c.wT[:, 2, k, :],
                                            start=(k == 0), stop=(k == KD - 1))
                    ins.then_inc(v_done[par], 1)


def stage_l1_quantise(nc, c):
    with ExitStack() as ctx:
        sb = lambda name, shape, dt: ctx.enter_context(nc.sbuf_tensor(name, shape, dt))
        sem = stage_semaphores(nc, ctx)
        pair = lambda name: [sem(name + "_a"), sem(name + "_b")]
        qi = sb("qi", [P, 2, 4, S], I16)
        qb = sb("qb", [P, 2, 4, S], F32)
        rest = sb("rest6", [P, 2, 4, S], F32)
        parts = sb("parts6", [P, 2, 3, 4, S], BF16)
        vi = sb("vi", [P, 2, 2, D], I16)
        qi_ready, qb_ready, hi_out, mid_in, mid_out, low_out, stored, vi_ready, nv_out = (
            pair(n) for n in ("qi_ready", "qb_ready", "hi_out6", "mid_in6", "mid_out6", "low_out6", "stored6",
                              "vi_ready", "nv_out"))
        block = ctx.enter_context(nc.Block())
        by_op = lambda t: t.rearrange("p (a m) t -> p a m t", a=2)
        row = lambda t: t[:, :, :].unsqueeze(2).broadcast_to([P, 2, 2, S])

        @block.vector
        def _(dve):
            with dve.Fori(0, NB // 2) as turn:
                for par in range(2):
                    b = turn * 2 + par
                    dve.wait_ge(qb_ready[par], turn)
                    dve.tensor_tensor(by_op(qi[:, par]), by_op(c.qk32[:, :, ds(b * S, S)]), row(c.qi_row), ALU.mult)\
                        .then_inc(qi_ready[par], 1)
                    dve.wait_ge(qi_ready[par], turn + 1)
                    dve.wait_ge(mid_in[par], turn)
                    dve.tensor_tensor(by_op(qb[:, par]), by_op(qi[:, par]), row(c.qs_row), ALU.mult)\
                        .then_inc(qb_ready[par], 1)
                    dve.wait_ge(nv_out[par], turn)
                    dve.tensor_scalar(vi[:, par], c.v32[:, ds(b * 2, 2), :], c.vinv[:, :], None, ALU.mult)\
                        .then_inc(vi_ready[par], 1)
                for par in range(2):
                    dve.wait_ge(hi_out[par], turn + 1)
                    dve.tensor_tensor(rest[:, par], qb[:, par], parts[:, par, 0], ALU.subtract)\
                        .then_inc(mid_in[par], 1)
                    dve.wait_ge(mid_out[par], turn + 1)
                    dve.tensor_tensor(parts[:, par, 2], rest[:, par], parts[:, par, 1], ALU.subtract)\
                        .then_inc(low_out[par], 1)

        @block.scalar
        def _(act):
            with act.Fori(0, NB // 2) as turn:
                for par in range(2):
                    act.wait_ge(qb_ready[par], turn + 1)
                    act.wait_ge(stored[par], turn * 16)
                    act.activation(parts[:, par, 0], qb[:, par], ACT.Copy).then_inc(hi_out[par], 1)
                    act.wait_ge(vi_ready[par], turn + 1)
                    act.activation(c.nv[:, ds((turn * 2 + par) * 2, 2), :], vi[:, par], ACT.Copy)\
                        .then_inc(nv_out[par], 1)
                for par in range(2):
                    act.wait_ge(mid_in[par], turn + 1)
                    act.activation(parts[:, par, 1], rest[:, par], ACT.Copy).then_inc(mid_out[par], 1)

        @block.sync
        def _(sp):
            with sp.Fori(0, NB // 2) as turn:
                for par in range(2):
                    sp.wait_ge(low_out[par], turn + 1)
                    sp.dma_start(c.qk_dram[ds(turn * 2 + par, 1)].rearrange("b q (m p) t -> p (b q m) t", p=P),
                                 parts[:, par].rearrange("p q m t -> p (q m) t")).then_inc(stored[par], 16)
            for par in range(2):
                sp.wait_ge(stored[par], 16 * NB // 2)


FIX = 2.0 ** 26
GROUP = 2.5
PC = 8


def need(eng, sem_, value):
    if not isinstance(value, int) or value > 0:
        eng.wait_ge(sem_, value)


def stage_l1_exponentials(nc, c):
    ms, cs = pla_table()
    a = [GROUP * m for m in ms[9:]]
    b_ = [3 * GROUP * m + k for m, k in zip(ms[9:], cs[9:])]
    unit = a[1] - a[0]
    edge1, edge2 = -4 + 1 / 3, -4 + 2 / 3
    with ExitStack() as ctx:
        sb = lambda name, shape, dt: ctx.enter_context(nc.sbuf_tensor(name, shape, dt))
        sem = stage_semaphores(nc, ctx)
        psum = lambda name, shape, dt: ctx.enter_context(nc.psum_tensor(name, shape, dt))
        q_st = [sb(f"q_st7{i}", [6 * DH, H, S], BF16) for i in range(2)]
        k_st = [sb(f"k_st7{i}", [6 * DH, H, S], BF16) for i in range(2)]
        nmax = sb("nmax7", [P, 2, H], F32)
        nrest = sb("nrest7", [P, 2, H], F32)
        nparts = sb("nparts7", [P, 2, P], BF16)
        nrow = sb("nrow7", [3 * H, S], BF16)
        W = 2 * 512
        fixed = sb("fixed", [P, 2, W], I32)
        group = sb("group", [P, 2, W], I16)
        local = sb("local", [P, 2, W], F32)
        base = sb("base", [P, 2, W], F32)
        step2 = sb("step2", [P, 2, W], F32)
        acc = sb("acc", [P, 2, W], F32)
        power = sb("power", [P, 2, W], F32)
        ex = sb("ex", [P, 2, W], F32)
        cols = sb("cols", [P, 4], F32)
        onesel = sb("onesel", [P, PC, PC], F32)
        srow = sb("srow", [PC, 2, 512], F32)
        pS = psum("pS7", [P, 2, 512], F32)
        pT = [psum(f"pT7{i}", [P, 2, 512], F32) for i in range(2)]
        psums = psum("psums", [PC, 512], F32)
        pnm = psum("pnm7", [P, S], BF16)
        ld = [[sem(f"ld7{p}{x}") for x in range(2)] for p in range(2)]
        names = ("s_done7", "maxed7", "nm_ready7", "nmT7", "nrow_out7", "t_done7", "fixed_out", "group_out",
                 "power_out", "local_out", "base_out", "step2_out", "acc_out", "ex_out", "summed7", "own7", "sums_out",
                 "consts7", "pool7")
        (s_done, maxed, nm_ready, nmT, nrow_out, t_done, fixed_out, group_out, power_out, local_out, base_out,
         step2_out, acc_out, ex_out, summed, own, sums_out, consts, pool_own) = (sem(n) for n in names)
        ex_stored = [sem("ex_stored_a"), sem("ex_stored_b")]
        sums_stored = [sem("sums_stored_a"), sem("sums_stored_b")]
        block = ctx.enter_context(nc.Block())

        def batches(body, eng):
            body(0, 0, 0)
            with eng.Fori(0, NB // 2 - 1) as turn:
                body(turn * 2 + 1, 1, turn)
                body(turn * 2 + 2, 0, turn + 1)
            body(NB - 1, 1, NB // 2 - 1)

        final = lambda b: isinstance(b, int) and b == NB - 1
        first = lambda b: isinstance(b, int) and b == 0

        @block.sync
        def _(sp):
            def load(b, par, half, rows):
                cut = slice(half * 8, half * 8 + 8)
                for r in rows:
                    st, part, base_ = (q_st, SPLIT_Q[r], 0) if r < 6 else (k_st, SPLIT_K[r - 6], 2 * P)
                    src = c.qk_dram[ds(b, 1), part, base_ + half * P:base_ + half * P + P, :]
                    sp.dma_start(st[par][(r % 6) * DH:(r % 6 + 1) * DH, cut, :],
                                 src.rearrange("a (h d) t -> d (a h) t", d=DH)).then_inc(ld[par][half], 16)

            for b, half in ((0, 0), (0, 1), (1, 0)):
                load(b, b, half, range(12))

            def body(b, par, n):
                for g in range(PC):
                    if g >= 1 or not first(b):
                        i, k = b * PC + g, (g - 1) % 2
                        sp.wait_ge(ex_out, i)
                        sp.dma_start(c.ex_dram[ds(i - 1, 1)].rearrange("a p n -> p (a n)"), ex[:, k, :])\
                            .then_inc(ex_stored[k], 16)
                    rows = range(3 * (g % 4), 3 * (g % 4) + 3)
                    if g < 4 and not final(b):
                        if not first(b):
                            sp.wait_ge(t_done, b * PC)
                        load(b + 1, 1 - par, 1, rows)
                    if g >= 4 and not (isinstance(b, int) and b >= NB - 2):
                        sp.wait_ge(t_done, b * PC + 4)
                        load(b + 2, par, 0, rows)

            body(0, 0, 0)
            with sp.Fori(0, NB // 2 - 2) as turn:
                body(turn * 2 + 1, 1, turn)
                body(turn * 2 + 2, 0, turn + 1)
            for b in range(NB - 3, NB):
                body(b, b % 2, b // 2)
            i = NB * PC
            sp.wait_ge(ex_out, i)
            sp.dma_start(c.ex_dram[i - 1], ex[:, 1, :]).then_inc(ex_stored[1], 16)
            for k in range(2):
                sp.wait_ge(ex_stored[k], 16 * NB * PC // 2)

        @block.gpsimd
        def _(pool):
            link = Link(pool, pool_own)
            link(pool.memset(onesel[:, :, :], 0.0))
            for g in range(PC):
                ins = pool.memset(onesel[:, g, g:g + 1], 1.0)
            link(ins)
            pool.sem_inc(consts, 1)

            def body(b, par, n):
                for g in range(PC):
                    i = b * PC + g
                    k = g % 2
                    pool.wait_ge(acc_out, i * 4 + 4)
                    pool.wait_ge(power_out, i + 1)
                    need(pool, summed, i - 1)
                    if g >= 2 or not first(b):
                        pool.wait_ge(ex_stored[k], (b * (PC // 2) + g // 2) * 16)
                    pool.tensor_tensor(ex[:, k, :], acc[:, k, :], power[:, k, :], ALU.mult).then_inc(ex_out, 1)

            batches(body, pool)

        @block.scalar
        def _(act):
            act.wait_ge(consts, 2)

            def late(i, k):
                act.wait_ge(local_out, i + 1)
                need(act, acc_out, (i - 1) * 4 - 3)
                need(act, acc_out, (i - 1) * 4)
                act.activation(base[:, k, :], local[:, k, :], ACT.Relu, bias=cols[:, 0:1], scale=a[0] / unit)\
                    .then_inc(base_out, 1)
                act.activation(step2[:, k, :], local[:, k, :], ACT.Identity, bias=cols[:, 1:2],
                               scale=(a[2] - a[1]) / unit).then_inc(step2_out, 1)

            def row_out(b):
                act.wait_ge(nmT, b + 1)
                if not first(b):
                    act.wait_ge(t_done, b * PC)
                act.activation(nrow[:, :], pnm[0:3 * H, :], ACT.Copy).then_inc(nrow_out, 1)

            def body(b, par, n):
                for g in range(PC):
                    i, k = b * PC + g, g % 2
                    act.wait_ge(t_done, i + 1)
                    need(act, local_out, i - 1)
                    act.activation(fixed[:, k, :], pT[k][:, :, :].rearrange("p a n -> p (a n)"), ACT.Relu,
                                   scale=-FIX * DH ** -0.5).then_inc(fixed_out, 1)
                    if g >= 1 or not first(b):
                        late(i - 1, 1 - k)
                    act.wait_ge(fixed_out, i + 1)
                    act.activation(group[:, k, :], fixed[:, k, :], ACT.Relu, bias=cols[:, 2:3],
                                   scale=-1 / (GROUP * FIX)).then_inc(group_out, 1)
                    if g == 2 and not first(b):
                        sums(b - 1)
                    act.wait_ge(group_out, i + 1)
                    need(act, ex_out, i - 1)
                    act.activation(power[:, k, :], group[:, k, :], ACT.Exp, bias=cols[:, 3:4], scale=GROUP)\
                        .then_inc(power_out, 1)
                if not final(b):
                    row_out(b + 1)

            def sums(b):
                act.wait_ge(summed, b * PC + PC)
                if isinstance(b, int):
                    k, turn = b % 2, b // 2
                else:
                    k, turn = state["par"], state["n"]
                if not isinstance(turn, int) or turn > 0:
                    act.wait_ge(sums_stored[k], turn * 16)
                act.activation(srow[:, k, :], psums[:, :], ACT.Copy).then_inc(sums_out, 1)
                act.wait_ge(sums_out, b + 1)
                act.dma_start(c.sum_dram[ds(b, 1)].rearrange("a g n -> g (a n)"), srow[:, k, :])\
                    .then_inc(sums_stored[k], 16)

            state = {}
            row_out(0)
            body(0, 0, 0)
            with act.Fori(0, NB // 2 - 1) as turn:
                state.update(par=0, n=turn)
                body(turn * 2 + 1, 1, turn)
                state.update(par=1, n=turn)
                body(turn * 2 + 2, 0, turn + 1)
            body(NB - 1, 1, NB // 2 - 1)
            late(NB * PC - 1, 1)
            sums(NB - 1)
            for k in range(2):
                act.wait_ge(sums_stored[k], 16 * NB // 2)

        @block.vector
        def _(dve):
            for x, value in enumerate((4 * a[0] / unit, (b_[2] - b_[1]) / unit, 3.5 * (1 - 2.0 ** -23), -3 * GROUP)):
                dve.memset(cols[:, x:x + 1], value)
            dve.memset(nparts[:, :, :], 0.0).then_inc(own, 1)
            dve.wait_ge(own, 1)
            dve.sem_inc(consts, 1)

            def row_max(b, g):
                dve.wait_ge(s_done, b * PC + g + 1)
                dve.tensor_reduce(nmax[:, :, 2 * g:2 * g + 2], pS[:, :, :].rearrange("p j (h k) -> p j h k", h=2),
                                  AX.X, ALU.max, negate=True).then_inc(maxed, 1)

            def max_parts(b):
                dve.wait_ge(maxed, b * PC + PC)
                if not first(b):
                    dve.wait_ge(nmT, b)
                dve.tensor_copy(nparts[:, :, 0:16], nmax[:, :, :]).then_inc(own, 1)
                dve.wait_ge(own, b * 3 + 2)
                dve.tensor_tensor(nrest[:, :, :], nmax[:, :, :], nparts[:, :, 0:16], ALU.subtract).then_inc(own, 1)
                dve.wait_ge(own, b * 3 + 3)
                dve.tensor_copy(nparts[:, :, 16:32], nrest[:, :, :]).then_inc(own, 1)
                dve.wait_ge(own, b * 3 + 4)
                dve.tensor_tensor(nparts[:, :, 32:48], nrest[:, :, :], nparts[:, :, 16:32], ALU.subtract)\
                    .then_inc(nm_ready, 1)

            def pieces(i, k, between):
                w, f = local[:, k, :], acc[:, k, :]
                dve.wait_ge(step2_out, i + 1)
                need(dve, ex_out, i - 1)
                dve.scalar_tensor_tensor(out=f, in0=w, scalar=edge2, in1=step2[:, k, :], op0=ALU.is_ge,
                                         op1=ALU.mult).then_inc(acc_out, 1)
                between()
                dve.wait_ge(acc_out, i * 4 + 1)
                dve.scalar_tensor_tensor(out=f, in0=f, scalar=(b_[1] - b_[0]) / unit, in1=w, op0=ALU.add,
                                         op1=ALU.add).then_inc(acc_out, 1)
                dve.wait_ge(acc_out, i * 4 + 2)
                dve.scalar_tensor_tensor(out=f, in0=w, scalar=edge1, in1=f, op0=ALU.is_ge, op1=ALU.mult)\
                    .then_inc(acc_out, 1)
                dve.wait_ge(acc_out, i * 4 + 3)
                dve.scalar_tensor_tensor(out=f, in0=f, scalar=(b_[0] - 4 * a[0]) / unit, in1=base[:, k, :],
                                         op0=ALU.add, op1=ALU.add).then_inc(acc_out, 1)

            for g in range(PC):
                row_max(0, g)
            max_parts(0)

            def body(b, par, n):
                for g in range(PC):
                    i, k = b * PC + g, g % 2
                    between = (lambda: None) if final(b) else (lambda: row_max(b + 1, g))
                    if g >= 1 or not first(b):
                        pieces(i - 1, 1 - k, between)
                    else:
                        between()
                    dve.wait_ge(group_out, i + 1)
                    dve.scalar_tensor_tensor(out=local[:, k, :], in0=fixed[:, k, :], scalar=-1 / (GROUP * FIX),
                                             in1=group[:, k, :], op0=ALU.mult, op1=ALU.subtract)\
                        .then_inc(local_out, 1)
                if not final(b):
                    max_parts(b + 1)

            batches(body, dve)
            pieces(NB * PC - 1, 1, lambda: None)

        @block.tensor
        def _(pe):
            pe.wait_ge(consts, 2)

            def scores(b, par, g):
                need(pe, maxed, b * PC + g)
                q, k = q_st[par], k_st[par]
                for j in range(2):
                    for x in range(2):
                        ins = pe.matmul(pS[:, j, x * S:(x + 1) * S], q[:, 2 * g + x, j * P:(j + 1) * P],
                                        k[:, 2 * g + x, :], start=True, stop=True, skip_group_check=True)
                ins.then_inc(s_done, 1)

            def turned(b, par, g):
                slot, q, k = pT[g % 2], q_st[par], k_st[par]
                need(pe, fixed_out, b * PC + g - 1)
                for j in range(2):
                    for x in range(2):
                        o = slot[:, j, x * S:(x + 1) * S]
                        pe.matmul(o, c.sel[:, 2 * g + x, :], nrow[:, :], start=True, stop=False,
                                  skip_group_check=True)
                        ins = pe.matmul(o, k[:, 2 * g + x, j * P:(j + 1) * P], q[:, 2 * g + x, :], start=False,
                                        stop=True, skip_group_check=True)
                ins.then_inc(t_done, 1)

            def row_sums(i, g):
                pe.wait_ge(ex_out, i + 1)
                if g == 0:
                    need(pe, sums_out, state["b"])
                for j in range(2):
                    ins = pe.matmul(psums[:, :], onesel[:, g, :], ex[:, g % 2, j * 512:(j + 1) * 512],
                                    start=(g == 0 and j == 0), stop=(g == PC - 1 and j == 1), skip_group_check=True)
                ins.then_inc(summed, 1)

            def max_rows(b):
                pe.wait_ge(nm_ready, b + 1)
                for j in range(2):
                    ins = pe.transpose(pnm[:, j * P:(j + 1) * P], nparts[:, j, :],
                                       c.identb[:, :])
                ins.then_inc(nmT, 1)

            state = {}
            for half in range(2):
                pe.wait_ge(ld[0][half], 12 * 16)
            for g in range(PC):
                scores(0, 0, g)
            max_rows(0)

            def body(b, par, n):
                state["b"] = b
                pe.wait_ge(nrow_out, b + 1)
                for g in range(PC):
                    i = b * PC + g
                    turned(b, par, g)
                    if not final(b):
                        if g % 4 == 0:
                            pe.wait_ge(ld[1 - par][g // 4], 12 * 16 * (n + (1 if par == 0 else 2)))
                        scores(b + 1, 1 - par, g)
                    if g >= 2:
                        row_sums(i - 2, g - 2)
                    elif not first(b):
                        row_sums(i - 2, PC + g - 2)
                if not final(b):
                    max_rows(b + 1)

            batches(body, pe)
            row_sums(NB * PC - 2, PC - 2)
            row_sums(NB * PC - 1, PC - 1)


def stage_l1_context(nc, c):
    ms, cs = pla_table()
    unit = GROUP * (ms[10] - ms[9])
    RING = 4
    with ExitStack() as ctx:
        sb = lambda name, shape, dt: ctx.enter_context(nc.sbuf_tensor(name, shape, dt))
        sem = stage_semaphores(nc, ctx)
        psum = lambda name, shape, dt: ctx.enter_context(nc.psum_tensor(name, shape, dt))
        sums = sb("sums8", [P, 512], F32)
        smax, smx = sb("smax8", [P, 1], F32), sb("smx8", [P, 1], F32)
        pscale, pinv, ptmp, cscale = (sb(n, [P, 1], F32) for n in ("pscale", "pinv", "ptmp", "cscale"))
        rows = sb("rows8", [PC, 2, 512], F32)
        pick = sb("pick8", [PC, PC, P], F32)
        ex = sb("ex8", [P, RING, 2, 512], F32)
        pi = sb("pi8", [P, 2, 2, 512], I16)
        pb = sb("pb8", [P, 2, 2, 512], BF16)
        pr = [psum(f"pr8{i}", [P, 512], F32) for i in range(2)]
        pc = [psum(f"pc8{i}", [P, 2, D], F32) for i in range(2)]
        loaded = [sem(f"ex_ld{i}") for i in range(RING)]
        sums_in, asked, reduced, own, inv_stored, picked, consts = (
            sem(n) for n in ("sums_in", "asked8", "reduced8", "own8", "inv_stored", "picked8", "consts8"))
        rows_in = [sem("rows_in_a"), sem("rows_in_b")]
        spread, rounded, cast, pv_done, c_out, c_own = (
            sem(n) for n in ("spread8", "rounded8", "cast8", "pv_done8", "c_out8", "c_own8"))
        block = ctx.enter_context(nc.Block())
        chunk = lambda turn, par, g: (turn * 2 + par) * PC + g

        @block.gpsimd
        def _(pool):
            link = Link(pool, picked)
            link(pool.memset(pick[:, :, :], 0.0))
            link(pool.affine_select(out=pick[:, :, :], in_=pick[:, :, :], compare_op=ALU.not_equal, fill=1.0,
                                    base=0, channel_multiplier=1, pattern=[[-1, PC], [0, P]]))
            pool.sem_inc(consts, 1)
            pool.wait_ge(asked, 1)
            pool.partition_all_reduce(smx[:, :], smax[:, :], P, RMAX).then_inc(reduced, 1)

        @block.sync
        def _(sp):
            sp.dma_start(sums[:, :], c.sum_dram.rearrange("b g n -> (b g) n")).then_inc(sums_in, 16)
            for r in range(RING):
                sp.dma_start(ex[:, r].rearrange("p a n -> p (a n)"), c.ex_dram[r]).then_inc(loaded[r], 16)
            sp.wait_ge(asked, 2)
            sp.dma_start(c.inv_dram.rearrange("b g n -> (b g) n"), sums[:, :]).then_inc(inv_stored, 16)
            sp.wait_ge(inv_stored, 16)
            for par in range(2):
                sp.dma_start(rows[:, par, :], c.inv_dram[par]).then_inc(rows_in[par], 16)

            def body(turn, last_turn):
                for par in range(2):
                    for g in range(PC):
                        i = chunk(turn, par, g)
                        if last_turn and par == 1 and g >= RING:
                            continue
                        sp.wait_ge(rounded, i + 1)
                        sp.dma_start(ex[:, g % RING].rearrange("p a n -> p (a n)"),
                                     c.ex_dram[ds(i + RING, 1)].rearrange("a p n -> p (a n)"))\
                            .then_inc(loaded[g % RING], 16)
                    if not last_turn:
                        sp.wait_ge(spread, chunk(turn, par, PC - 1) + 1)
                        sp.dma_start(rows[:, par, :], c.inv_dram[ds(turn * 2 + par + 2, 1)].rearrange(
                            "a g n -> g (a n)")).then_inc(rows_in[par], 16)

            with sp.Fori(0, NB // 2 - 1) as turn:
                body(turn, False)
            body(NB // 2 - 1, True)

        @block.vector
        def _(dve):
            link = Link(dve, own)
            dve.wait_ge(sums_in, 16)
            link(dve.tensor_scalar(sums[:, :], sums[:, :], 1e-9 / unit, None, ALU.add))
            link(dve.reciprocal(sums[:, :], sums[:, :]))
            link(dve.tensor_reduce(smax[:, :], sums[:, :], AX.X, ALU.max))
            dve.sem_inc(asked, 1)
            dve.wait_ge(reduced, 1)
            link(dve.tensor_scalar(pscale[:, :], smx[:, :], cs[11] / unit, None, ALU.mult))
            scale_of(dve, link, pscale[:, :], pinv[:, :], ptmp[:, :])
            link(dve.tensor_tensor(cscale[:, :], pscale[:, :], c.qscale[:, 2 * NBLK:], ALU.mult))
            link(dve.tensor_scalar(sums[:, :], sums[:, :], pinv[:, :], None, ALU.mult))
            dve.sem_inc(asked, 1)

            def context(turn, par, b):
                dve.wait_ge(pv_done, b * PC + PC)
                ins = dve.tensor_scalar(c.ctx[:, ds(b * 2, 2), :], pc[par][:, :, :], cscale[:, :], None, ALU.mult)
                ins.then_inc(c_out, 1)
                dve.wait_ge(c_out, b + 1)
                dve.tensor_reduce(c.cmax[:, ds(b, 1)], c.ctx[:, ds(b * 2, 2), :].rearrange("p j d -> p (j d)"),
                                  AX.X, ALU.max, apply_absolute_value=True)

            def body(turn, first_turn):
                for par in range(2):
                    for g in range(PC):
                        i = chunk(turn, par, g)
                        dve.wait_ge(spread, i + 1)
                        dve.wait_ge(loaded[g % RING], (turn * 4 + par * 2 + g // RING + 1) * 16)
                        if not (first_turn and par == 0 and g < 2):
                            dve.wait_ge(cast, i - 1)
                        dve.tensor_tensor(pi[:, g % 2], ex[:, g % RING],
                                          pr[g % 2][:, :].unsqueeze(1).broadcast_to([P, 2, 512]), ALU.mult)\
                            .then_inc(rounded, 1)
                        if g == 3 and not (first_turn and par == 0):
                            context(turn, 1 - par, turn * 2 + par - 1)

            body(0, True)
            with dve.Fori(1, NB // 2) as turn:
                body(turn, False)
            context(None, 1, NB - 1)

        @block.scalar
        def _(act):
            def body(turn, first_turn):
                for par in range(2):
                    for g in range(PC):
                        i = chunk(turn, par, g)
                        act.wait_ge(rounded, i + 1)
                        if not (first_turn and par == 0 and g < 2):
                            act.wait_ge(pv_done, i - 1)
                        act.activation(pb[:, g % 2], pi[:, g % 2], ACT.Copy).then_inc(cast, 1)

            body(0, True)
            with act.Fori(1, NB // 2) as turn:
                body(turn, False)

        @block.tensor
        def _(pe):
            pe.wait_ge(consts, 1)

            def spread_row(turn, par, g, i, early):
                if g == 0:
                    pe.wait_ge(rows_in[par], (turn + 1) * 16)
                if not early:
                    pe.wait_ge(rounded, i - 1)
                pe.matmul(pr[g % 2][:, :], pick[:, g, :], rows[:, par, :], start=True, stop=True)\
                    .then_inc(spread, 1)

            def values(turn, par, g, i, b, first_batches):
                pe.wait_ge(cast, i + 1)
                if g == 0 and not first_batches:
                    pe.wait_ge(c_out, b - 1)
                for x in range(2):
                    h = 2 * g + x
                    for j in range(2):
                        for k in range(2):
                            ins = pe.matmul(pc[par][:, j, h * DH:(h + 1) * DH],
                                            pb[:, g % 2, k, x * S + j * P:x * S + (j + 1) * P],
                                            c.nv[:, ds(b * 2 + k, 1), h * DH:(h + 1) * DH].rearrange(
                                                "p a d -> p (a d)"),
                                            start=(k == 0), stop=(k == 1), skip_group_check=True)
                ins.then_inc(pv_done, 1)

            def body(turn, first_turn):
                for par in range(2):
                    for g in range(PC):
                        i = chunk(turn, par, g)
                        spread_row(turn, par, g, i, first_turn and par == 0 and g < 2)
                        if g >= 1:
                            values(turn, par, g - 1, i - 1, turn * 2 + par, first_turn)
                        elif par == 1:
                            values(turn, 0, PC - 1, i - 1, turn * 2, first_turn)
                        elif not first_turn:
                            values(turn, 1, PC - 1, i - 1, turn * 2 - 1, first_turn)

            body(0, True)
            with pe.Fori(1, NB // 2) as turn:
                body(turn, False)
            values(None, 1, PC - 1, NB * PC - 1, NB - 1, False)


def stage_l1_output(nc, c):
    with ExitStack() as ctx:
        sb = lambda name, shape, dt: ctx.enter_context(nc.sbuf_tensor(name, shape, dt))
        sem = stage_semaphores(nc, ctx)
        pair = lambda name: [sem(name + "_a"), sem(name + "_b")]
        psum = lambda name, shape, dt: ctx.enter_context(nc.psum_tensor(name, shape, dt))
        cm, cs_, cinv, ctmp = (sb(n, [P, 1], F32) for n in ("cm9", "cs9", "cinv9", "ctmp9"))
        wos = sb("wos9", [P, D], F32)
        ci = sb("ci9", [P, 2, 2, D], I16)
        cb = sb("cb9", [P, 2, 2, D], BF16)
        cT = sb("cT9", [P, 2, KD, S], BF16)
        out = sb("out9", [P, 2, 2, D], F32)
        pT = [psum(f"pT9{i}", [P, KD, S], BF16) for i in range(2)]
        po = [psum(f"po9{i}", [P, 2, D], F32) for i in range(2)]
        asked, reduced, own = (sem(n) for n in ("asked9", "reduced9", "own9"))
        ci_ready, cb_ready, cT_done, cT_out, o_done, o_out, biased, h_done = (
            pair(n) for n in ("ci_ready", "cb_ready", "cT_done", "cT_out", "o_done9", "o_out9", "biased9", "h_done9"))
        block = ctx.enter_context(nc.Block())

        @block.gpsimd
        def _(pool):
            pool.wait_ge(asked, 1)
            pool.partition_all_reduce(cs_[:, :], cm[:, :], P, RMAX).then_inc(reduced, 1)
            with pool.Fori(0, NB // 2) as turn:
                for par in range(2):
                    pool.wait_ge(o_out[par], turn + 1)
                    pool.tensor_tensor(out[:, par], out[:, par], c.bo[:, :].unsqueeze(1).broadcast_to([P, 2, D]),
                                       ALU.add).then_inc(biased[par], 1)

        @block.vector
        def _(dve):
            link = Link(dve, own)
            link(dve.tensor_reduce(cm[:, :], c.cmax[:, :], AX.X, ALU.max))
            dve.sem_inc(asked, 1)
            dve.wait_ge(reduced, 1)
            scale_of(dve, link, cs_[:, :], cinv[:, :], ctmp[:, :])
            link(dve.tensor_scalar(wos[:, :], c.wvo[:, 1, :], cs_[:, :], None, ALU.mult))

            with dve.Fori(0, NB // 2) as turn:
                for par in range(2):
                    b = turn * 2 + par
                    dve.wait_ge(cb_ready[par], turn)
                    dve.tensor_scalar(ci[:, par], c.ctx[:, ds(b * 2, 2), :], cinv[:, :], None, ALU.mult)\
                        .then_inc(ci_ready[par], 1)
                for par in range(2):
                    dve.wait_ge(o_done[par], turn + 1)
                    dve.wait_ge(h_done[par], turn)
                    dve.tensor_tensor(out[:, par], po[par][:, :, :], wos[:, :].unsqueeze(1).broadcast_to([P, 2, D]),
                                      ALU.mult).then_inc(o_out[par], 1)
                for par in range(2):
                    b = turn * 2 + par
                    dve.wait_ge(biased[par], turn + 1)
                    dve.tensor_tensor(c.h[:, ds(b * 2, 2), :], c.h[:, ds(b * 2, 2), :], out[:, par], ALU.add)\
                        .then_inc(h_done[par], 1)
                    dve.wait_ge(h_done[par], turn + 1)
                    for j in range(2):
                        dve.bn_stats(c.stats[:, ds(b * 2 + j, 1), :], c.h[:, ds(b * 2 + j, 1), :])

        @block.scalar
        def _(act):
            with act.Fori(0, NB // 2) as turn:
                for par in range(2):
                    act.wait_ge(ci_ready[par], turn + 1)
                    act.wait_ge(cT_done[par], turn)
                    act.activation(cb[:, par], ci[:, par], ACT.Copy).then_inc(cb_ready[par], 1)
                for par in range(2):
                    act.wait_ge(cT_done[par], turn + 1)
                    act.activation(cT[:, par], pT[par][:, :, :], ACT.Copy).then_inc(cT_out[par], 1)

        @block.tensor
        def _(pe):
            with pe.Fori(0, NB // 2) as turn:
                for par in range(2):
                    pe.wait_ge(cb_ready[par], turn + 1)
                    pe.wait_ge(cT_out[par], turn)
                    for j in range(2):
                        for k in range(KD):
                            ins = pe.transpose(pT[par][:, k, j * P:(j + 1) * P], cb[:, par, j, k * P:(k + 1) * P],
                                               c.identb[:, :])
                    ins.then_inc(cT_done[par], 1)
                for par in range(2):
                    pe.wait_ge(cT_out[par], turn + 1)
                    pe.wait_ge(o_out[par], turn)
                    for j in range(2):
                        for k in range(KD):
                            ins = pe.matmul(po[par][:, j, :], cT[:, par, k, j * P:(j + 1) * P], c.wT[:, 3, k, :],
                                            start=(k == 0), stop=(k == KD - 1))
                    ins.then_inc(o_done[par], 1)


def stage_router(nc, c):
    with ExitStack() as ctx:
        sb = lambda name, shape, dt: ctx.enter_context(nc.sbuf_tensor(name, shape, dt))
        sem = stage_semaphores(nc, ctx)
        pair = lambda name: [sem(name + "_a"), sem(name + "_b")]
        psum = lambda name, shape, dt: ctx.enter_context(nc.psum_tensor(name, shape, dt))
        xt = sb("xt10", [P, 2, 2, D], F32)
        xT = sb("xT10", [P, 2, KD, S], F32)
        xs = sb("xs10", [P, NT, D], F32)
        rr = sb("rr10", [P, NT], F32)
        lg = sb("lg10", [P, NT, NE], F32)
        one_hot = sb("one_hot", [P, NT, NE], F32)
        one_hotb = sb("one_hotb", [P, NT, NE], BF16)
        work = sb("work10", [P, NT, NE], F32)
        row = sb("row10", [P, 2, NT], F32)
        count = sb("count10", [P, 2, NT, NE], F32)
        tiles_i, tiles = sb("tiles_i", [P, NE], I32), sb("tiles10", [P, NE], F32)
        start = sb("start10", [P, 2, NE], F32)
        slot_f = sb("slot_f", [P, NT], F32)
        number, number_i = sb("number10", [P, XT], F32), sb("number_i", [P, XT], I32)
        which, tile_f = sb("which10", [P, XT, NE], F32), sb("tile_f", [P, XT], F32)
        before = sb("before", [P, P], BF16)
        oneb = sb("oneb10", [P, P], BF16)
        pT = psum("pT10", [P, 2, KD, S], F32)
        pl = [psum(f"pl10{i}", [P, 2, NE], F32) for i in range(2)]
        prank, ptotal = psum("prank", [P, NT, NE], F32), psum("ptotal", [P, NT, NE], F32)
        own, sqa, sqd, consts, p_own = (sem(n) for n in ("own10", "sqa10", "sqd10", "consts10", "p_own10"))
        asked, expd, hot, ranked, slotted, scattered = (
            sem(n) for n in ("asked10", "expd10", "hot10", "ranked10", "slotted", "scattered"))
        x_ready, xT_done, xT_out, l_done, l_out, scaled, moved = (
            pair(n) for n in ("x_ready10", "xT_done10", "xT_out10", "l_done10", "l_out10", "scaled10", "moved10"))
        block = ctx.enter_context(nc.Block())

        @block.gpsimd
        def _(pool):
            link = Link(pool, p_own)
            link(pool.iota(number_i[:, :], pattern=[[1, XT]], base=0, channel_multiplier=0))
            link(pool.tensor_copy(number[:, :], number_i[:, :]))
            link(pool.memset(oneb[:, :], 1.0))
            link(pool.affine_select(out=before[:, :], in_=oneb[:, :], compare_op=ALU.is_gt, fill=0.0, base=0,
                                    channel_multiplier=-1, pattern=[[1, P]]))
            pool.sem_inc(consts, 1)
            with pool.Fori(0, NB // 2) as turn:
                for par in range(2):
                    b = turn * 2 + par
                    pool.wait_ge(scaled[par], turn + 1)
                    pool.tensor_tensor(xs[:, ds(b * 2, 2), :], xs[:, ds(b * 2, 2), :],
                                       c.ln_b[:, :].unsqueeze(1).broadcast_to([P, 2, D]), ALU.add)\
                        .then_inc(moved[par], 1)
            pool.wait_ge(slotted, 1)
            for par in range(2):
                pool.wait_ge(moved[par], NB // 2)
            for t in range(NT):
                pool.indirect_dma_start(
                    out=c.sorted_x, out_offset=bass.IndirectOffsetOnAxis(ap=c.slot[:, t:t + 1], axis=0),
                    in_=xs[:, t, :], in_offset=None).then_inc(scattered, 16)
            pool.wait_ge(scattered, 16 * NT)

        @block.vector
        def _(dve):
            link = Link(dve, own)
            rstd_vector(dve, link, c, 1e-5, sqa, sqd, 1)
            link(dve.tensor_tensor(c.veps[:, :], c.rstd[:, :], c.rstd[:, :], ALU.mult))
            link(dve.tensor_tensor(c.veps[:, :], c.veps[:, :], c.var[:, :], ALU.mult))
            link(dve.tensor_scalar(c.veps[:, :], c.veps[:, :], 1e-5, None, ALU.add))
            root(dve, link, c, rr, sqa, sqd, 2)

            with dve.Fori(0, NB // 2) as turn:
                for par in range(2):
                    b = turn * 2 + par
                    dve.wait_ge(xT_done[par], turn)
                    dve.wait_ge(scaled[par], turn)
                    for j in range(2):
                        t = b * 2 + j
                        ins = dve.tensor_scalar(xt[:, par, j, :], c.h[:, ds(t, 1), :], c.mean[:, ds(t, 1)],
                                                c.rstd[:, ds(t, 1)], ALU.subtract, ALU.mult)
                    ins.then_inc(x_ready[par], 1)
                for par in range(2):
                    b = turn * 2 + par
                    dve.wait_ge(x_ready[par], turn + 1)
                    for j in range(2):
                        t = b * 2 + j
                        ins = dve.scalar_tensor_tensor(out=xs[:, ds(t, 1), :], in0=xt[:, par, j, :].unsqueeze(1),
                                                       scalar=rr[:, ds(t, 1)], in1=c.ln_g[:, :].unsqueeze(1),
                                                       op0=ALU.mult, op1=ALU.mult)
                    ins.then_inc(scaled[par], 1)
                for par in range(2):
                    b = turn * 2 + par
                    dve.wait_ge(l_done[par], turn + 1)
                    dve.tensor_tensor(lg[:, ds(b * 2, 2), :], pl[par][:, :, :],
                                      c.br[:, :].unsqueeze(1).broadcast_to([P, 2, NE]), ALU.add)\
                        .then_inc(l_out[par], 1)
            for par in range(2):
                dve.wait_ge(l_out[par], NB // 2)
            wide = lambda a: a.unsqueeze(2).broadcast_to([P, NT, NE])
            link(dve.tensor_reduce(row[:, 0, :], lg[:, :, :], AX.X, ALU.max))
            link(dve.tensor_tensor(lg[:, :, :], lg[:, :, :], wide(row[:, 0, :]), ALU.subtract))
            dve.sem_inc(asked, 1)
            dve.wait_ge(expd, 1)
            link(dve.tensor_reduce(row[:, 1, :], work[:, :, :], AX.X, ALU.add))
            link(dve.reciprocal(row[:, 1, :], row[:, 1, :]))
            link(dve.tensor_tensor(work[:, :, :], work[:, :, :], wide(row[:, 1, :]), ALU.mult))
            link(dve.tensor_reduce(c.gate[:, :], work[:, :, :], AX.X, ALU.max))
            link(dve.tensor_tensor(work[:, :, :], work[:, :, :], wide(c.gate[:, :]), ALU.is_equal))
            dve.wait_ge(consts, 1)
            experts = number[:, 0:NE].unsqueeze(1).broadcast_to([P, NT, NE])
            link(dve.tensor_scalar(work[:, :, :], work[:, :, :], -float(NE), float(NE), ALU.mult, ALU.add))
            link(dve.tensor_tensor(work[:, :, :], work[:, :, :], experts, ALU.add))
            link(dve.tensor_reduce(row[:, 0, :], work[:, :, :], AX.X, ALU.min))
            link(dve.tensor_tensor(one_hot[:, :, :], wide(row[:, 0, :]), experts, ALU.is_equal))
            dve.tensor_copy(one_hotb[:, :, :], one_hot[:, :, :]).then_inc(hot, 1)
            dve.wait_ge(ranked, 1)
            link(dve.tensor_copy(count[:, 0], ptotal[:, :, :]))
            a, b, step = 0, 1, 1
            while step < NT:
                dve.tensor_copy(count[:, b, 0:step, :], count[:, a, 0:step, :])
                link(dve.tensor_tensor(count[:, b, step:, :], count[:, a, step:, :], count[:, a, :NT - step, :],
                                       ALU.add))
                a, b, step = b, a, step * 2
            link(dve.tensor_scalar(tiles_i[:, :], count[:, a, NT - 1, :], 1.0 / P, (P - 1) / 2 / P, ALU.mult,
                                   ALU.add))
            link(dve.tensor_copy(tiles[:, :], tiles_i[:, :]))
            link(dve.memset(start[:, 0, :], 0.0))
            for e in range(1, NE):
                link(dve.tensor_tensor(start[:, 0, e:e + 1], start[:, 0, e - 1:e], tiles[:, e - 1:e], ALU.add))
            link(dve.tensor_scalar(start[:, 1, :], start[:, 0, :], float(P), None, ALU.mult))
            link(dve.tensor_tensor(work[:, :, :], count[:, a], ptotal[:, :, :], ALU.subtract))
            link(dve.tensor_tensor(work[:, :, :], work[:, :, :], prank[:, :, :], ALU.add))
            link(dve.tensor_tensor(work[:, :, :], work[:, :, :],
                                   start[:, 1, :].unsqueeze(1).broadcast_to([P, NT, NE]), ALU.add))
            link(dve.tensor_tensor(work[:, :, :], work[:, :, :], one_hot[:, :, :], ALU.mult))
            link(dve.tensor_reduce(slot_f[:, :], work[:, :, :], AX.X, ALU.add))
            dve.tensor_copy(c.slot[:, :], slot_f[:, :]).then_inc(slotted, 1)
            link(dve.tensor_tensor(which[:, :, :], start[:, 0, :].unsqueeze(1).broadcast_to([P, XT, NE]),
                                   number[:, :].unsqueeze(2).broadcast_to([P, XT, NE]), ALU.is_le))
            link(dve.tensor_reduce(tile_f[:, :], which[:, :, :], AX.X, ALU.add))
            link(dve.tensor_scalar(c.tile_expert[:, :], tile_f[:, :], -1.0, None, ALU.add))

        @block.scalar
        def _(act):
            root_scalar(act, c, sqa, sqd, 1)
            root_scalar(act, c, sqa, sqd, 2)
            with act.Fori(0, NB // 2) as turn:
                for par in range(2):
                    act.wait_ge(xT_done[par], turn + 1)
                    act.activation(xT[:, par], pT[:, par], ACT.Copy).then_inc(xT_out[par], 1)
            act.wait_ge(asked, 1)
            act.activation(work[:, :, :], lg[:, :, :], ACT.Exp).then_inc(expd, 1)

        @block.tensor
        def _(pe):
            with pe.Fori(0, NB // 2) as turn:
                for par in range(2):
                    pe.wait_ge(x_ready[par], turn + 1)
                    pe.wait_ge(xT_out[par], turn)
                    for j in range(2):
                        for k in range(KD):
                            ins = pe.transpose(pT[:, par, k, j * P:(j + 1) * P], xt[:, par, j, k * P:(k + 1) * P],
                                               c.ident[:, :])
                    ins.then_inc(xT_done[par], 1)
                for par in range(2):
                    pe.wait_ge(xT_out[par], turn + 1)
                    pe.wait_ge(l_out[par], turn)
                    for j in range(2):
                        for k in range(KD):
                            ins = pe.matmul(pl[par][:, j, :], xT[:, par, k, j * P:(j + 1) * P], c.wr[:, k, :],
                                            start=(k == 0), stop=(k == KD - 1))
                    ins.then_inc(l_done[par], 1)
            pe.wait_ge(hot, 1)
            pe.wait_ge(consts, 1)
            hots = one_hotb[:, :, :].rearrange("p t e -> p (t e)")
            pe.matmul(ptotal[:, :, :].rearrange("p t e -> p (t e)"), oneb[:, :], hots, start=True, stop=True)
            pe.matmul(prank[:, :, :].rearrange("p t e -> p (t e)"), before[:, :], hots, start=True, stop=True)\
                .then_inc(ranked, 1)


def stage_experts(nc, c):
    FC = FF // P
    with ExitStack() as ctx:
        sb = lambda name, shape, dt: ctx.enter_context(nc.sbuf_tensor(name, shape, dt))
        sem = stage_semaphores(nc, ctx)
        psum = lambda name, shape, dt: ctx.enter_context(nc.psum_tensor(name, shape, dt))
        w1, w2, b1, b2 = c.ew1, c.ew2, c.eb1, c.eb2
        x = sb("x11", [P, 2, D], F32)
        xT = sb("xT11", [P, 2, KD, P], F32)
        w1_now = sb("w1_now", [P, 2, KD, FF], F32)
        b1_now = sb("b1_now", [P, 2, FC], F32)
        hT = sb("hT11", [P, 2, FC, P], F32)
        y = sb("y11", [P, 2, D], F32)
        pT = [psum(f"pT11{i}", [P, KD, P], F32) for i in range(2)]
        ph = [psum(f"ph11{i}", [P, 4, P], F32) for i in range(4)]
        py = [psum(f"py11{i}", [P, D], F32) for i in range(2)]
        w_in = sem("w_in11")
        w2_in = sem("w2_in11")
        x_in, y_out, y_stored = ([sem(f"{n}{i}") for i in range(2)] for n in ("x_in11", "y_out11", "y_stored11"))
        xT_done, xT_out, w_ready, h_done, h_out, y_done = (
            sem(n) for n in ("xT_done11", "xT_out11", "w_ready11", "h_done11", "h_out11", "y_done11"))
        block = ctx.enter_context(nc.Block())

        def tiles(eng, body):
            body(0, 0, 0, True)
            body(1, 1, 0, True)
            with eng.Fori(1, XT // 2) as turn:
                body(turn * 2, 0, turn, False)
                body(turn * 2 + 1, 1, turn, False)
            if XT % 2:
                body(XT - 1, 0, XT // 2, False)

        @block.sync
        def _(sp):
            i = c.ins
            for e in range(NE):
                sp.dma_start(w1[:, e], i["L1_ffn_W1"][e].rearrange("(k p) f -> p k f", p=P)).then_inc(w_in, 16)
            sp.dma_start(b1[:, :], i["L1_ffn_b1"]).then_inc(w_in, 16)
            for e in range(NE):
                sp.dma_start(w2[:, e], i["L1_ffn_W2"][e].rearrange("(m p) d -> p m d", p=P)).then_inc(w2_in, 16)
                sp.dma_start(b2[:, e, :], i["L1_ffn_b2"][e].partition_broadcast(P)).then_inc(w2_in, 16)

            def body(t, par, n, first):
                if not first:
                    sp.wait_ge(xT_done, t - 1)
                sp.dma_start(x[:, par, :], c.sorted_x[ds(t * P, P), :]).then_inc(x_in[par], 16)
            tiles(sp, body)

        @block.gpsimd
        def _(pool):
            def body(t, par, n, first):
                pool.wait_ge(y_out[par], n + 1)
                pool.dma_start(c.sorted_y[ds(t * P, P), :], y[:, par, :]).then_inc(y_stored[par], 16)
            tiles(pool, body)
            for par in range(2):
                pool.wait_ge(y_stored[par], 16 * ((XT + 1 - par) // 2))

        @block.vector
        def _(dve):
            def body(t, par, n, first):
                e = dve.value_load(c.tile_expert[0:1, ds(t, 1)], min_val=0, max_val=NE - 1)
                if not first:
                    dve.wait_ge(h_done, t * 2 - 2)
                    dve.wait_ge(h_out, t * 2 - 2)
                elif par == 0:
                    dve.wait_ge(w_in, 16 * (NE + 1))
                dve.tensor_copy(b1_now[:, par, :], b1[:, ds(e * FC, FC)])
                dve.tensor_copy(w1_now[:, par].rearrange("p k f -> p (k f)"),
                                w1[:, ds(e, 1)].rearrange("p a k f -> p (a k f)")).then_inc(w_ready, 1)
                if not first or par == 1:
                    output(t - 1, 1 - par, n if par == 1 else n - 1)
                    
            def output(t, par, n):
                e = dve.value_load(c.tile_expert[0:1, ds(t, 1)], min_val=0, max_val=NE - 1)
                dve.wait_ge(y_done, t + 1)
                if not isinstance(n, int) or n > 0:
                    dve.wait_ge(y_stored[par], n * 16)
                dve.tensor_tensor(y[:, par, :], py[par][:, :], b2[:, ds(e, 1)].rearrange("p a d -> p (a d)"), ALU.add)\
                    .then_inc(y_out[par], 1)

            tiles(dve, body)
            output(XT - 1, (XT - 1) % 2, (XT - 1) // 2)

        @block.scalar
        def _(act):
            def turned(t, par):
                act.wait_ge(xT_done, t + 1)
                act.activation(xT[:, par], pT[par][:, :, :], ACT.Copy).then_inc(xT_out, 1)

            def body(t, par, n, first):
                if first and par == 0:
                    turned(t, par)
                if not (isinstance(t, int) and t == XT - 1):
                    turned(t + 1, 1 - par)
                if not first:
                    act.wait_ge(y_done, t - 1)
                for half in range(2):
                    act.wait_ge(h_done, t * 2 + half + 1)
                    for q in range(4):
                        m = half * 4 + q
                        ins = act.activation(hT[:, par, m, :], ph[par * 2 + half][:, q, :], ACT.Relu,
                                             bias=b1_now[:, par, m:m + 1])
                    ins.then_inc(h_out, 1)
            tiles(act, body)

        @block.tensor
        def _(pe):
            def turn_x(t, par, n, first):
                pe.wait_ge(x_in[par], (n + 1) * 16)
                if not first:
                    pe.wait_ge(xT_out, t - 1)
                for k in range(KD):
                    ins = pe.transpose(pT[par][:, k, :], x[:, par, k * P:(k + 1) * P], c.ident[:, :])
                ins.then_inc(xT_done, 1)

            def second(t, par):
                e = pe.value_load(c.tile_expert[0:1, ds(t, 1)], min_val=0, max_val=NE - 1)
                for m in range(FC):
                    if m % 4 == 0:
                        pe.wait_ge(h_out, t * 2 + m // 4 + 1)
                    ins = pe.matmul(py[par][:, :], hT[:, par, m, :],
                                    w2[:, ds(e, 1), m, :].rearrange("p a d -> p (a d)"),
                                    start=(m == 0), stop=(m == FC - 1))
                ins.then_inc(y_done, 1)

            def body(t, par, n, first):
                if first and par == 0:
                    turn_x(0, 0, 0, True)
                pe.wait_ge(w_ready, t + 1)
                pe.wait_ge(xT_out, t + 1)
                if not first:
                    pe.wait_ge(h_out, t * 2 - 2)
                for m in range(FC):
                    for k in range(KD):
                        ins = pe.matmul(ph[par * 2 + m // 4][:, m % 4, :], w1_now[:, par, k, m * P:(m + 1) * P],
                                        xT[:, par, k, :], start=(k == 0), stop=(k == KD - 1))
                    if m % 4 == 3:
                        ins.then_inc(h_done, 1)
                if not (isinstance(t, int) and t == XT - 1):
                    turn_x(t + 1, 1 - par, n if par == 0 else n + 1, first and par == 0)
                if first and par == 0:
                    pe.wait_ge(w2_in, 32 * NE)
                elif first:
                    second(0, 0)
                else:
                    if par == 0 or True:
                        pe.wait_ge(y_out[1 - par], (n - 1) if par == 0 else n)
                    second(t - 1, 1 - par)
            tiles(pe, body)
            pe.wait_ge(y_out[(XT - 1) % 2], (XT - 1) // 2)
            second(XT - 1, (XT - 1) % 2)


def stage_output(nc, c):
    RING = 8
    with ExitStack() as ctx:
        sem = stage_semaphores(nc, ctx)
        y = ctx.enter_context(nc.sbuf_tensor("y12", [P, RING, D], F32))
        fetched = [sem(f"fetched{i}") for i in range(RING)]
        added, stored = sem("added12"), sem("stored12")
        block = ctx.enter_context(nc.Block())

        @block.gpsimd
        def _(pool):
            for t in range(NT):
                if t >= RING:
                    pool.wait_ge(added, t - RING + 1)
                pool.indirect_dma_start(
                    out=y[:, t % RING, :], out_offset=None, in_=c.sorted_y,
                    in_offset=bass.IndirectOffsetOnAxis(ap=c.slot[:, t:t + 1], axis=0))\
                    .then_inc(fetched[t % RING], 16)

        @block.vector
        def _(dve):
            for t in range(NT):
                dve.wait_ge(fetched[t % RING], 16 * (t // RING + 1))
                dve.scalar_tensor_tensor(out=c.h[:, t, :], in0=y[:, t % RING, :], scalar=c.gate[:, t:t + 1],
                                         in1=c.h[:, t, :], op0=ALU.mult, op1=ALU.add).then_inc(added, 1)

        @block.sync
        def _(sp):
            for b in range(NB):
                sp.wait_ge(added, b * 2 + 2)
                sp.dma_start(c.out[b].rearrange("(j p) d -> p j d", p=P), c.h[:, 2 * b:2 * b + 2, :])\
                    .then_inc(stored, 16)
            sp.wait_ge(stored, 16 * NB)


def second_layer_attention(nc, c):
    with ExitStack() as ctx:
        sb = lambda name, shape, dt: ctx.enter_context(nc.sbuf_tensor(name, shape, dt))
        dram = lambda name, shape, dt: nc.dram_tensor(name, shape, dt).ap()
        c.nv = sb("nv", [P, NT, D], BF16)
        c.qscale, c.vinv = sb("qscale", [P, 2 * NBLK + 1], F32), sb("vinv", [P, 1], F32)
        c.ex_dram = dram("ex_dram", (NB * PC, P, 1024), F32)
        c.sum_dram = dram("sum_dram", (NB, PC, 512), F32)
        with ExitStack() as proj:
            sb1 = lambda name, shape, dt: proj.enter_context(nc.sbuf_tensor(name, shape, dt))
            c.qk32, c.v32 = sb1("qk32", [P, 4, NB * S], F32), sb1("v32", [P, NT, D], F32)
            c.qs_row, c.qi_row = sb1("qs_row", [P, 2, S], F32), sb1("qi_row", [P, 2, S], F32)
            stage_l1_project(nc, c)
            stage_l1_quantise(nc, c)
        stage_l1_exponentials(nc, c)
        c.inv_dram = dram("inv_dram", (NB, PC, 512), F32)
        with ExitStack() as context:
            c.ctx = context.enter_context(nc.sbuf_tensor("ctx", [P, NT, D], F32))
            c.cmax = context.enter_context(nc.sbuf_tensor("cmax", [P, NB], F32))
            stage_l1_context(nc, c)
            stage_l1_output(nc, c)


def second_layer_ffn(nc, c):
    with ExitStack() as ctx:
        sb = lambda name, shape, dt: ctx.enter_context(nc.sbuf_tensor(name, shape, dt))
        c.gate, c.slot = sb("gate", [P, NT], F32), sb("slot", [P, NT], I32)
        c.tile_expert = sb("tile_expert", [P, XT], I32)
        stage_router(nc, c)
        with ExitStack() as experts:
            sb1 = lambda name, shape, dt: experts.enter_context(nc.sbuf_tensor(name, shape, dt))
            c.ew1, c.ew2 = sb1("ew1", [P, NE, KD, FF], F32), sb1("ew2", [P, NE, FF // P, D], F32)
            c.eb1, c.eb2 = sb1("eb1", [P, NE * FF // P], F32), sb1("eb2", [P, NE, D], F32)
            stage_experts(nc, c)
        stage_output(nc, c)


FIRST_LAYER = [stage_setup, stage_l0_project, stage_l0_attention, stage_l0_ffn]


def build(nc, ins, out):
    with ExitStack() as ctx:
        sb = lambda name, shape, dt: ctx.enter_context(nc.sbuf_tensor(name, shape, dt))
        dram = lambda name, shape, dt: nc.dram_tensor(name, shape, dt).ap()
        c = Core()
        c.ins, c.out = ins, out
        c.h = sb("h", [P, NT, D], F32)
        c.stats = sb("stats", [P, NT, 6], F32)
        c.mean, c.var, c.veps = (sb(n, [P, NT], F32) for n in ("mean", "var", "veps"))
        c.rstd, c.sd = sb("rstd", [P, NT], F32), sb("sd", [P, NT], F32)
        c.small = sb("small", [P, 2, NT], F32)
        c.ident, c.identb = sb("ident", [P, P], F32), sb("identb", [P, P], BF16)
        c.wr, c.br = sb("wr", [P, KD, NE], F32), sb("br", [P, NE], F32)
        c.ln_g, c.ln_b = sb("ln_g", [P, D], F32), sb("ln_b", [P, D], F32)
        c.qk_dram = dram("qk_dram", (NB, 3, 4 * P, S), BF16)
        c.sorted_x = dram("sorted_x", (XT * P, D), F32)
        c.sorted_y = dram("sorted_y", (XT * P, D), F32)
        with ExitStack() as attention:
            sb2 = lambda name, shape, dt: attention.enter_context(nc.sbuf_tensor(name, shape, dt))
            c.sel = sb2("sel", [3 * H, H, P], BF16)
            c.wT = sb2("wT", [P, 4, KD, D], BF16)
            c.wscale = sb2("wscale", [P, 8], F32)
            c.wvo = sb2("wvo", [P, 2, D], F32)
            c.bqk = sb2("bqk", [P, 4], F32)
            c.bv, c.bo = sb2("bv", [P, D], F32), sb2("bo", [P, D], F32)
            with ExitStack() as first:
                sb1 = lambda name, shape, dt: first.enter_context(nc.sbuf_tensor(name, shape, dt))
                c.wqkv, c.wo0 = sb1("wqkv", [P, KD, 3 * D], F32), sb1("wo0", [P, KD, D], F32)
                c.mask_qk, c.mask_kq = sb1("mask_qk", [P, 3, P], BF16), sb1("mask_kq", [P, 2, P], BF16)
                c.mask4 = sb1("mask4", [P, 4, 512], BF16)
                c.win = sb1("win", [P, KD, M_UNITS], F32)
                c.w1col, c.b1col = sb1("w1col", [P, 8], F32), sb1("b1col", [P, 8], F32)
                c.bin, c.b2u = sb1("bin", [M_UNITS, 1], F32), sb1("b2u", [M_UNITS, 1], F32)
                c.w2m, c.spread = sb1("w2m", [P, NBLK, M_UNITS], F32), sb1("spread", [M_UNITS, NBLK, P], F32)
                c.wout = sb1("wout", [M_UNITS + 1, D], F32)
                c.vaug = sb1("vaug", [P, NT, H, VA], F32)
                for stage in FIRST_LAYER:
                    stage(nc, c)
            second_layer_attention(nc, c)
        second_layer_ffn(nc, c)


COLUMNS = ("x", "L0_attn_g", "L0_ffn_W1", "L0_ffn_b1", "L0_ffn_W2", "L1_attn_bq", "L1_attn_bk", "L1_ffn_b1")


def kernel(**inputs):
    import concourse.bacc as bacc
    from concourse.bass_utils import run_bass_kernel_spmd

    nc = bacc.Bacc("TRN2", target_bir_lowering=False, num_devices=1)
    arrays, ins = {}, {}
    for name, value in inputs.items():
        a = np.asarray(value)
        if name == "L0_tok_weight":
            name, a = "table", a.T
        elif name in COLUMNS:
            a = a.reshape(-1, P).T
        a = np.ascontiguousarray(a)
        arrays["in_" + name] = a
        ins[name] = nc.dram_tensor("in_" + name, a.shape, mybir.dt.from_np(a.dtype), kind="ExternalInput").ap()
    out = nc.dram_tensor("out", (NB, S, D), F32, kind="ExternalOutput").ap()
    build(nc, ins, out)
    result = run_bass_kernel_spmd(nc, [arrays], core_ids=[0])
    return result.results[0]["out"]
```

```python
from contextlib import ExitStack

import numpy as np

import concourse.bass as bass
from concourse import mybir

F32 = mybir.dt.float32
BF16 = mybir.dt.bfloat16
I32 = mybir.dt.int32
U32 = mybir.dt.uint32
I16 = mybir.dt.int16
ALU = mybir.AluOpType
ACT = mybir.ActivationFunctionType
AX = mybir.AxisListType
RMAX = bass.bass_isa.ReduceOp.max
ds = bass.ds

P = 128
NB, S, D = 16, 256, 256
NT = NB * S // P
KD = D // P
H, DH = 16, 16
NBLK = 8
M_UNITS, INNER = 64, 16
NE, FF = 8, 1024
QMAX = 127.0
NEG = -1e30
VA = DH + 1
XT = NT + NE - 1
SPLIT_Q = (0, 0, 1, 0, 2, 1)
SPLIT_K = (0, 1, 0, 2, 0, 1)


def pla_table():
    xs = np.linspace(-10.0, 0.0, 1001)
    ys = np.exp(xs)
    edges = np.linspace(-10.0, 0.0, 13)
    ms, cs = [], []
    for i in range(12):
        inside = (xs >= edges[i]) & (xs <= edges[i + 1])
        a, b = np.polyfit(xs[inside], ys[inside], 1)
        ms.append(float(a))
        cs.append(float(b))
    return ms, cs


def stage_semaphores(nc, ctx):
    taken = []

    def give_back():
        nc.clear_and_free_semaphores(taken)
        nc.all_engine_barrier()

    def sem(name):
        taken.append(nc.alloc_semaphore(name))
        return taken[-1]

    ctx.callback(give_back)
    return sem


class Link:

    def __init__(self, eng, sem):
        self.eng, self.sem, self.n, self.base = eng, sem, 0, None

    def loop(self, turn, per_turn):
        self.start, self.per_turn = self.n, per_turn
        self.base = turn * per_turn + self.n
        self.n = 0

    def end(self, turns):
        assert self.n == self.per_turn, self.n
        self.n = self.start + turns * self.per_turn
        self.base = None

    def __call__(self, ins):
        ins.then_inc(self.sem, 1)
        self.n += 1
        self.eng.wait_ge(self.sem, self.n if self.base is None else self.base + self.n)


class Core:
    pass


def rstd_vector(dve, link, c, eps, sqrt_asked, sqrt_done, asks):
    st, a, b = c.stats, c.small[:, 0, :], c.small[:, 1, :]
    link(dve.tensor_tensor(a, st[:, :, 1], st[:, :, 4], ALU.add))
    link(dve.tensor_scalar(c.mean[:, :], a, 0.5, None, ALU.mult))
    link(dve.tensor_tensor(a, st[:, :, 1], st[:, :, 4], ALU.subtract))
    link(dve.tensor_tensor(a, a, a, ALU.mult))
    link(dve.tensor_tensor(b, st[:, :, 2], st[:, :, 5], ALU.add))
    link(dve.tensor_scalar(b, b, 1.0 / D, None, ALU.mult))
    link(dve.scalar_tensor_tensor(out=c.var[:, :], in0=a, scalar=0.25, in1=b, op0=ALU.mult, op1=ALU.add))
    link(dve.tensor_scalar(c.veps[:, :], c.var[:, :], eps, None, ALU.add))
    root(dve, link, c, c.rstd, sqrt_asked, sqrt_done, asks)


def root(dve, link, c, out, sqrt_asked, sqrt_done, asks):
    b = c.small[:, 1, :]
    dve.sem_inc(sqrt_asked, 1)
    dve.wait_ge(sqrt_done, asks)
    link(dve.reciprocal(out[:, :], c.sd[:, :]))
    link(dve.tensor_tensor(b, out[:, :], out[:, :], ALU.mult))
    link(dve.tensor_tensor(b, b, c.veps[:, :], ALU.mult))
    link(dve.tensor_scalar(b, b, -0.5, 1.5, ALU.mult, ALU.add))
    link(dve.tensor_tensor(out[:, :], out[:, :], b, ALU.mult))


def root_scalar(act, c, sqrt_asked, sqrt_done, asks):
    act.wait_ge(sqrt_asked, asks)
    act.activation(c.sd[:, :], c.veps[:, :], ACT.Sqrt).then_inc(sqrt_done, 1)


def stage_setup(nc, c):
    with ExitStack() as ctx:
        sb = lambda name, shape, dt: ctx.enter_context(nc.sbuf_tensor(name, shape, dt))
        sem = stage_semaphores(nc, ctx)
        idx = sb("idx", [P, NT], I32)
        tok_bias = sb("tok_bias", [P, D], F32)
        gcol = sb("gcol", [P, KD], F32)
        ones = sb("ones_tmp", [P, P], F32)
        wl1 = sb("wl1", [P, 4, KD, D], F32)
        wi = sb("wi", [P, 4, KD, D], I16)
        wb = sb("wb", [P, 4, KD, D], BF16)
        wa = sb("wa", [P, 8], F32)
        wz = sb("wz", [P, 8], F32)
        winv = sb("winv", [P, 8], F32)
        wrow = sb("wrow", [P, 4, P], F32)
        zero = sb("zero", [P, D], F32)
        pw = ctx.enter_context(nc.psum_tensor("pw", [P, 4, KD, 2 * D], BF16))
        pr = ctx.enter_context(nc.psum_tensor("pr", [P, 2, D], F32))
        idx_in, bias_in, g_in, w1_in, w_in = (sem(n) for n in ("idx_in", "bias_in", "g_in", "lw_in", "w_in"))
        rows_in = [sem(f"rows_in{i}") for i in range(4)]
        zero_set, zero_out = sem("zero_set"), sem("zero_out")
        pool_own, dve_own = sem("pool_own0"), sem("dve_own0")
        consts_set, wq_ready, wT, wT_out, wr_ready, wr, masked = (
            sem(n) for n in ("consts_set", "wq_ready", "wT", "wT_out", "wr_ready", "wr", "w2_masked"))
        block = ctx.enter_context(nc.Block())
        i = c.ins

        @block.sync
        def _(sp):
            sp.dma_start(idx[:, :], i["x"]).then_inc(idx_in, 16)
            sp.dma_start(tok_bias[:, :], i["L0_tok_bias"].partition_broadcast(P)).then_inc(bias_in, 16)
            for n, w in enumerate(("Wq", "Wk", "Wv", "Wo")):
                sp.dma_start(wl1[:, n], i[f"L1_attn_{w}"].rearrange("(m p) i -> p m i", p=P)).then_inc(w1_in, 16)
            sp.dma_start(gcol[:, :], i["L0_attn_g"]).then_inc(g_in, 16)
            sp.dma_start(c.wqkv[:, :, :], i["L0_attn_Wqkv"].rearrange("(k p) n -> p k n", p=P)).then_inc(g_in, 16)
            sp.dma_start(c.w2col[:, :], i["L0_ffn_W2"]).then_inc(g_in, 16)
            sp.dma_start(c.wo0[:, :, :], i["L0_attn_Wo"].rearrange("(k p) n -> p k n", p=P)).then_inc(w_in, 16)
            sp.dma_start(c.win[:, :, :], i["L0_ffn_Win"].rearrange("(k p) n -> p k n", p=P)).then_inc(w_in, 16)
            sp.dma_start(c.w1col[:, :], i["L0_ffn_W1"]).then_inc(w_in, 16)
            sp.dma_start(c.b1col[:, :], i["L0_ffn_b1"]).then_inc(w_in, 16)
            sp.dma_start(c.bin[:, :], i["L0_ffn_bin_"].rearrange("(p a) -> p a", a=1)).then_inc(w_in, 16)
            sp.dma_start(c.b2u[:, :], i["L0_ffn_b2"].rearrange("(p a) -> p a", a=1)).then_inc(w_in, 16)
            sp.dma_start(c.wout[0:M_UNITS, :], i["L0_ffn_Wout"]).then_inc(w_in, 16)
            sp.dma_start(c.wout[M_UNITS:M_UNITS + 1, :], i["L0_ffn_bout"].rearrange("(a n) -> a n", a=1))\
                .then_inc(w_in, 16)
            sp.dma_start(c.bqk[:, 0:2], i["L1_attn_bq"]).then_inc(w_in, 16)
            sp.dma_start(c.bqk[:, 2:4], i["L1_attn_bk"]).then_inc(w_in, 16)
            sp.dma_start(c.bv[:, :], i["L1_attn_bv"].partition_broadcast(P)).then_inc(w_in, 16)
            sp.dma_start(c.bo[:, :], i["L1_attn_bo"].partition_broadcast(P)).then_inc(w_in, 16)
            sp.dma_start(c.wr[:, :, :], i["L1_ffn_Wr"].rearrange("(k p) n -> p k n", p=P)).then_inc(w_in, 16)
            sp.dma_start(c.br[:, :], i["L1_ffn_br"].partition_broadcast(P)).then_inc(w_in, 16)
            sp.dma_start(c.ln_g[:, :], i["L1_ffn_ln_g"].partition_broadcast(P)).then_inc(w_in, 16)
            sp.dma_start(c.ln_b[:, :], i["L1_ffn_ln_b"].partition_broadcast(P)).then_inc(w_in, 16)
            sp.wait_ge(zero_set, 1)
            for t in range(XT):
                sp.dma_start(c.sorted_x[t * P:(t + 1) * P, :], zero[:, :]).then_inc(zero_out, 16)
            sp.wait_ge(w_in, 16 * 16)
            sp.wait_ge(zero_out, 16 * XT)

        @block.gpsimd
        def _(pool):
            link = Link(pool, pool_own)
            link(pool.memset(ones[:, :], 1.0))
            link(pool.memset(c.ident[:, :], 0.0))
            pick = lambda out, in_, op, fill, base, cm, pattern: link(pool.affine_select(
                out=out, in_=in_, compare_op=op, fill=fill, base=base, channel_multiplier=cm, pattern=pattern))
            pick(c.ident[:, :], c.ident[:, :], ALU.not_equal, 1.0, 0, 1, [[-1, P]])
            link(pool.tensor_copy(c.identb[:, :], c.ident[:, :]))
            pool.sem_inc(consts_set, 1)
            pool.wait_ge(idx_in, 16)
            for t in range(NT):
                pool.indirect_dma_start(
                    out=c.h[:, t, :], out_offset=None, in_=i["table"],
                    in_offset=bass.IndirectOffsetOnAxis(ap=idx[:, t:t + 1], axis=0)).then_inc(rows_in[t // 8], 16)

        @block.vector
        def _(dve):
            link = Link(dve, dve_own)
            dve.memset(zero[:, :], 0.0).then_inc(zero_set, 1)
            dve.wait_ge(w1_in, 64)
            w8 = wl1[:, :, :, :].rearrange("p n m i -> p (n m) i")
            link(dve.tensor_reduce(wa[:, :], w8, AX.X, ALU.max, apply_absolute_value=True))
            link(dve.tensor_scalar(wa[:, :], wa[:, :], 1.0 / QMAX, None, ALU.mult))
            link(dve.tensor_scalar(wz[:, :], wa[:, :], 0.0, None, ALU.is_equal))
            link(dve.tensor_tensor(c.wscale[:, :], wa[:, :], wz[:, :], ALU.add))
            link(dve.reciprocal(winv[:, :], c.wscale[:, :]))
            for n in range(8):
                link(dve.tensor_scalar(wi[:, n // 2, n % 2, :], wl1[:, n // 2, n % 2, :], winv[:, n:n + 1], None,
                                       ALU.mult))
            dve.tensor_copy(wb[:, :, :, :], wi[:, :, :, :]).then_inc(wq_ready, 1)
            dve.wait_ge(bias_in, 16)
            for t in range(NT):
                if t % 8 == 0:
                    dve.wait_ge(rows_in[t // 8], 16 * 8)
                link(dve.tensor_tensor(c.h[:, t, :], c.h[:, t, :], tok_bias[:, :], ALU.add))
                dve.bn_stats(c.stats[:, t, :], c.h[:, t, :])
            dve.wait_ge(consts_set, 1)
            for n in range(4):
                t = dve.tensor_scalar(wrow[:, n, :], ones[:, 0:P], c.wscale[:, 4 + n:5 + n], None, ALU.mult)
            t.then_inc(wr_ready, 1)
            dve.wait_ge(g_in, 48)
            for k in range(KD):
                link(dve.tensor_scalar(c.wqkv[:, k, :], c.wqkv[:, k, :], gcol[:, k:k + 1], None, ALU.mult))
            dve.wait_ge(wT, 1)
            dve.tensor_copy(c.wT[:, :, :, :], pw[:, :, :, 0:D])
            dve.wait_ge(wr, 1)
            dve.tensor_copy(c.wvo[:, :, :], pr[:, :, :])

        @block.tensor
        def _(pe):
            pe.wait_ge(wq_ready, 1)
            pe.wait_ge(consts_set, 1)
            for n in range(4):
                for m in range(KD):
                    for k in range(KD):
                        t = pe.transpose(pw[:, n, k, m * P:(m + 1) * P], wb[:, n, m, k * P:(k + 1) * P],
                                         c.identb[:, :])
            t.then_inc(wT, 1)
            pe.wait_ge(wr_ready, 1)
            for n in range(4):
                t = pe.matmul(pr[:, n // 2, (n % 2) * P:(n % 2 + 1) * P], wrow[:, n, :], c.ident[:, :],
                              start=True, stop=True)
            t.then_inc(wr, 1)


def need(eng, sem_, value):
    if not isinstance(value, int) or value > 0:
        eng.wait_ge(sem_, value)


def ahead(eng, first, rest, turns, ways=2):
    for way in range(ways):
        first(way, 0)
    with eng.Fori(0, turns - 1) as turn:
        for step, t in ((first, turn + 1), (rest, turn)):
            for way in range(ways):
                step(way, t)
    for way in range(ways):
        rest(way, turns - 1)


def start_at(eng, value, *pairs):
    for both in pairs:
        for one in both:
            eng.sem_inc(one, value)


def stage_l0_project(nc, c):
    with ExitStack() as ctx:
        sb = lambda name, shape, dt: ctx.enter_context(nc.sbuf_tensor(name, shape, dt))
        sem = stage_semaphores(nc, ctx)
        pair = lambda name: [sem(name + "_a"), sem(name + "_b")]
        xn = sb("xn", [P, 2, 2, D], F32)
        xT = sb("xT", [P, 2, KD, S], F32)
        rest = sb("rest", [P, 2, 4, S], F32)
        parts = sb("parts", [P, 2, 3, 4, S], BF16)
        rall, rp1, mr = sb("rall", [P, NT], F32), sb("rp1", [P, NT], F32), sb("mr", [P, NT], F32)
        pT = ctx.enter_context(nc.psum_tensor("pT", [P, 2, KD, S], F32))
        pqk = ctx.enter_context(nc.psum_tensor("pqk", [P, 2, 4, S], F32))
        pv = ctx.enter_context(nc.psum_tensor("pv", [P, 2, 2, D], F32))
        own, sqa, sqd, pool_own = sem("own1"), sem("sqa1"), sem("sqd1"), sem("pool_own1")
        ones = sb("ones_tmp1", [P, 1024], F32)
        zb = sb("zeros_tmp1", [P, P], BF16)[:, :]
        x_ready, xT_done, xT_out, qk_done, v_done, v_out, hi_out, mid_in, mid_out, low_out, stored = (
            pair(n) for n in ("x_ready", "xT_done", "xT_out", "qk_done", "v_done", "v_out", "hi_out", "mid_in",
                              "mid_out", "low_out", "stored"))
        block = ctx.enter_context(nc.Block())

        @block.vector
        def _(dve):
            link = Link(dve, own)
            rstd_vector(dve, link, c, 1e-5, sqa, sqd, 1)
            link(dve.tensor_tensor(c.veps[:, :], c.rstd[:, :], c.rstd[:, :], ALU.mult))
            link(dve.tensor_tensor(c.veps[:, :], c.veps[:, :], c.var[:, :], ALU.mult))
            link(dve.tensor_scalar(c.veps[:, :], c.veps[:, :], 1e-6, None, ALU.add))
            root(dve, link, c, rall, sqa, sqd, 2)
            link(dve.tensor_tensor(rall[:, :], rall[:, :], c.rstd[:, :], ALU.mult))
            link(dve.tensor_scalar(rp1[:, :], c.rstd[:, :], 1.0, None, ALU.add))
            link(dve.tensor_tensor(mr[:, :], c.mean[:, :], c.rstd[:, :], ALU.mult))

            def normalise(b, par, turn):
                dve.wait_ge(xT_done[par], turn + 1)
                for j in range(2):
                    t = b * 2 + j
                    ins = dve.tensor_scalar(xn[:, par, j, :], c.h[:, ds(t, 1), :], c.mean[:, ds(t, 1)],
                                            rall[:, ds(t, 1)], ALU.subtract, ALU.mult)
                ins.then_inc(x_ready[par], 1)
                for j in range(2):
                    t = b * 2 + j
                    dve.tensor_scalar(c.h[:, ds(t, 1), :], c.h[:, ds(t, 1), :], rp1[:, ds(t, 1)],
                                      mr[:, ds(t, 1)], ALU.mult, ALU.subtract)

            def split(par, turn):
                dve.wait_ge(hi_out[par], turn + 1)
                dve.tensor_tensor(rest[:, par], pqk[:, par], parts[:, par, 0], ALU.subtract)\
                    .then_inc(mid_in[par], 1)
                dve.wait_ge(mid_out[par], turn + 1)
                dve.tensor_tensor(parts[:, par, 2], rest[:, par], parts[:, par, 1], ALU.subtract)\
                    .then_inc(low_out[par], 1)

            ahead(dve, lambda par, turn: normalise(turn * 2 + par, par, turn), split, NB // 2)

        @block.scalar
        def _(act):
            root_scalar(act, c, sqa, sqd, 1)
            root_scalar(act, c, sqa, sqd, 2)
            with act.Fori(0, NB // 2) as turn:
                for par in range(2):
                    act.wait_ge(xT_done[par], turn + 2)
                    act.activation(xT[:, par], pT[:, par], ACT.Copy).then_inc(xT_out[par], 1)
                for par in range(2):
                    act.wait_ge(qk_done[par], turn + 1)
                    act.wait_ge(stored[par], turn * 16 + 16)
                    act.activation(parts[:, par, 0], pqk[:, par], ACT.Copy).then_inc(hi_out[par], 1)
                    act.wait_ge(v_done[par], turn + 1)
                    for j in range(2):
                        t = turn * 4 + par * 2 + j
                        ins = act.activation(c.vaug[:, ds(t, 1), :, 0:DH],
                                             pv[:, par, j, :].rearrange("p (a h d) -> p a h d", a=1, h=H), ACT.Copy)
                    ins.then_inc(v_out[par], 1)
                    act.wait_ge(mid_in[par], turn + 2)
                    act.activation(parts[:, par, 1], rest[:, par], ACT.Copy).then_inc(mid_out[par], 1)

        @block.gpsimd
        def _(pool):
            link = Link(pool, pool_own)
            pool.memset(c.vaug[:, :, :, DH:VA], 1.0)
            link(pool.memset(ones[:, :], 1.0))
            link(pool.memset(zb, 0.0))
            link(pool.memset(c.sel[:, :, :], 0.0))
            pick = lambda out, in_, op, fill, base, cm, pattern: link(pool.affine_select(
                out=out, in_=in_, compare_op=op, fill=fill, base=base, channel_multiplier=cm, pattern=pattern))
            pick(c.mask_qk[:, 0, :], zb, ALU.is_ge, NEG, 0, 1, [[-1, P]])
            pick(c.mask_qk[:, 1, :], zb, ALU.is_gt, NEG, 0, -1, [[1, P]])
            pick(c.mask_qk[:, 2, :], zb, ALU.is_ge, NEG, 0, 1, [[-1, P]])
            pick(c.mask_kq[:, 0, :], zb, ALU.is_ge, NEG, 0, -1, [[1, P]])
            pick(c.mask_kq[:, 1, :], zb, ALU.is_gt, NEG, 0, 1, [[-1, P]])
            for x in range(4):
                cut = slice(x * P, (x + 1) * P)
                pool.tensor_copy(c.mask4[:, 0, cut], c.mask_qk[:, 0, :])
                pool.tensor_copy(c.mask4[:, 1, cut], c.mask_qk[:, 1 + x % 2, :])
                pool.tensor_copy(c.mask4[:, 2, cut], c.mask_kq[:, x % 2, :])
                link(pool.tensor_copy(c.mask4[:, 3, cut], c.mask_kq[:, 0, :]))
            for part in range(3):
                pick(c.sel[:, :, :], c.sel[:, :, :], ALU.not_equal, 1.0, -H * part, 1, [[-1, H], [0, P]])
            sp_, on = c.spread[:, :, :], ones[0:M_UNITS, 0:1024].rearrange("p (j q) -> p j q", j=NBLK)
            pick(sp_, on, ALU.is_ge, 0.0, 0, -INNER, [[P, NBLK], [1, P]])
            pick(sp_, sp_, ALU.is_ge, 0.0, INNER - 1, INNER, [[-P, NBLK], [-1, P]])
            wm, on = c.w2m[:, :, :], ones[:, 0:512].rearrange("p (j m) -> p j m", j=NBLK)
            pick(wm, on, ALU.is_ge, 0.0, 0, 1, [[P, NBLK], [-INNER, M_UNITS]])
            pick(wm, wm, ALU.is_ge, 0.0, INNER - 1, -1, [[-P, NBLK], [INNER, M_UNITS]])

        @block.tensor
        def _(pe):
            start_at(pe, 1, mid_in, v_out, xT_done, xT_out)
            start_at(pe, 16, stored)
            with pe.Fori(0, NB // 2) as turn:
                for par in range(2):
                    pe.wait_ge(x_ready[par], turn + 1)
                    pe.wait_ge(xT_out[par], turn + 1)
                    for j in range(2):
                        for k in range(KD):
                            ins = pe.transpose(pT[:, par, k, j * P:(j + 1) * P], xn[:, par, j, k * P:(k + 1) * P],
                                               c.ident[:, :])
                    ins.then_inc(xT_done[par], 1)
                for par in range(2):
                    pe.wait_ge(xT_out[par], turn + 2)
                    pe.wait_ge(mid_in[par], turn + 1)
                    for m in range(4):
                        for k in range(KD):
                            ins = pe.matmul(pqk[:, par, m, :], c.wqkv[:, k, m * P:(m + 1) * P], xT[:, par, k, :],
                                            start=(k == 0), stop=(k == KD - 1))
                    ins.then_inc(qk_done[par], 1)
                    pe.wait_ge(v_out[par], turn + 1)
                    for j in range(2):
                        for k in range(KD):
                            ins = pe.matmul(pv[:, par, j, :], xT[:, par, k, j * P:(j + 1) * P],
                                            c.wqkv[:, k, 2 * D:3 * D], start=(k == 0), stop=(k == KD - 1))
                    ins.then_inc(v_done[par], 1)

        @block.sync
        def _(sp):
            with sp.Fori(0, NB // 2) as turn:
                for par in range(2):
                    sp.wait_ge(low_out[par], turn + 1)
                    sp.dma_start(c.qk_dram[ds(turn * 2 + par, 1)].rearrange("b q (m p) t -> p (b q m) t", p=P),
                                 parts[:, par].rearrange("p q m t -> p (q m) t")).then_inc(stored[par], 16)
            for par in range(2):
                sp.wait_ge(stored[par], 16 * NB // 2 + 16)


def load_stacks(sp, c, st, part_of, base, b, heads, sem_):
    lo, hi = heads
    for g, part in enumerate(part_of):
        rows = c.qk_dram[ds(b, 1), part, base + lo * DH:base + hi * DH, :]
        sp.dma_start(st[g * DH:(g + 1) * DH, lo:hi, :], rows.rearrange("a (h d) t -> d (a h) t", d=DH))\
            .then_inc(sem_, 16)


def stage_l0_attention(nc, c):
    K = 6 * DH
    G = 4
    with ExitStack() as ctx:
        sb = lambda name, shape, dt: ctx.enter_context(nc.sbuf_tensor(name, shape, dt))
        sem = stage_semaphores(nc, ctx)
        psum = lambda name, shape, dt: ctx.enter_context(nc.psum_tensor(name, shape, dt))
        q_st = [sb(f"q_st{i}", [P, H, S], BF16) for i in range(2)]
        k_st = [sb(f"k_st{i}", [P, H, S], BF16) for i in range(2)]
        nmax = sb("nmax", [P, 2, H], F32)
        nparts = sb("nparts", [P, 2, 2, H], BF16)
        prob = sb("prob", [P, 2, 3 * G * P], F32)
        v_now = sb("v_now", [P, 2, 2, H, VA], F32)
        rsum = sb("rsum", [P, 2, H], F32)
        on = sb("on", [P, 2, D], F32)
        oT = sb("oT", [P, KD, S], F32)
        ring = [psum(f"ring{i}", [P, 3, 512], F32) for i in range(2)]
        po = psum("po", [P, 2, 512], F32)
        pnm = po[0:2 * H, 1, 384:512].bitcast(BF16)
        loaded = [sem("ld_a"), sem("ld_b")]
        names = ("s_done", "maxed", "nm_ready", "nmT", "nrow_out", "t_done", "exped", "pv_done", "o_ready", "oT_done",
                 "oT_out", "wo_done", "h_done", "own2", "v_copied")
        (s_done, maxed, nm_ready, nmT, nrow_out, t_done, exped, pv_done, o_ready, oT_done, oT_out, wo_done, h_done,
         own, v_copied) = (sem(n) for n in names)
        picks = sem("picks2")
        block = ctx.enter_context(nc.Block())

        def batches(eng, body, tail):
            body(0, 0, 0, True)
            with eng.Fori(0, NB // 2 - 1) as turn:
                body(turn * 2 + 1, 1, turn, False)
                body(turn * 2 + 2, 0, turn + 1, False)
            body(NB - 1, 1, NB // 2 - 1, False)
            tail()

        @block.sync
        def _(sp):
            def load(b, par):
                load_stacks(sp, c, q_st[par], SPLIT_Q, 0, b, (0, H), loaded[par])
                load_stacks(sp, c, k_st[par], SPLIT_K, 2 * P, b, (0, H), loaded[par])
            load(0, 0)
            load(1, 1)
            with sp.Fori(0, NB // 2 - 1) as turn:
                for par in range(2):
                    sp.wait_ge(t_done, turn * 8 + 4 * par + 4)
                    load(turn * 2 + 2 + par, par)

        @block.gpsimd
        def _(pool):
            def body(b, par, n, first):
                if not first:
                    pool.wait_ge(s_done, b * 4 - 2)
                pool.tensor_copy(v_now[:, par], c.vaug[:, ds(b * 2, 2), :, :]).then_inc(v_copied, 1)

            batches(pool, body, lambda: None)

        @block.tensor
        def _(pe):
            def scores(b, g):
                slot = ring[g % 2]
                for bank in range(3):
                    pe.matmul(slot[:, bank, :], c.identb[:, :], c.mask4[:, bank if bank < 2 else 1, :],
                              start=True, stop=False, skip_group_check=True)
                for x in range(G):
                    h = G * g + x
                    q, k = stacks[0], stacks[1]
                    pe.matmul(slot[:, 0, x * P:(x + 1) * P], q[0:K, h, 0:P], k[0:K, h, 0:P], start=False, stop=True,
                              skip_group_check=True)
                    ins = pe.matmul(slot[:, 1 + x // 2, (x % 2) * S:(x % 2 + 1) * S], q[0:K, h, P:S], k[0:K, h, :],
                                    start=False, stop=True, skip_group_check=True)
                ins.then_inc(s_done, 1)

            def turned(b, g):
                pe.wait_ge(nrow_out, b * 4 + g + 1)
                slot = ring[g % 2]
                q, k = stacks
                for bank in range(3):
                    pe.matmul(slot[:, bank, :], c.identb[:, :], c.mask4[:, 2 if bank < 2 else 3, :],
                              start=True, stop=False, skip_group_check=True)
                for x in range(G):
                    h = G * g + x
                    both, own_ = slot[:, x // 2, (x % 2) * S:(x % 2 + 1) * S], slot[:, 2, x * P:(x + 1) * P]
                    pe.matmul(both, k[:, h, 0:P], q[:, h, :], start=False, stop=True, skip_group_check=True)
                    ins = pe.matmul(own_, k[:, h, P:S], q[:, h, P:S], start=False, stop=True, skip_group_check=True)
                ins.then_inc(t_done, 1)

            def values(b, g, par):
                pt, v = prob[:, g % 2, :], v_now[:, par]
                if g == 0:
                    pe.wait_ge(v_copied, b + 1)
                for x in range(G):
                    h = G * g + x
                    o = slice(h * VA, (h + 1) * VA)
                    pe.matmul(po[:, 0, o], pt[:, x * S:x * S + P], v[:, 0, h, :], start=True,
                              stop=True, skip_group_check=True)
                    pe.matmul(po[:, 1, o], pt[:, x * S + P:(x + 1) * S], v[:, 0, h, :], start=True,
                              stop=False, skip_group_check=True)
                    ins = pe.matmul(po[:, 1, o], pt[:, 2 * 512 + x * P:2 * 512 + (x + 1) * P],
                                    v[:, 1, h, :], start=False, stop=True, skip_group_check=True)
                ins.then_inc(pv_done, 1)

            def out_turn(b):
                pe.wait_ge(o_ready, b + 1)
                slot = ring[0]
                for j in range(2):
                    for k in range(KD):
                        ins = pe.transpose(slot[:, 0, k * S + j * P:k * S + (j + 1) * P],
                                           on[:, j, k * P:(k + 1) * P], c.ident[:, :])
                ins.then_inc(oT_done, 1)

            def out_project(b):
                pe.wait_ge(oT_out, b + 1)
                slot = ring[1]
                for j in range(2):
                    for k in range(KD):
                        ins = pe.matmul(slot[:, 0, j * D:(j + 1) * D], oT[:, k, j * P:(j + 1) * P], c.wo0[:, k, :],
                                        start=(k == 0), stop=(k == KD - 1), skip_group_check=True)
                ins.then_inc(wo_done, 1)

            stacks = [None, None]
            pe.wait_ge(picks, 4)

            def body(b, par, n, first):
                stacks[:] = [q_st[par], k_st[par]]
                pe.wait_ge(loaded[par], 12 * 16 * (n + 1))
                if not first:
                    pe.wait_ge(exped, b * 4 - 1)
                scores(b, 0)
                if not first:
                    pe.wait_ge(exped, b * 4)
                    values(b - 1, 3, 1 - par)
                scores(b, 1)
                pe.wait_ge(maxed, b * 4 + 1)
                scores(b, 2)
                pe.wait_ge(maxed, b * 4 + 2)
                scores(b, 3)
                if not first:
                    pe.wait_ge(maxed, b * 4 + 3)
                    out_turn(b - 1)
                pe.wait_ge(nm_ready, b + 1)
                for j in range(2):
                    ins = pe.transpose(pnm[:, j * P:(j + 1) * P], nparts[:, j].rearrange("p a h -> p (a h)"),
                                       c.identb[:, :])
                ins.then_inc(nmT, 1)
                if not first:
                    pe.wait_ge(maxed, b * 4 + 4)
                    out_project(b - 1)
                    pe.wait_ge(oT_out, b)
                turned(b, 0)
                if first:
                    pe.wait_ge(maxed, 4)
                else:
                    pe.wait_ge(h_done, b)
                turned(b, 1)
                for g in range(3):
                    pe.wait_ge(exped, b * 4 + g + 1)
                    if g == 0 and not first:
                        pe.wait_ge(o_ready, b)
                    if g + 2 < 4 and g < 2:
                        turned(b, g + 2)
                    values(b, g, par)

            def tail():
                b = NB - 1
                pe.wait_ge(exped, b * 4 + 4)
                values(b, 3, 1)
                out_turn(b)
                out_project(b)

            batches(pe, body, tail)

        @block.scalar
        def _(act):
            def body(b, par, n, first):
                if not first:
                    act.wait_ge(oT_done, b)
                    act.activation(oT[:, :, :], ring[0][:, 0, :].rearrange("p (k t) -> p k t", k=KD), ACT.Copy)\
                        .then_inc(oT_out, 1)
                act.wait_ge(nmT, b + 1)
                if not first:
                    act.wait_ge(t_done, b * 4)
                for g in range(4):
                    act.activation(q_st[par][K:P, G * g:G * g + G, :],
                                   pnm[:, :].unsqueeze(1).broadcast_to([2 * H, G, S]), ACT.Copy)\
                        .then_inc(nrow_out, 1)
                for g in range(4):
                    act.wait_ge(t_done, b * 4 + g + 1)
                    if not first:
                        act.wait_ge(pv_done, b * 4 + g - 1)
                    elif g >= 2:
                        act.wait_ge(pv_done, g - 1)
                    act.activation(prob[:, g % 2, :], ring[g % 2][:, :, :].rearrange("p a n -> p (a n)"), ACT.Exp,
                                   scale=DH ** -0.5).then_inc(exped, 1)

            def tail():
                act.wait_ge(oT_done, NB)
                act.activation(oT[:, :, :], ring[0][:, 0, :].rearrange("p (k t) -> p k t", k=KD), ACT.Copy)\
                    .then_inc(oT_out, 1)

            batches(act, body, tail)

        @block.vector
        def _(dve):
            for par in range(2):
                for j in range(2):
                    dve.tensor_copy(k_st[par][K:P, :, j * P:(j + 1) * P], c.sel[0:2 * H, :, :]).then_inc(picks, 1)

            def outputs(b):
                dve.wait_ge(pv_done, b * 4 + 4)
                o = po[:, :, 0:H * VA].rearrange("p j (h v) -> p j h v", v=VA)
                dve.reciprocal(rsum[:, :, :], o[:, :, :, DH]).then_inc(own, 1)
                dve.wait_ge(own, b * 2 + 2)
                for j in range(2):
                    ins = dve.tensor_tensor(on[:, j, :].rearrange("p (h d) -> p h d", h=H), o[:, j, :, 0:DH],
                                            rsum[:, j, :].unsqueeze(2).broadcast_to([P, H, DH]), ALU.mult)
                ins.then_inc(o_ready, 1)

            def residual(b):
                dve.wait_ge(wo_done, b + 1)
                for j in range(2):
                    ins = dve.tensor_tensor(c.h[:, ds(b * 2 + j, 1), :], c.h[:, ds(b * 2 + j, 1), :],
                                            ring[1][:, 0, j * D:(j + 1) * D].unsqueeze(1), ALU.add)
                ins.then_inc(h_done, 1)
                dve.wait_ge(h_done, b + 1)
                for j in range(2):
                    dve.bn_stats(c.stats[:, ds(b * 2 + j, 1), :], c.h[:, ds(b * 2 + j, 1), :])

            def body(b, par, n, first):
                for g in range(4):
                    dve.wait_ge(s_done, b * 4 + g + 1)
                    hs = slice(G * g, G * g + G)
                    dve.tensor_reduce(nmax[:, 0, hs], ring[g % 2][:, 0, :].rearrange("p (h k) -> p h k", h=G), AX.X,
                                      ALU.max, negate=True)
                    dve.tensor_reduce(nmax[:, 1, hs],
                                      ring[g % 2][:, 1:3, :].rearrange("p a (h k) -> p (a h) k", h=2), AX.X,
                                      ALU.max, negate=True).then_inc(maxed, 1)
                    if g == 0 and not first:
                        outputs(b - 1)
                dve.wait_ge(maxed, b * 4 + 4)
                if not first:
                    dve.wait_ge(nmT, b)
                dve.tensor_copy(nparts[:, :, 0, :], nmax[:, :, :]).then_inc(own, 1)
                dve.wait_ge(own, b * 2 + 1)
                dve.tensor_tensor(nparts[:, :, 1, :], nmax[:, :, :], nparts[:, :, 0, :], ALU.subtract)\
                    .then_inc(nm_ready, 1)
                if not first:
                    residual(b - 1)

            def tail():
                outputs(NB - 1)
                residual(NB - 1)

            batches(dve, body, tail)


def stage_l0_ffn(nc, c):
    W = 512
    TW = W // P
    STEPS = NB * S // W
    M = M_UNITS
    with ExitStack() as ctx:
        sb = lambda name, shape, dt: ctx.enter_context(nc.sbuf_tensor(name, shape, dt))
        sem = stage_semaphores(nc, ctx)
        pair = lambda name: [sem(name + "_a"), sem(name + "_b")]
        psum = lambda name, shape, dt: ctx.enter_context(nc.psum_tensor(name, shape, dt))
        xn = sb("xn3", [P, 2, TW, D], F32)
        xT = sb("xT3", [P, 2, KD, W], F32)
        s_in = sb("s_in", [M, 2, W], F32)
        s_rest = sb("s_rest", [M, W], F32)
        s_mid = sb("s_mid", [M, W], BF16)
        s_two = sb("s_two", [2 * M, 2, W], BF16)
        s_low = sb("s_low", [M, 2, W], BF16)
        spreadb = sb("spreadb", [2 * M, NBLK, P], BF16)
        unit = sb("unit", [P, 2, W], F32)
        g_out = sb("g_out", [M + 1, 2, W], F32)
        pT = psum("pT3", [P, KD, W], F32)
        ps = psum("ps3", [M, W], F32)
        pb = [psum(f"pb3{i}", [P, W], F32) for i in range(2)]
        pg = psum("pg3", [M, W], F32)
        po = psum("po3", [P, TW, D], F32)
        own, sqa, sqd, row_set, spread_set, split = (
            sem(n) for n in ("own3", "sqa3", "sqd3", "row_set", "spread_set", "split3"))
        x_ready, xT_done, xT_out, s_done, s_out, s_parts, g_ready, o_done, o_added = (
            sem(n) for n in ("x_ready3", "xT_done3", "xT_out3", "s_done3", "s_out3", "s_parts3", "g_ready3",
                             "o_done3", "o_added3"))
        spread, unit_out, summed = pair("spread3"), pair("unit_out3"), pair("summed3")
        block = ctx.enter_context(nc.Block())

        def steps(eng, body):
            body(0, 0, True)
            with eng.Fori(0, STEPS // 2 - 1) as turn:
                body(turn * 2 + 1, 1, True)
                body(turn * 2 + 2, 0, True)
            body(STEPS - 1, 1, False)

        @block.gpsimd
        def _(pool):
            pool.memset(g_out[M:M + 1, :, :], 1.0).then_inc(row_set, 1)

        @block.vector
        def _(dve):
            link = Link(dve, own)
            rstd_vector(dve, link, c, 1e-5, sqa, sqd, 1)

            def normalise(i, par):
                need(dve, xT_done, i - 1)
                for x in range(TW):
                    t = i * TW + x
                    ins = dve.tensor_scalar(xn[:, par, x, :], c.h[:, ds(t, 1), :], c.mean[:, ds(t, 1)],
                                            c.rstd[:, ds(t, 1)], ALU.subtract, ALU.mult)
                ins.then_inc(x_ready, 1)

            def parts(i, par):
                dve.wait_ge(s_out, i + 1)
                need(dve, spread[1], (i - 1) * 4)
                dve.tensor_copy(s_two[0:M, par, :], s_in[:, par, :]).then_inc(split, 1)
                dve.wait_ge(split, i * 3 + 1)
                need(dve, s_parts, i)
                dve.tensor_tensor(s_rest[:, :], s_in[:, par, :], s_two[0:M, par, :], ALU.subtract).then_inc(split, 1)
                dve.wait_ge(split, i * 3 + 2)
                dve.tensor_copy(s_mid[:, :], s_rest[:, :]).then_inc(split, 1)
                dve.wait_ge(split, i * 3 + 3)
                dve.tensor_copy(s_two[M:2 * M, par, :], s_mid[:, :])
                dve.tensor_tensor(s_low[:, par, :], s_rest[:, :], s_mid[:, :], ALU.subtract).then_inc(s_parts, 1)

            def residual(i):
                dve.wait_ge(o_done, i + 2)
                t = i * TW
                dve.tensor_tensor(c.h[:, ds(t, TW), :], c.h[:, ds(t, TW), :], po[:, :, :], ALU.add)\
                    .then_inc(o_added, 1)
                dve.wait_ge(o_added, i + 2)
                for x in range(TW):
                    dve.bn_stats(c.stats[:, ds(t + x, 1), :], c.h[:, ds(t + x, 1), :])

            def body(i, par, more):
                if more:
                    normalise(i + 1, 1 - par)
                if not isinstance(i, int) or i > 0:
                    residual(i - 1)
                if more:
                    parts(i + 1, 1 - par)

            normalise(0, 0)
            for half in range(2):
                dve.tensor_copy(spreadb[half * M:(half + 1) * M, :, :], c.spread[:, :, :]).then_inc(spread_set, 1)
            for j in range(NBLK):
                dve.tensor_scalar(c.w2m[:, j, :], c.w2m[:, j, :], c.w2col[:, j:j + 1], None, ALU.mult)\
                    .then_inc(spread_set, 1)
            parts(0, 0)
            steps(dve, body)
            residual(STEPS - 1)

        @block.scalar
        def _(act):
            root_scalar(act, c, sqa, sqd, 1)

            def x_out(i, par):
                act.wait_ge(xT_done, i + 1)
                need(act, s_done, i - 1)
                act.activation(xT[:, par], pT[:, :, :], ACT.Copy).then_inc(xT_out, 1)

            def inputs_out(i, par):
                act.wait_ge(s_done, i + 1)
                need(act, s_parts, i - 1)
                act.activation(s_in[:, par], ps[:, :], ACT.Identity, bias=c.bin[:, :]).then_inc(s_out, 1)

            def body(i, par, more):
                for j in range(NBLK):
                    u, count = j % 2, i * 4 + j // 2
                    act.wait_ge(spread[u], count + 1)
                    need(act, summed[u], count)
                    act.activation(unit[:, u], pb[u][:, :], ACT.Relu, bias=c.b1col[:, j:j + 1],
                                   scale=c.w1col[:, j:j + 1]).then_inc(unit_out[u], 1)
                    if more and j == 2:
                        x_out(i + 1, 1 - par)
                    if more and j == 5:
                        inputs_out(i + 1, 1 - par)
                act.wait_ge(summed[1], i * 4 + 4)
                need(act, o_done, i)
                act.activation(g_out[0:M, par], pg[:, :], ACT.Identity, bias=c.b2u[:, :]).then_inc(g_ready, 1)

            x_out(0, 0)
            inputs_out(0, 0)
            steps(act, body)

        @block.tensor
        def _(pe):
            def turn_x(i, par):
                pe.wait_ge(x_ready, i + 1)
                need(pe, xT_out, i)
                for x in range(TW):
                    for k in range(KD):
                        ins = pe.transpose(pT[:, k, x * P:(x + 1) * P], xn[:, par, x, k * P:(k + 1) * P],
                                           c.ident[:, :])
                ins.then_inc(xT_done, 1)

            def inputs(i, par):
                pe.wait_ge(xT_out, i + 1)
                need(pe, s_out, i)
                for k in range(KD):
                    ins = pe.matmul(ps[:, :], c.win[:, k, :], xT[:, par, k, :], start=(k == 0), stop=(k == KD - 1))
                ins.then_inc(s_done, 1)

            def outputs(i, par):
                pe.wait_ge(g_ready, i + 1)
                pe.wait_ge(o_added, i + 1)
                for x in range(TW):
                    ins = pe.matmul(po[:, x, :], g_out[:, par, x * P:(x + 1) * P], c.wout[:, :], start=True,
                                    stop=True)
                ins.then_inc(o_done, 1)

            def body(i, par, more):
                pe.wait_ge(s_parts, i + 1)
                for j in range(NBLK + 1):
                    if j < NBLK:
                        u, count = j % 2, i * 4 + j // 2
                        need(pe, unit_out[u], count)
                        pe.matmul(pb[u][:, :], spreadb[:, j, :], s_two[:, par, :], start=True, stop=False)
                        pe.matmul(pb[u][:, :], spreadb[0:M, j, :], s_low[:, par, :], start=False, stop=True)\
                            .then_inc(spread[u], 1)
                    if j > 0:
                        u, count = (j - 1) % 2, i * 4 + (j - 1) // 2
                        pe.wait_ge(unit_out[u], count + 1)
                        if j == 1:
                            need(pe, g_ready, i)
                        pe.matmul(pg[:, :], c.w2m[:, j - 1, :], unit[:, u], start=(j == 1), stop=(j == NBLK))\
                            .then_inc(summed[u], 1)
                    if j == 1 and (not isinstance(i, int) or i > 0):
                        outputs(i - 1, 1 - par)
                    if j == 2 and more:
                        turn_x(i + 1, 1 - par)
                    if j == 5 and more:
                        inputs(i + 1, 1 - par)

            start_at(pe, 1, (o_done, o_added))
            pe.wait_ge(row_set, 1)
            turn_x(0, 0)
            inputs(0, 0)
            pe.wait_ge(spread_set, 2 + NBLK)
            steps(pe, body)
            outputs(STEPS - 1, 1)


def scale_of(dve, link, scale, inverse, tmp):
    link(dve.tensor_scalar(scale, scale, 1.0 / QMAX, None, ALU.mult))
    link(dve.tensor_scalar(tmp, scale, 0.0, None, ALU.is_equal))
    link(dve.tensor_tensor(scale, scale, tmp, ALU.add))
    link(dve.reciprocal(inverse, scale))


def stage_l1_project(nc, c):
    with ExitStack() as ctx:
        sb = lambda name, shape, dt: ctx.enter_context(nc.sbuf_tensor(name, shape, dt))
        sem = stage_semaphores(nc, ctx)
        pair = lambda name: [sem(name + "_a"), sem(name + "_b")]
        psum = lambda name, shape, dt: ctx.enter_context(nc.psum_tensor(name, shape, dt))
        xl = sb("xl", [P, 2, 4, D], F32)
        xmax = sb("xmax", [P, 8], F32)
        xm, xs, xinv, xtmp = (sb(n, [P, 1], F32) for n in ("xm", "xs", "xinv", "xtmp"))
        rinv = sb("rinv", [P, NT], F32)
        qks = sb("qks", [P, 4], F32)
        wvs = sb("wvs", [P, D], F32)
        xi = sb("xi", [P, 2, 2, D], I16)
        xb = sb("xb", [P, 2, 2, D], BF16)
        xT = sb("xT5", [P, 2, KD, S], BF16)
        vt = sb("vt", [P, 2, 2, D], F32)
        bmax = sb("bmax", [P, NB, 4 * NBLK], F32)
        vmax = sb("vmax", [P, NB], F32)
        m1 = sb("m1", [P, 4 * NBLK], F32)
        qm = sb("qm", [P, 2 * NBLK + 1], F32)
        qinv, qtmp = sb("qinv", [P, 2 * NBLK + 1], F32), sb("qtmp", [P, 2 * NBLK + 1], F32)
        pT = [psum(f"pT5{i}", [P, KD, S], BF16) for i in range(2)]
        pqk = psum("pqk5", [P, 2, 4, S], F32)
        pv = psum("pv5", [P, 2, 2, D], F32)
        own, sqa, sqd, asked, reduced = (sem(n) for n in ("own5", "sqa5", "sqd5", "asked5", "reduced5"))
        own_loop = sem("own5l")
        xi_ready, xb_ready, xT_done, xT_out, qk_done, v_done, qk_out, v_out, q_maxed = (
            pair(n) for n in ("xi_ready", "xb_ready", "xT_done5", "xT_out5", "qk_done5", "v_done5", "qk_out5",
                              "v_out5", "q_maxed"))
        block = ctx.enter_context(nc.Block())

        @block.vector
        def _(dve):
            link = Link(dve, own)
            rstd_vector(dve, link, c, 1e-5, sqa, sqd, 1)
            llink = Link(dve, own_loop)
            with dve.Fori(0, 4) as turn:
                llink.loop(turn, 2)
                for par in range(2):
                    g = turn * 2 + par
                    for x in range(4):
                        t = g * 4 + x
                        ins = dve.tensor_scalar(xl[:, par, x, :], c.h[:, ds(t, 1), :], c.mean[:, ds(t, 1)],
                                                c.rstd[:, ds(t, 1)], ALU.subtract, ALU.mult)
                    llink(ins)
                    dve.tensor_reduce(xmax[:, ds(g, 1)], xl[:, par].rearrange("p x d -> p (x d)"), AX.X, ALU.max,
                                      apply_absolute_value=True)
                llink.end(4)
            link(dve.memset(qtmp[:, :], 0.0))
            link(dve.tensor_reduce(xm[:, :], xmax[:, :], AX.X, ALU.max))
            dve.sem_inc(asked, 1)
            dve.wait_ge(reduced, 1)
            scale_of(dve, link, xs[:, :], xinv[:, :], xtmp[:, :])
            link(dve.tensor_scalar(rinv[:, :], c.rstd[:, :], xinv[:, :], None, ALU.mult))
            link(dve.tensor_scalar(qks[:, :], c.wscale[:, 0:4], xs[:, :], None, ALU.mult))
            link(dve.tensor_scalar(wvs[:, :], c.wvo[:, 0, :], xs[:, :], None, ALU.mult))

            def quantise(par, turn):
                dve.wait_ge(xb_ready[par], turn + 1)
                for j in range(2):
                    t = (turn * 2 + par) * 2 + j
                    ins = dve.tensor_scalar(xi[:, par, j, :], c.h[:, ds(t, 1), :], c.mean[:, ds(t, 1)],
                                            rinv[:, ds(t, 1)], ALU.subtract, ALU.mult)
                ins.then_inc(xi_ready[par], 1)

            def results(par, turn):
                b = turn * 2 + par
                dve.wait_ge(v_done[par], turn + 1)
                dve.tensor_tensor(vt[:, par], pv[:, par], wvs[:, :].unsqueeze(1).broadcast_to([P, 2, D]), ALU.mult)\
                    .then_inc(v_out[par], 1)
                dve.wait_ge(v_out[par], turn * 2 + 3)
                dve.tensor_tensor(c.v32[:, ds(b * 2, 2), :], vt[:, par],
                                  c.bv[:, :].unsqueeze(1).broadcast_to([P, 2, D]), ALU.add).then_inc(v_out[par], 1)
                dve.wait_ge(qk_out[par], turn * 4 + 8)
                dve.tensor_reduce(bmax[:, ds(b, 1), :],
                                  c.qk32[:, :, ds(b * S, S)].rearrange("p m (k t) -> p m k t", t=32), AX.X, ALU.max,
                                  apply_absolute_value=True)
                dve.wait_ge(v_out[par], turn * 2 + 4)
                dve.tensor_reduce(vmax[:, ds(b, 1)], c.v32[:, ds(b * 2, 2), :].rearrange("p j d -> p (j d)"), AX.X,
                                  ALU.max, apply_absolute_value=True)

            ahead(dve, quantise, results, NB // 2)
            link(dve.memset(qtmp[:, :], 0.0))
            link(dve.tensor_reduce(m1[:, :], bmax[:, :, :].rearrange("p b k -> p k b"), AX.X, ALU.max))
            link(dve.tensor_tensor(qm[:, 0:NBLK], m1[:, 0:NBLK], m1[:, NBLK:2 * NBLK], ALU.max))
            link(dve.tensor_tensor(qm[:, NBLK:2 * NBLK], m1[:, 2 * NBLK:3 * NBLK], m1[:, 3 * NBLK:], ALU.max))
            link(dve.tensor_reduce(qm[:, 2 * NBLK:], vmax[:, :], AX.X, ALU.max))
            dve.sem_inc(asked, 1)
            dve.wait_ge(reduced, 2)
            scale_of(dve, link, c.qscale[:, :], qinv[:, :], qtmp[:, :])
            for out, src in ((c.qs_row, c.qscale), (c.qi_row, qinv)):
                link(dve.tensor_copy(out[:, :, :].rearrange("p a (k t) -> p (a k) t", t=32),
                                     src[:, 0:2 * NBLK].unsqueeze(2).broadcast_to([P, 2 * NBLK, 32])))
            link(dve.tensor_copy(c.vinv[:, :], qinv[:, 2 * NBLK:]))

        @block.gpsimd
        def _(pool):
            pool.wait_ge(asked, 1)
            pool.partition_all_reduce(xs[:, :], xm[:, :], P, RMAX).then_inc(reduced, 1)
            pool.wait_ge(asked, 2)
            pool.partition_all_reduce(c.qscale[:, :], qm[:, :], P, RMAX).then_inc(reduced, 1)

        @block.scalar
        def _(act):
            root_scalar(act, c, sqa, sqd, 1)
            with act.Fori(0, NB // 2) as turn:
                for par in range(2):
                    act.wait_ge(xi_ready[par], turn + 1)
                    act.wait_ge(xT_done[par], turn + 1)
                    act.activation(xb[:, par], xi[:, par], ACT.Copy).then_inc(xb_ready[par], 1)
                for par in range(2):
                    act.wait_ge(xT_done[par], turn + 2)
                    act.activation(xT[:, par], pT[par][:, :, :], ACT.Copy).then_inc(xT_out[par], 1)
                for par in range(2):
                    b = turn * 2 + par
                    act.wait_ge(qk_done[par], turn + 1)
                    for m in range(4):
                        act.activation(c.qk32[:, m, ds(b * S, S)], pqk[:, par, m, :], ACT.Identity,
                                       bias=c.bqk[:, m:m + 1], scale=qks[:, m:m + 1]).then_inc(qk_out[par], 1)

        @block.tensor
        def _(pe):
            start_at(pe, 1, xT_done, xT_out, xb_ready)
            start_at(pe, 4, qk_out)
            start_at(pe, 2, v_out)
            with pe.Fori(0, NB // 2) as turn:
                for par in range(2):
                    pe.wait_ge(xb_ready[par], turn + 2)
                    pe.wait_ge(xT_out[par], turn + 1)
                    for j in range(2):
                        for k in range(KD):
                            ins = pe.transpose(pT[par][:, k, j * P:(j + 1) * P], xb[:, par, j, k * P:(k + 1) * P],
                                               c.identb[:, :])
                    ins.then_inc(xT_done[par], 1)
                for par in range(2):
                    pe.wait_ge(xT_out[par], turn + 2)
                    pe.wait_ge(qk_out[par], turn * 4 + 4)
                    for m in range(4):
                        for k in range(KD):
                            ins = pe.matmul(pqk[:, par, m, :], c.wT[:, m // 2, k, (m % 2) * P:(m % 2 + 1) * P],
                                            xT[:, par, k, :], start=(k == 0), stop=(k == KD - 1))
                    ins.then_inc(qk_done[par], 1)
                    pe.wait_ge(v_out[par], turn * 2 + 2)
                    for j in range(2):
                        for k in range(KD):
                            ins = pe.matmul(pv[:, par, j, :], xT[:, par, k, j * P:(j + 1) * P], c.wT[:, 2, k, :],
                                            start=(k == 0), stop=(k == KD - 1))
                    ins.then_inc(v_done[par], 1)


def stage_l1_quantise(nc, c):
    WAYS = 4
    with ExitStack() as ctx:
        sb = lambda name, shape, dt: ctx.enter_context(nc.sbuf_tensor(name, shape, dt))
        sem = stage_semaphores(nc, ctx)
        ways = lambda name: [sem(f"{name}{x}") for x in range(WAYS)]
        qi = sb("qi", [P, WAYS, 4, S], I16)
        parts = sb("parts6", [P, WAYS, 3, 4, S], BF16)
        vi = sb("vi", [P, WAYS, 2, D], I16)
        qi_ready, qb_ready, hi_out, mid_in, mid_out, low_out, stored, vi_ready, nv_out = (
            ways(n) for n in ("qi_ready", "qb_ready", "hi_out6", "mid_in6", "mid_out6", "low_out6", "stored6",
                              "vi_ready", "nv_out"))
        at_work = sem("at_work6")
        block = ctx.enter_context(nc.Block())
        by_op = lambda t: t.rearrange("p (a m) t -> p a m t", a=2)
        row = lambda t: t[:, :, :].unsqueeze(2).broadcast_to([P, 2, 2, S])
        batch = lambda way, turn: turn * WAYS + way
        values = lambda way, turn: c.qk32[:, :, ds(batch(way, turn) * S, S)]

        @block.vector
        def _(dve):
            def quantise(way, turn):
                dve.wait_ge(qb_ready[way], turn + 1)
                dve.tensor_tensor(by_op(qi[:, way]), by_op(values(way, turn)), row(c.qi_row), ALU.mult)\
                    .then_inc(qi_ready[way], 1)
                dve.wait_ge(nv_out[way], turn + 1)
                dve.tensor_scalar(vi[:, way], c.v32[:, ds(batch(way, turn) * 2, 2), :], c.vinv[:, :], None, ALU.mult)\
                    .then_inc(vi_ready[way], 1)
                dve.wait_ge(qi_ready[way], turn + 1)
                dve.tensor_tensor(by_op(values(way, turn)), by_op(qi[:, way]), row(c.qs_row), ALU.mult)\
                    .then_inc(qb_ready[way], 1)

            def split(way, turn):
                dve.wait_ge(mid_out[way], turn + 1)
                dve.tensor_tensor(parts[:, way, 2], values(way, turn), parts[:, way, 1], ALU.subtract)\
                    .then_inc(low_out[way], 1)

            ahead(dve, quantise, split, NB // WAYS, WAYS)

        @block.gpsimd
        def _(pool):
            with pool.Fori(0, NB // WAYS) as turn:
                for way in range(WAYS):
                    pool.wait_ge(hi_out[way], turn + 1)
                    pool.tensor_tensor(values(way, turn), values(way, turn), parts[:, way, 0], ALU.subtract)\
                        .then_inc(mid_in[way], 1)

        @block.scalar
        def _(act):
            start_at(act, 1, nv_out, qb_ready)
            start_at(act, 16, stored)
            with act.Fori(0, NB // WAYS) as turn:
                for way in range(WAYS):
                    act.wait_ge(qb_ready[way], turn + 2)
                    act.wait_ge(stored[way], turn * 16 + 16)
                    act.sem_inc(at_work, 1)
                    act.activation(parts[:, way, 0], values(way, turn), ACT.Copy).then_inc(hi_out[way], 1)
                    act.wait_ge(vi_ready[way], turn + 1)
                    act.activation(c.nv[:, ds(batch(way, turn) * 2, 2), :], vi[:, way], ACT.Copy)\
                        .then_inc(nv_out[way], 1)
                for way in range(WAYS):
                    act.wait_ge(mid_in[way], turn + 1)
                    act.sem_inc(at_work, 1)
                    act.activation(parts[:, way, 1], values(way, turn), ACT.Copy).then_inc(mid_out[way], 1)

        @block.sync
        def _(sp):
            with sp.Fori(0, NB // WAYS) as turn:
                for way in range(WAYS):
                    sp.wait_ge(low_out[way], turn + 1)
                    sp.dma_start(c.qk_dram[ds(batch(way, turn), 1)].rearrange("b q (m p) t -> p (b q m) t", p=P),
                                 parts[:, way].rearrange("p q m t -> p (q m) t")).then_inc(stored[way], 16)
            for way in range(WAYS):
                sp.wait_ge(stored[way], 16 * NB // WAYS + 16)


FIX = 2.0 ** 26
GROUP = 2.5
PC = 8


def stage_l1_exponentials(nc, c):
    ms, cs = pla_table()
    a = [GROUP * m for m in ms[9:]]
    b_ = [3 * GROUP * m + k for m, k in zip(ms[9:], cs[9:])]
    unit = a[1] - a[0]
    edge1, edge2 = -4 + 1 / 3, -4 + 2 / 3
    with ExitStack() as ctx:
        sb = lambda name, shape, dt: ctx.enter_context(nc.sbuf_tensor(name, shape, dt))
        sem = stage_semaphores(nc, ctx)
        psum = lambda name, shape, dt: ctx.enter_context(nc.psum_tensor(name, shape, dt))
        q_st = [sb(f"q_st7{i}", [6 * DH, H, S], BF16) for i in range(2)]
        k_st = [sb(f"k_st7{i}", [6 * DH, H, S], BF16) for i in range(2)]
        nmax = sb("nmax7", [P, 2, H], F32)
        nrest = sb("nrest7", [P, 2, H], F32)
        nparts = sb("nparts7", [P, 2, P], BF16)
        nrow = sb("nrow7", [3 * H, 2, S], BF16)
        W = 2 * 512
        fixed = sb("fixed", [P, 2, W], I32)
        group = sb("group", [P, 2, W], I16)
        local = sb("local", [P, 2, W], F32)
        base = sb("base", [P, 2, W], F32)
        step2 = sb("step2", [P, 2, W], F32)
        acc = sb("acc", [P, 2, W], F32)
        power = sb("power", [P, 4, W], F32)
        ex = sb("ex", [P, 4, W], F32)
        cols = sb("cols", [P, 4], F32)
        onesel = sb("onesel", [P, PC, PC], F32)
        srow = sb("srow", [PC, 2, 512], F32)
        pS = psum("pS7", [P, 2, 512], F32)
        pT = [psum(f"pT7{i}", [P, 2, 512], F32) for i in range(2)]
        psums = psum("psums", [PC, 512], F32)
        pnm = psum("pnm7", [P, S], BF16)
        ld = [[sem(f"ld7{p}{x}") for x in range(2)] for p in range(2)]
        names = ("s_done7", "maxed7", "nm_ready7", "nmT7", "nrow_out7", "t_done7", "fixed_out", "group_out",
                 "power_out", "local_out", "base_out", "step2_out", "acc_out", "ex_out", "summed7", "own7", "sums_out",
                 "consts7", "pool7")
        (s_done, maxed, nm_ready, nmT, nrow_out, t_done, fixed_out, group_out, power_out, local_out, base_out,
         step2_out, acc_out, ex_out, summed, own, sums_out, consts, pool_own) = (sem(n) for n in names)
        stacks_free, upper_out, middle_out, edge_out = (
            sem(n) for n in ("stacks_free", "upper_out", "middle_out", "edge_out"))
        ex_stored = [sem(f"ex_stored{x}") for x in range(4)]
        sums_stored = [sem("sums_stored_a"), sem("sums_stored_b")]
        block = ctx.enter_context(nc.Block())

        def batches(body, eng):
            body(0, 0, 0)
            with eng.Fori(0, NB // 2 - 1) as turn:
                body(turn * 2 + 1, 1, turn)
                body(turn * 2 + 2, 0, turn + 1)
            body(NB - 1, 1, NB // 2 - 1)

        final = lambda b: isinstance(b, int) and b == NB - 1
        first = lambda b: isinstance(b, int) and b == 0
        scores_in = lambda b, g: pT[0] if first(b) and g % 2 else pS

        @block.sync
        def _(sp):
            def load(b, par, half, rows):
                cut = slice(half * 8, half * 8 + 8)
                for r in rows:
                    st, part, base_ = (q_st, SPLIT_Q[r], 0) if r < 6 else (k_st, SPLIT_K[r - 6], 2 * P)
                    src = c.qk_dram[ds(b, 1), part, base_ + half * P:base_ + half * P + P, :]
                    sp.dma_start(st[par][(r % 6) * DH:(r % 6 + 1) * DH, cut, :],
                                 src.rearrange("a (h d) t -> d (a h) t", d=DH)).then_inc(ld[par][half], 16)

            for b, half in ((0, 0), (0, 1), (1, 0)):
                load(b, b, half, range(12))

            def body(b, par, n):
                for g in range(PC):
                    rows = range(4 * (g % 4), min(4 * (g % 4) + 4, 12))
                    if g < 4 and not final(b):
                        if g == 0 and not first(b):
                            sp.wait_ge(t_done, b * PC)
                            sp.sem_inc(stacks_free, 1)
                        load(b + 1, 1 - par, 1, rows)
                    if g >= 4 and not (isinstance(b, int) and b >= NB - 2):
                        if g == 4:
                            sp.wait_ge(t_done, b * PC + 4)
                            sp.sem_inc(stacks_free, 1)
                        load(b + 2, par, 0, rows)
                    if g >= 1 or not first(b):
                        i, k = b * PC + g, (g - 1) % 4
                        sp.wait_ge(ex_out, i)
                        sp.dma_start(c.ex_dram[ds(i - 1, 1)].rearrange("a p n -> p (a n)"), ex[:, k, :])\
                            .then_inc(ex_stored[k], 16)

            body(0, 0, 0)
            with sp.Fori(0, NB // 2 - 2) as turn:
                body(turn * 2 + 1, 1, turn)
                body(turn * 2 + 2, 0, turn + 1)
            for b in range(NB - 3, NB):
                body(b, b % 2, b // 2)
            i = NB * PC
            sp.wait_ge(ex_out, i)
            sp.dma_start(c.ex_dram[i - 1], ex[:, 3, :]).then_inc(ex_stored[3], 16)
            for k in range(4):
                sp.wait_ge(ex_stored[k], 16 * NB * PC // 4)

        @block.gpsimd
        def _(pool):
            link = Link(pool, pool_own)
            link(pool.memset(onesel[:, :, :], 0.0))
            for g in range(PC):
                ins = pool.memset(onesel[:, g, g:g + 1], 1.0)
            link(ins)
            pool.sem_inc(consts, 1)

            def body(b, par, n):
                for g in range(PC):
                    i = b * PC + g
                    k = g % 2
                    pool.wait_ge(acc_out, i + 1)
                    pool.wait_ge(power_out, i + 1)
                    need(pool, summed, i - 3)
                    if g >= 4 or not first(b):
                        pool.wait_ge(ex_stored[g % 4], (b * (PC // 4) + g // 4) * 16)
                    pool.tensor_tensor(ex[:, g % 4, :], acc[:, k, :], power[:, g % 4, :], ALU.mult)\
                        .then_inc(ex_out, 1)

            batches(body, pool)

        @block.scalar
        def _(act):
            act.wait_ge(consts, 2)

            def late(i, k):
                act.wait_ge(local_out, i + 1)
                need(act, acc_out, i - 1)
                act.activation(base[:, k, :], local[:, k, :], ACT.Relu, bias=cols[:, 0:1], scale=a[0] / unit)\
                    .then_inc(base_out, 1)
                act.activation(step2[:, k, :], local[:, k, :], ACT.Identity, bias=cols[:, 1:2],
                               scale=(a[2] - a[1]) / unit).then_inc(step2_out, 1)

            def row_out(b, par):
                act.wait_ge(nmT, b + 1)
                need(act, t_done, (b - 1) * PC)
                act.activation(nrow[:, par, :], pnm[0:3 * H, :], ACT.Copy).then_inc(nrow_out, 1)

            def body(b, par, n):
                for g in range(PC):
                    i, k = b * PC + g, g % 2
                    if g >= 1 or not first(b):
                        late(i - 1, 1 - k)
                    act.wait_ge(t_done, i + 1)
                    need(act, local_out, i - 1)
                    act.activation(fixed[:, k, :], pT[k][:, :, :].rearrange("p a n -> p (a n)"), ACT.Relu,
                                   scale=-FIX * DH ** -0.5).then_inc(fixed_out, 1)
                    if g == 4 and not first(b):
                        sums(b - 1)
                    act.wait_ge(fixed_out, i + 1)
                    act.activation(group[:, k, :], fixed[:, k, :], ACT.Relu, bias=cols[:, 2:3],
                                   scale=-1 / (GROUP * FIX)).then_inc(group_out, 1)
                    if g == PC - 1 and not final(b):
                        row_out(b + 1, 1 - par)
                    act.wait_ge(group_out, i + 1)
                    need(act, ex_out, i - 3)
                    act.activation(power[:, g % 4, :], group[:, k, :], ACT.Exp, bias=cols[:, 3:4], scale=GROUP)\
                        .then_inc(power_out, 1)

            def sums(b):
                act.wait_ge(summed, b * PC + PC)
                if isinstance(b, int):
                    k, turn = b % 2, b // 2
                else:
                    k, turn = state["par"], state["n"]
                if not isinstance(turn, int) or turn > 0:
                    act.wait_ge(sums_stored[k], turn * 16 + 16)
                act.activation(srow[:, k, :], psums[:, :], ACT.Copy).then_inc(sums_out, 1)
                act.wait_ge(sums_out, b + 1)
                act.dma_start(c.sum_dram[ds(b, 1)].rearrange("a g n -> g (a n)"), srow[:, k, :])\
                    .then_inc(sums_stored[k], 16)

            state = {}
            row_out(0, 0)
            body(0, 0, 0)
            with act.Fori(0, NB // 2 - 1) as turn:
                state.update(par=0, n=turn)
                body(turn * 2 + 1, 1, turn)
                state.update(par=1, n=turn)
                body(turn * 2 + 2, 0, turn + 1)
            body(NB - 1, 1, NB // 2 - 1)
            late(NB * PC - 1, 1)
            sums(NB - 1)
            for k in range(2):
                act.wait_ge(sums_stored[k], 16 * NB // 2 + 16)

        @block.vector
        def _(dve):
            for x, value in enumerate((4 * a[0] / unit, (b_[2] - b_[1]) / unit, 3.5 * (1 - 2.0 ** -23), -3 * GROUP)):
                dve.memset(cols[:, x:x + 1], value)
            dve.memset(nparts[:, :, :], 0.0).then_inc(own, 1)
            dve.wait_ge(own, 1)
            dve.sem_inc(consts, 1)

            def row_max(b, g):
                dve.wait_ge(s_done, b * PC + g + 1)
                dve.tensor_reduce(nmax[:, :, 2 * g:2 * g + 2], scores_in(b, g)[:, :, :].rearrange("p j (h k) -> p j h k", h=2),
                                  AX.X, ALU.max, negate=True).then_inc(maxed, 1)

            def max_parts(b):
                dve.wait_ge(maxed, b * PC + PC)
                if not first(b):
                    dve.wait_ge(nmT, b)
                dve.tensor_copy(nparts[:, :, 0:16], nmax[:, :, :]).then_inc(own, 1)
                dve.wait_ge(own, b * 3 + 2)
                dve.tensor_tensor(nrest[:, :, :], nmax[:, :, :], nparts[:, :, 0:16], ALU.subtract).then_inc(own, 1)
                dve.wait_ge(own, b * 3 + 3)
                dve.tensor_copy(nparts[:, :, 16:32], nrest[:, :, :]).then_inc(own, 1)
                dve.wait_ge(own, b * 3 + 4)
                dve.tensor_tensor(nparts[:, :, 32:48], nrest[:, :, :], nparts[:, :, 16:32], ALU.subtract)\
                    .then_inc(nm_ready, 1)

            def upper(i, k):
                dve.wait_ge(step2_out, i + 1)
                need(dve, ex_out, i - 1)
                dve.scalar_tensor_tensor(out=acc[:, k, :], in0=local[:, k, :], scalar=edge2, in1=step2[:, k, :],
                                         op0=ALU.is_ge, op1=ALU.mult).then_inc(upper_out, 1)

            def middle(i, k):
                f = acc[:, k, :]
                dve.wait_ge(upper_out, i + 1)
                dve.scalar_tensor_tensor(out=f, in0=f, scalar=(b_[1] - b_[0]) / unit, in1=local[:, k, :],
                                         op0=ALU.add, op1=ALU.add).then_inc(middle_out, 1)

            def middle_edge(i, k):
                f = acc[:, k, :]
                dve.wait_ge(middle_out, i + 1)
                dve.scalar_tensor_tensor(out=f, in0=local[:, k, :], scalar=edge1, in1=f, op0=ALU.is_ge,
                                         op1=ALU.mult).then_inc(edge_out, 1)

            def lower(i, k):
                f = acc[:, k, :]
                dve.wait_ge(edge_out, i + 1)
                dve.scalar_tensor_tensor(out=f, in0=f, scalar=(b_[0] - 4 * a[0]) / unit, in1=base[:, k, :],
                                         op0=ALU.add, op1=ALU.add).then_inc(acc_out, 1)

            def coordinate(i, k):
                need(dve, edge_out, i - 1)
                dve.wait_ge(group_out, i + 1)
                dve.scalar_tensor_tensor(out=local[:, k, :], in0=fixed[:, k, :], scalar=-1 / (GROUP * FIX),
                                         in1=group[:, k, :], op0=ALU.mult, op1=ALU.subtract)\
                    .then_inc(local_out, 1)

            for g in range(PC):
                row_max(0, g)
            max_parts(0)

            def body(b, par, n):
                for g in range(PC):
                    i, k = b * PC + g, g % 2
                    def next_max(g=g):
                        if g < PC - 1 and not final(b):
                            row_max(b + 1, g)

                    if g == PC - 1 and not final(b):
                        row_max(b + 1, g)
                        max_parts(b + 1)
                    if g == 0 and first(b):
                        coordinate(i, k)
                        next_max()
                    elif g == 0:
                        upper(i - 1, 1 - k)
                        lower(i - 2, k)
                        middle(i - 1, 1 - k)
                        coordinate(i, k)
                        next_max()
                        middle_edge(i - 1, 1 - k)
                    else:
                        upper(i - 1, 1 - k)
                        if g >= 2 or not first(b):
                            lower(i - 2, k)
                        coordinate(i, k)
                        middle(i - 1, 1 - k)
                        next_max()
                        middle_edge(i - 1, 1 - k)
            batches(body, dve)
            i = NB * PC - 1
            upper(i, 1)
            lower(i - 1, 0)
            middle(i, 1)
            middle_edge(i, 1)
            lower(i, 1)

        @block.tensor
        def _(pe):
            start_at(pe, 16, sums_stored)
            pe.wait_ge(consts, 2)

            def scores(b, par, g):
                slot = scores_in(b, g)
                need(pe, maxed, b * PC + g - (1 if first(b) else 0))
                q, k = q_st[par], k_st[par]
                for j in range(2):
                    for x in range(2):
                        ins = pe.matmul(slot[:, j, x * S:(x + 1) * S], q[:, 2 * g + x, j * P:(j + 1) * P],
                                        k[:, 2 * g + x, :], start=True, stop=True, skip_group_check=True)
                ins.then_inc(s_done, 1)

            def turned(b, par, g):
                if first(b) and g == 0:
                    pe.wait_ge(maxed, PC)
                slot, q, k = pT[g % 2], q_st[par], k_st[par]
                need(pe, fixed_out, b * PC + g - 1)
                for j in range(2):
                    for x in range(2):
                        o = slot[:, j, x * S:(x + 1) * S]
                        pe.matmul(o, c.sel[:, 2 * g + x, :], nrow[:, par, :], start=True, stop=False,
                                  skip_group_check=True)
                        ins = pe.matmul(o, k[:, 2 * g + x, j * P:(j + 1) * P], q[:, 2 * g + x, :], start=False,
                                        stop=True, skip_group_check=True)
                ins.then_inc(t_done, 1)

            def row_sums(i, g):
                pe.wait_ge(ex_out, i + 1)
                if g == 0:
                    need(pe, sums_out, state["b"])
                for j in range(2):
                    ins = pe.matmul(psums[:, :], onesel[:, g, :], ex[:, g % 4, j * 512:(j + 1) * 512],
                                    start=(g == 0 and j == 0), stop=(g == PC - 1 and j == 1), skip_group_check=True)
                ins.then_inc(summed, 1)

            def max_rows(b):
                pe.wait_ge(nm_ready, b + 1)
                for j in range(2):
                    ins = pe.transpose(pnm[:, j * P:(j + 1) * P], nparts[:, j, :],
                                       c.identb[:, :])
                ins.then_inc(nmT, 1)

            state = {}
            for g in range(PC):
                if g % 4 == 0:
                    pe.wait_ge(ld[0][g // 4], 12 * 16)
                scores(0, 0, g)
            max_rows(0)

            def body(b, par, n):
                state["b"] = b
                pe.wait_ge(nrow_out, b + 1)
                for g in range(PC):
                    i = b * PC + g
                    turned(b, par, g)
                    if not final(b):
                        if g % 4 == 0:
                            pe.wait_ge(ld[1 - par][g // 4], 12 * 16 * (n + (1 if par == 0 else 2)))
                        scores(b + 1, 1 - par, g)
                        if g == PC - 1:
                            max_rows(b + 1)
                    if g >= 4:
                        row_sums(i - 4, g - 4)
                    elif not first(b):
                        row_sums(i - 4, PC + g - 4)

            batches(body, pe)
            row_sums(NB * PC - 4, PC - 4)
            row_sums(NB * PC - 3, PC - 3)
            row_sums(NB * PC - 2, PC - 2)
            row_sums(NB * PC - 1, PC - 1)


def stage_l1_context(nc, c):
    ms, cs = pla_table()
    unit = GROUP * (ms[10] - ms[9])
    RING = 4
    with ExitStack() as ctx:
        sb = lambda name, shape, dt: ctx.enter_context(nc.sbuf_tensor(name, shape, dt))
        sem = stage_semaphores(nc, ctx)
        psum = lambda name, shape, dt: ctx.enter_context(nc.psum_tensor(name, shape, dt))
        sums = sb("sums8", [P, 512], F32)
        smax, smx = sb("smax8", [P, 1], F32), sb("smx8", [P, 1], F32)
        pscale, pinv, ptmp, cscale = (sb(n, [P, 1], F32) for n in ("pscale", "pinv", "ptmp", "cscale"))
        rest = sb("rest8", [P, 512], F32)
        parts = sb("parts8", [P, 3, 512], BF16)
        rows = sb("rows8", [3 * PC, 2, 512], BF16)
        pick = sb("pick8", [3 * PC, PC, P], BF16)
        ex = sb("ex8", [P, RING, 2, 512], F32)
        nv_now = sb("nv_now", [P, 2, 2, D], BF16)
        pi = sb("pi8", [P, 2, 2, 512], I16)
        pb = sb("pb8", [P, 2, 2, 512], BF16)
        pr = [psum(f"pr8{i}", [P, 512], F32) for i in range(2)]
        pc = [psum(f"pc8{i}", [P, 2, D], F32) for i in range(2)]
        loaded = [sem(f"ex_ld{i}") for i in range(RING)]
        sums_in, asked, reduced, own, inv_stored, picked, consts = (
            sem(n) for n in ("sums_in", "asked8", "reduced8", "own8", "inv_stored", "picked8", "consts8"))
        rows_in = [sem("rows_in_a"), sem("rows_in_b")]
        spread, rounded, cast, pv_done, c_out = (
            sem(n) for n in ("spread8", "rounded8", "cast8", "pv_done8", "c_out8"))
        v_copied = sem("v_copied8")
        block = ctx.enter_context(nc.Block())
        chunk = lambda turn, par, g: (turn * 2 + par) * PC + g

        @block.gpsimd
        def _(pool):
            link = Link(pool, picked)
            link(pool.memset(pick[:, :, :], 0.0))
            for part in range(3):
                link(pool.affine_select(out=pick[:, :, :], in_=pick[:, :, :], compare_op=ALU.not_equal, fill=1.0,
                                        base=-PC * part, channel_multiplier=1, pattern=[[-1, PC], [0, P]]))
            pool.sem_inc(consts, 1)
            pool.wait_ge(asked, 1)
            pool.partition_all_reduce(smx[:, :], smax[:, :], P, RMAX).then_inc(reduced, 1)

            def copy(b, par):
                pool.tensor_copy(nv_now[:, par], c.nv[:, ds(b * 2, 2), :]).then_inc(v_copied, 1)

            for b in range(2):
                copy(b, b)
            with pool.Fori(1, NB // 2) as turn:
                for par in range(2):
                    pool.wait_ge(spread, (turn * 2 + par - 1) * PC + 3)
                    copy(turn * 2 + par, par)

        @block.sync
        def _(sp):
            sp.dma_start(sums[:, :], c.sum_dram.rearrange("b g n -> (b g) n")).then_inc(sums_in, 16)
            for r in range(RING):
                sp.dma_start(ex[:, r].rearrange("p a n -> p (a n)"), c.ex_dram[r]).then_inc(loaded[r], 16)
            sp.wait_ge(asked, 2)
            for part in range(3):
                sp.dma_start(c.inv_dram[part].rearrange("b g n -> (b g) n"), parts[:, part, :])\
                    .then_inc(inv_stored, 16)
            sp.wait_ge(inv_stored, 48)

            def load_rows(b, par):
                for part in range(3):
                    sp.dma_start(rows[part * PC:(part + 1) * PC, par, :],
                                 c.inv_dram[part, ds(b, 1)].rearrange("a g n -> g (a n)")).then_inc(rows_in[par], 16)

            for par in range(2):
                load_rows(par, par)

            def body(turn, last_turn):
                for par in range(2):
                    for g in range(PC):
                        i = chunk(turn, par, g)
                        if last_turn and par == 1 and g >= RING:
                            continue
                        sp.wait_ge(rounded, i + 1)
                        sp.dma_start(ex[:, g % RING].rearrange("p a n -> p (a n)"),
                                     c.ex_dram[ds(i + RING, 1)].rearrange("a p n -> p (a n)"))\
                            .then_inc(loaded[g % RING], 16)
                    if not last_turn:
                        sp.wait_ge(spread, chunk(turn, par, PC - 1) + 1)
                        load_rows(turn * 2 + par + 2, par)

            with sp.Fori(0, NB // 2 - 1) as turn:
                body(turn, False)
            body(NB // 2 - 1, True)

        @block.vector
        def _(dve):
            link = Link(dve, own)
            dve.wait_ge(sums_in, 16)
            link(dve.tensor_scalar(sums[:, :], sums[:, :], 1e-9 / unit, None, ALU.add))
            link(dve.reciprocal(sums[:, :], sums[:, :]))
            link(dve.tensor_reduce(smax[:, :], sums[:, :], AX.X, ALU.max))
            dve.sem_inc(asked, 1)
            dve.wait_ge(reduced, 1)
            link(dve.tensor_scalar(pscale[:, :], smx[:, :], cs[11] / unit, None, ALU.mult))
            scale_of(dve, link, pscale[:, :], pinv[:, :], ptmp[:, :])
            link(dve.tensor_tensor(cscale[:, :], pscale[:, :], c.qscale[:, 2 * NBLK:], ALU.mult))
            link(dve.tensor_scalar(sums[:, :], sums[:, :], pinv[:, :], None, ALU.mult))
            link(dve.tensor_copy(parts[:, 0, :], sums[:, :]))
            link(dve.tensor_tensor(rest[:, :], sums[:, :], parts[:, 0, :], ALU.subtract))
            link(dve.tensor_copy(parts[:, 1, :], rest[:, :]))
            link(dve.tensor_tensor(parts[:, 2, :], rest[:, :], parts[:, 1, :], ALU.subtract))
            dve.sem_inc(asked, 1)

            def context(turn, par, b):
                dve.wait_ge(pv_done, b * PC + PC)
                ins = dve.tensor_scalar(c.ctx[:, ds(b * 2, 2), :], pc[par][:, :, :], cscale[:, :], None, ALU.mult)
                ins.then_inc(c_out, 1)
                dve.wait_ge(c_out, b + 1)
                dve.tensor_reduce(c.cmax[:, ds(b, 1)], c.ctx[:, ds(b * 2, 2), :].rearrange("p j d -> p (j d)"),
                                  AX.X, ALU.max, apply_absolute_value=True)

            def body(turn, first_turn):
                for par in range(2):
                    for g in range(PC):
                        i = chunk(turn, par, g)
                        dve.wait_ge(spread, i + 1)
                        dve.wait_ge(loaded[g % RING], (turn * 4 + par * 2 + g // RING + 1) * 16)
                        if not (first_turn and par == 0 and g < 2):
                            dve.wait_ge(cast, i - 1)
                        dve.tensor_tensor(pi[:, g % 2], ex[:, g % RING],
                                          pr[g % 2][:, :].unsqueeze(1).broadcast_to([P, 2, 512]), ALU.mult)\
                            .then_inc(rounded, 1)
                        if g == 3 and not (first_turn and par == 0):
                            context(turn, 1 - par, turn * 2 + par - 1)

            body(0, True)
            with dve.Fori(1, NB // 2) as turn:
                body(turn, False)
            context(None, 1, NB - 1)

        @block.scalar
        def _(act):
            for e in range(NE):
                act.dma_start(c.ew1[:, e], c.ins["L1_ffn_W1"][e].rearrange("(k p) f -> p k f", p=P))\
                    .then_inc(c.w1_in, 16)
            act.dma_start(c.eb1[:, :], c.ins["L1_ffn_b1"]).then_inc(c.w1_in, 16)

            def body(turn, first_turn):
                for par in range(2):
                    for g in range(PC):
                        i = chunk(turn, par, g)
                        act.wait_ge(rounded, i + 1)
                        if not (first_turn and par == 0 and g < 2):
                            act.wait_ge(pv_done, i - 1)
                        act.activation(pb[:, g % 2], pi[:, g % 2], ACT.Copy).then_inc(cast, 1)

            body(0, True)
            with act.Fori(1, NB // 2) as turn:
                body(turn, False)

        @block.tensor
        def _(pe):
            pe.wait_ge(consts, 1)

            def spread_row(turn, par, g, i, early):
                if g == 0:
                    pe.wait_ge(rows_in[par], (turn + 1) * 48)
                if not early:
                    pe.wait_ge(rounded, i - 1)
                pe.matmul(pr[g % 2][:, :], pick[:, g, :], rows[:, par, :], start=True, stop=True)\
                    .then_inc(spread, 1)

            def values(turn, par, g, i, b, first_batches):
                pe.wait_ge(cast, i + 1)
                if g == 0:
                    pe.wait_ge(v_copied, b + 1)
                    if not first_batches:
                        pe.wait_ge(c_out, b - 1)
                for x in range(2):
                    h = 2 * g + x
                    for j in range(2):
                        for k in range(2):
                            ins = pe.matmul(pc[par][:, j, h * DH:(h + 1) * DH],
                                            pb[:, g % 2, k, x * S + j * P:x * S + (j + 1) * P],
                                            nv_now[:, par, k, h * DH:(h + 1) * DH],
                                            start=(k == 0), stop=(k == 1), skip_group_check=True)
                ins.then_inc(pv_done, 1)

            def body(turn, first_turn):
                for par in range(2):
                    for g in range(PC):
                        i = chunk(turn, par, g)
                        spread_row(turn, par, g, i, first_turn and par == 0 and g < 2)
                        if g >= 2:
                            values(turn, par, g - 2, i - 2, turn * 2 + par, first_turn)
                        elif par == 1:
                            values(turn, 0, PC + g - 2, i - 2, turn * 2, first_turn)
                        elif not first_turn:
                            values(turn, 1, PC + g - 2, i - 2, turn * 2 - 1, first_turn)

            body(0, True)
            with pe.Fori(1, NB // 2) as turn:
                body(turn, False)
            for g in (PC - 2, PC - 1):
                values(None, 1, g, (NB - 1) * PC + g, NB - 1, False)


def stage_l1_output(nc, c):
    with ExitStack() as ctx:
        sb = lambda name, shape, dt: ctx.enter_context(nc.sbuf_tensor(name, shape, dt))
        sem = stage_semaphores(nc, ctx)
        pair = lambda name: [sem(name + "_a"), sem(name + "_b")]
        psum = lambda name, shape, dt: ctx.enter_context(nc.psum_tensor(name, shape, dt))
        cm, cs_, cinv, ctmp = (sb(n, [P, 1], F32) for n in ("cm9", "cs9", "cinv9", "ctmp9"))
        wos = sb("wos9", [P, D], F32)
        ci = sb("ci9", [P, 2, 2, D], I16)
        cb = sb("cb9", [P, 2, 2, D], BF16)
        cT = sb("cT9", [P, 2, KD, S], BF16)
        out = sb("out9", [P, 2, 2, D], F32)
        pT = [psum(f"pT9{i}", [P, KD, S], BF16) for i in range(2)]
        po = [psum(f"po9{i}", [P, 2, D], F32) for i in range(2)]
        asked, reduced, own = (sem(n) for n in ("asked9", "reduced9", "own9"))
        ci_ready, cb_ready, cT_done, cT_out, o_done, o_out, biased, h_done = (
            pair(n) for n in ("ci_ready", "cb_ready", "cT_done", "cT_out", "o_done9", "o_out9", "biased9", "h_done9"))
        block = ctx.enter_context(nc.Block())

        @block.gpsimd
        def _(pool):
            pool.wait_ge(asked, 1)
            pool.partition_all_reduce(cs_[:, :], cm[:, :], P, RMAX).then_inc(reduced, 1)
            with pool.Fori(0, NB // 2) as turn:
                for par in range(2):
                    b = turn * 2 + par
                    pool.tensor_tensor(c.h[:, ds(b * 2, 2), :], c.h[:, ds(b * 2, 2), :],
                                       c.bo[:, :].unsqueeze(1).broadcast_to([P, 2, D]), ALU.add)\
                        .then_inc(biased[par], 1)

        @block.vector
        def _(dve):
            link = Link(dve, own)
            link(dve.tensor_reduce(cm[:, :], c.cmax[:, :], AX.X, ALU.max))
            dve.sem_inc(asked, 1)
            dve.wait_ge(reduced, 1)
            scale_of(dve, link, cs_[:, :], cinv[:, :], ctmp[:, :])
            link(dve.tensor_scalar(wos[:, :], c.wvo[:, 1, :], cs_[:, :], None, ALU.mult))

            def quantise(par, turn):
                dve.wait_ge(cb_ready[par], turn + 1)
                dve.tensor_scalar(ci[:, par], c.ctx[:, ds((turn * 2 + par) * 2, 2), :], cinv[:, :], None, ALU.mult)\
                    .then_inc(ci_ready[par], 1)

            def results(par, turn):
                b = turn * 2 + par
                dve.wait_ge(o_done[par], turn + 1)
                dve.wait_ge(h_done[par], turn + 1)
                dve.tensor_tensor(out[:, par], po[par][:, :, :], wos[:, :].unsqueeze(1).broadcast_to([P, 2, D]),
                                  ALU.mult).then_inc(o_out[par], 1)
                dve.wait_ge(o_out[par], turn + 2)
                dve.wait_ge(biased[par], turn + 1)
                dve.tensor_tensor(c.h[:, ds(b * 2, 2), :], c.h[:, ds(b * 2, 2), :], out[:, par], ALU.add)\
                    .then_inc(h_done[par], 1)
                dve.wait_ge(h_done[par], turn + 2)
                for j in range(2):
                    dve.bn_stats(c.stats[:, ds(b * 2 + j, 1), :], c.h[:, ds(b * 2 + j, 1), :])

            ahead(dve, quantise, results, NB // 2)

        @block.scalar
        def _(act):
            with act.Fori(0, NB // 2) as turn:
                for par in range(2):
                    act.wait_ge(ci_ready[par], turn + 1)
                    act.wait_ge(cT_done[par], turn + 1)
                    act.activation(cb[:, par], ci[:, par], ACT.Copy).then_inc(cb_ready[par], 1)
                for par in range(2):
                    act.wait_ge(cT_done[par], turn + 2)
                    act.activation(cT[:, par], pT[par][:, :, :], ACT.Copy).then_inc(cT_out[par], 1)

        @block.tensor
        def _(pe):
            start_at(pe, 1, cT_done, cT_out, cb_ready, h_done, o_out)
            with pe.Fori(0, NB // 2) as turn:
                for par in range(2):
                    pe.wait_ge(cb_ready[par], turn + 2)
                    pe.wait_ge(cT_out[par], turn + 1)
                    for j in range(2):
                        for k in range(KD):
                            ins = pe.transpose(pT[par][:, k, j * P:(j + 1) * P], cb[:, par, j, k * P:(k + 1) * P],
                                               c.identb[:, :])
                    ins.then_inc(cT_done[par], 1)
                for par in range(2):
                    pe.wait_ge(cT_out[par], turn + 2)
                    pe.wait_ge(o_out[par], turn + 1)
                    for j in range(2):
                        for k in range(KD):
                            ins = pe.matmul(po[par][:, j, :], cT[:, par, k, j * P:(j + 1) * P], c.wT[:, 3, k, :],
                                            start=(k == 0), stop=(k == KD - 1))
                    ins.then_inc(o_done[par], 1)


def stage_router(nc, c):
    with ExitStack() as ctx:
        sb = lambda name, shape, dt: ctx.enter_context(nc.sbuf_tensor(name, shape, dt))
        sem = stage_semaphores(nc, ctx)
        pair = lambda name: [sem(name + "_a"), sem(name + "_b")]
        psum = lambda name, shape, dt: ctx.enter_context(nc.psum_tensor(name, shape, dt))
        xt = sb("xt10", [P, 2, 2, D], F32)
        xT = sb("xT10", [P, 2, KD, S], F32)
        RING = 8
        xs = sb("xs10", [P, RING, D], F32)
        rr = sb("rr10", [P, NT], F32)
        lg = sb("lg10", [P, NT, NE], F32)
        one_hot = sb("one_hot", [P, NT, NE], F32)
        one_hotb = sb("one_hotb", [P, NT, NE], BF16)
        work = sb("work10", [P, NT, NE], F32)
        row = sb("row10", [P, 2, NT], F32)
        count = sb("count10", [P, 2, NT, NE], F32)
        tiles_i, tiles = sb("tiles_i", [P, NE], I32), sb("tiles10", [P, NE], F32)
        start = sb("start10", [P, 2, NE], F32)
        slot_f = sb("slot_f", [P, NT], F32)
        number, number_i = sb("number10", [P, XT], F32), sb("number_i", [P, XT], I32)
        which, tile_f = sb("which10", [P, XT, NE], F32), sb("tile_f", [P, XT], F32)
        before = sb("before", [P, P], BF16)
        oneb = sb("oneb10", [P, P], BF16)
        pT = psum("pT10", [P, 2, KD, S], F32)
        pl = [psum(f"pl10{i}", [P, 2, NE], F32) for i in range(2)]
        prank, ptotal = psum("prank", [P, NT, NE], F32), psum("ptotal", [P, NT, NE], F32)
        own, sqa, sqd, consts, p_own = (sem(n) for n in ("own10", "sqa10", "sqd10", "consts10", "p_own10"))
        asked, expd, hot, ranked, slotted, xs_own, xs_ready = (
            sem(n) for n in ("asked10", "expd10", "hot10", "ranked10", "slotted", "xs_own", "xs_ready"))
        scattered = [sem(f"scattered{i}") for i in range(RING)]
        x_ready, xT_done, xT_out, l_done, l_out = (
            pair(n) for n in ("x_ready10", "xT_done10", "xT_out10", "l_done10", "l_out10"))
        block = ctx.enter_context(nc.Block())

        @block.gpsimd
        def _(pool):
            link = Link(pool, p_own)
            link(pool.iota(number_i[:, :], pattern=[[1, XT]], base=0, channel_multiplier=0))
            link(pool.tensor_copy(number[:, :], number_i[:, :]))
            link(pool.memset(oneb[:, :], 1.0))
            link(pool.affine_select(out=before[:, :], in_=oneb[:, :], compare_op=ALU.is_gt, fill=0.0, base=0,
                                    channel_multiplier=-1, pattern=[[1, P]]))
            pool.sem_inc(consts, 1)
            pool.wait_ge(slotted, 1)
            for t in range(NT):
                pool.wait_ge(xs_ready, t + 1)
                pool.indirect_dma_start(
                    out=c.sorted_x, out_offset=bass.IndirectOffsetOnAxis(ap=c.slot[:, t:t + 1], axis=0),
                    in_=xs[:, t % RING, :], in_offset=None).then_inc(scattered[t % RING], 16)
            for x in range(RING):
                pool.wait_ge(scattered[x], 16 * NT // RING)

        @block.sync
        def _(sp):
            i = c.ins
            for e in range(NE):
                sp.dma_start(c.ew2[:, e], i["L1_ffn_W2"][e].rearrange("(m p) d -> p m d", p=P))\
                    .then_inc(c.w2_in, 16)
                sp.dma_start(c.eb2[:, e, :], i["L1_ffn_b2"][e].partition_broadcast(P)).then_inc(c.w2_in, 16)

        @block.vector
        def _(dve):
            link = Link(dve, own)
            rstd_vector(dve, link, c, 1e-5, sqa, sqd, 1)
            link(dve.tensor_tensor(c.veps[:, :], c.rstd[:, :], c.rstd[:, :], ALU.mult))
            link(dve.tensor_tensor(c.veps[:, :], c.veps[:, :], c.var[:, :], ALU.mult))
            link(dve.tensor_scalar(c.veps[:, :], c.veps[:, :], 1e-5, None, ALU.add))
            root(dve, link, c, rr, sqa, sqd, 2)

            def normalise(par, turn):
                dve.wait_ge(xT_done[par], turn + 1)
                for j in range(2):
                    t = (turn * 2 + par) * 2 + j
                    ins = dve.tensor_scalar(xt[:, par, j, :], c.h[:, ds(t, 1), :], c.mean[:, ds(t, 1)],
                                            c.rstd[:, ds(t, 1)], ALU.subtract, ALU.mult)
                ins.then_inc(x_ready[par], 1)

            def logits(par, turn):
                dve.wait_ge(l_done[par], turn + 1)
                dve.tensor_tensor(lg[:, ds((turn * 2 + par) * 2, 2), :], pl[par][:, :, :],
                                  c.br[:, :].unsqueeze(1).broadcast_to([P, 2, NE]), ALU.add).then_inc(l_out[par], 1)

            ahead(dve, normalise, logits, NB // 2)
            for par in range(2):
                dve.wait_ge(l_out[par], NB // 2 + 1)
            wide = lambda a: a.unsqueeze(2).broadcast_to([P, NT, NE])
            link(dve.tensor_reduce(row[:, 0, :], lg[:, :, :], AX.X, ALU.max))
            link(dve.tensor_tensor(lg[:, :, :], lg[:, :, :], wide(row[:, 0, :]), ALU.subtract))
            dve.sem_inc(asked, 1)
            dve.wait_ge(expd, 1)
            link(dve.tensor_reduce(row[:, 1, :], work[:, :, :], AX.X, ALU.add))
            link(dve.reciprocal(row[:, 1, :], row[:, 1, :]))
            link(dve.tensor_tensor(work[:, :, :], work[:, :, :], wide(row[:, 1, :]), ALU.mult))
            link(dve.tensor_reduce(c.gate[:, :], work[:, :, :], AX.X, ALU.max))
            link(dve.tensor_tensor(work[:, :, :], work[:, :, :], wide(c.gate[:, :]), ALU.is_equal))
            dve.wait_ge(consts, 1)
            experts = number[:, 0:NE].unsqueeze(1).broadcast_to([P, NT, NE])
            link(dve.tensor_scalar(work[:, :, :], work[:, :, :], -float(NE), float(NE), ALU.mult, ALU.add))
            link(dve.tensor_tensor(work[:, :, :], work[:, :, :], experts, ALU.add))
            link(dve.tensor_reduce(row[:, 0, :], work[:, :, :], AX.X, ALU.min))
            link(dve.tensor_tensor(one_hot[:, :, :], wide(row[:, 0, :]), experts, ALU.is_equal))
            dve.tensor_copy(one_hotb[:, :, :], one_hot[:, :, :]).then_inc(hot, 1)
            dve.wait_ge(ranked, 1)
            link(dve.tensor_copy(count[:, 0], ptotal[:, :, :]))
            a, b, step = 0, 1, 1
            while step < NT:
                dve.tensor_copy(count[:, b, 0:step, :], count[:, a, 0:step, :])
                link(dve.tensor_tensor(count[:, b, step:, :], count[:, a, step:, :], count[:, a, :NT - step, :],
                                       ALU.add))
                a, b, step = b, a, step * 2
            link(dve.tensor_scalar(tiles_i[:, :], count[:, a, NT - 1, :], 1.0 / P, (P - 1) / 2 / P, ALU.mult,
                                   ALU.add))
            link(dve.tensor_copy(tiles[:, :], tiles_i[:, :]))
            link(dve.memset(start[:, 0, :], 0.0))
            for e in range(1, NE):
                link(dve.tensor_tensor(start[:, 0, e:e + 1], start[:, 0, e - 1:e], tiles[:, e - 1:e], ALU.add))
            link(dve.tensor_scalar(start[:, 1, :], start[:, 0, :], float(P), None, ALU.mult))
            link(dve.tensor_tensor(work[:, :, :], count[:, a], ptotal[:, :, :], ALU.subtract))
            link(dve.tensor_tensor(work[:, :, :], work[:, :, :], prank[:, :, :], ALU.add))
            link(dve.tensor_tensor(work[:, :, :], work[:, :, :],
                                   start[:, 1, :].unsqueeze(1).broadcast_to([P, NT, NE]), ALU.add))
            link(dve.tensor_tensor(work[:, :, :], work[:, :, :], one_hot[:, :, :], ALU.mult))
            link(dve.tensor_reduce(slot_f[:, :], work[:, :, :], AX.X, ALU.add))
            dve.tensor_copy(c.slot[:, :], slot_f[:, :]).then_inc(slotted, 1)
            link(dve.tensor_tensor(which[:, :, :], start[:, 0, :].unsqueeze(1).broadcast_to([P, XT, NE]),
                                   number[:, :].unsqueeze(2).broadcast_to([P, XT, NE]), ALU.is_le))
            link(dve.tensor_reduce(tile_f[:, :], which[:, :, :], AX.X, ALU.add))
            link(dve.tensor_scalar(c.tile_expert[:, :], tile_f[:, :], -1.0, None, ALU.add))
            link(dve.tensor_tensor(rr[:, :], rr[:, :], c.rstd[:, :], ALU.mult))
            for t in range(NT):
                x = xs[:, t % RING, :]
                if t >= RING:
                    dve.wait_ge(scattered[t % RING], 16 * (t // RING))
                dve.tensor_scalar(x, c.h[:, t, :], c.mean[:, t:t + 1], rr[:, t:t + 1], ALU.subtract, ALU.mult)\
                    .then_inc(xs_own, 1)
                dve.wait_ge(xs_own, 2 * t + 1)
                dve.tensor_tensor(x, x, c.ln_g[:, :], ALU.mult).then_inc(xs_own, 1)
                dve.wait_ge(xs_own, 2 * t + 2)
                dve.tensor_tensor(x, x, c.ln_b[:, :], ALU.add).then_inc(xs_ready, 1)

        @block.scalar
        def _(act):
            root_scalar(act, c, sqa, sqd, 1)
            root_scalar(act, c, sqa, sqd, 2)
            with act.Fori(0, NB // 2) as turn:
                for par in range(2):
                    act.wait_ge(xT_done[par], turn + 2)
                    act.activation(xT[:, par], pT[:, par], ACT.Copy).then_inc(xT_out[par], 1)
            act.wait_ge(asked, 1)
            act.activation(work[:, :, :], lg[:, :, :], ACT.Exp).then_inc(expd, 1)

        @block.tensor
        def _(pe):
            start_at(pe, 1, l_out, xT_done, xT_out)
            with pe.Fori(0, NB // 2) as turn:
                for par in range(2):
                    pe.wait_ge(x_ready[par], turn + 1)
                    pe.wait_ge(xT_out[par], turn + 1)
                    for j in range(2):
                        for k in range(KD):
                            ins = pe.transpose(pT[:, par, k, j * P:(j + 1) * P], xt[:, par, j, k * P:(k + 1) * P],
                                               c.ident[:, :])
                    ins.then_inc(xT_done[par], 1)
                for par in range(2):
                    pe.wait_ge(xT_out[par], turn + 2)
                    pe.wait_ge(l_out[par], turn + 1)
                    for j in range(2):
                        for k in range(KD):
                            ins = pe.matmul(pl[par][:, j, :], xT[:, par, k, j * P:(j + 1) * P], c.wr[:, k, :],
                                            start=(k == 0), stop=(k == KD - 1))
                    ins.then_inc(l_done[par], 1)
            pe.wait_ge(hot, 1)
            pe.wait_ge(consts, 1)
            hots = one_hotb[:, :, :].rearrange("p t e -> p (t e)")
            pe.matmul(ptotal[:, :, :].rearrange("p t e -> p (t e)"), oneb[:, :], hots, start=True, stop=True)
            pe.matmul(prank[:, :, :].rearrange("p t e -> p (t e)"), before[:, :], hots, start=True, stop=True)\
                .then_inc(ranked, 1)


def stage_experts(nc, c):
    FC = FF // P
    with ExitStack() as ctx:
        sb = lambda name, shape, dt: ctx.enter_context(nc.sbuf_tensor(name, shape, dt))
        sem = stage_semaphores(nc, ctx)
        psum = lambda name, shape, dt: ctx.enter_context(nc.psum_tensor(name, shape, dt))
        w1, w2, b1, b2 = c.ew1, c.ew2, c.eb1, c.eb2
        x = sb("x11", [P, 2, D], F32)
        xT = sb("xT11", [P, 2, KD, P], F32)
        w1_now = sb("w1_now", [P, 2, KD, FF], F32)
        b1_now = sb("b1_now", [P, 2, FC], F32)
        hT = sb("hT11", [P, 2, FC, P], F32)
        y = sb("y11", [P, 2, D], F32)
        pT = [psum(f"pT11{i}", [P, KD, P], F32) for i in range(2)]
        ph = [psum(f"ph11{i}", [P, 4, P], F32) for i in range(4)]
        py = [psum(f"py11{i}", [P, D], F32) for i in range(2)]
        x_in, y_out, y_stored = ([sem(f"{n}{i}") for i in range(2)] for n in ("x_in11", "y_out11", "y_stored11"))
        xT_done, xT_out, w_ready, h_done, h_out, y_done = (
            sem(n) for n in ("xT_done11", "xT_out11", "w_ready11", "h_done11", "h_out11", "y_done11"))
        block = ctx.enter_context(nc.Block())

        def tiles(eng, body):
            body(0, 0, 0, True)
            body(1, 1, 0, True)
            with eng.Fori(1, XT // 2) as turn:
                body(turn * 2, 0, turn, False)
                body(turn * 2 + 1, 1, turn, False)
            if XT % 2:
                body(XT - 1, 0, XT // 2, False)

        @block.sync
        def _(sp):
            def store(t, par, n):
                sp.wait_ge(y_out[par], n + 2)
                sp.dma_start(c.sorted_y[ds(t * P, P), :], y[:, par, :]).then_inc(y_stored[par], 16)

            tiles(sp, lambda t, par, n, first: store(t, par, n))
            for par in range(2):
                sp.wait_ge(y_stored[par], 16 * ((XT + 1 - par) // 2) + 16)

        @block.gpsimd
        def _(pool):
            def body(t, par, n, first):
                if not first:
                    pool.wait_ge(xT_done, t - 1)
                pool.dma_start(x[:, par, :], c.sorted_x[ds(t * P, P), :]).then_inc(x_in[par], 16)
            tiles(pool, body)

        @block.vector
        def _(dve):
            def body(t, par, n, first):
                e = dve.value_load(c.tile_expert[0:1, ds(t, 1)], min_val=0, max_val=NE - 1)
                if not first:
                    dve.wait_ge(h_done, t * 2 - 2)
                    dve.wait_ge(h_out, t * 2 - 2)
                elif par == 0:
                    dve.wait_ge(c.w2_in, 32 * NE)
                    dve.wait_ge(c.w1_in, 16 * (NE + 1))
                dve.tensor_copy(b1_now[:, par, :], b1[:, ds(e * FC, FC)])
                dve.tensor_copy(w1_now[:, par].rearrange("p k f -> p (k f)"),
                                w1[:, ds(e, 1)].rearrange("p a k f -> p (a k f)")).then_inc(w_ready, 1)
                if not first:
                    output(t - 2, par, n - 1)

            def output(t, par, n):
                e = dve.value_load(c.tile_expert[0:1, ds(t, 1)], min_val=0, max_val=NE - 1)
                dve.wait_ge(y_done, t + 1)
                dve.wait_ge(y_stored[par], n * 16 + 16)
                dve.tensor_tensor(y[:, par, :], py[par][:, :], b2[:, ds(e, 1)].rearrange("p a d -> p (a d)"), ALU.add)\
                    .then_inc(y_out[par], 1)

            tiles(dve, body)
            for t in (XT - 2, XT - 1):
                output(t, t % 2, t // 2)

        @block.scalar
        def _(act):
            def turned(t, par):
                act.wait_ge(xT_done, t + 1)
                act.activation(xT[:, par], pT[par][:, :, :], ACT.Copy).then_inc(xT_out, 1)

            def body(t, par, n, first):
                if first and par == 0:
                    turned(t, par)
                if not (isinstance(t, int) and t == XT - 1):
                    turned(t + 1, 1 - par)
                if not first:
                    act.wait_ge(y_done, t - 1)
                for half in range(2):
                    act.wait_ge(h_done, t * 2 + half + 1)
                    for q in range(4):
                        m = half * 4 + q
                        ins = act.activation(hT[:, par, m, :], ph[par * 2 + half][:, q, :], ACT.Relu,
                                             bias=b1_now[:, par, m:m + 1])
                    ins.then_inc(h_out, 1)
            tiles(act, body)

        @block.tensor
        def _(pe):
            start_at(pe, 1, y_out)
            start_at(pe, 16, y_stored)

            def expert(t):
                return pe.value_load(c.tile_expert[0:1, ds(t, 1)], min_val=0, max_val=NE - 1)

            def turn_x(t, par, n, first):
                pe.wait_ge(x_in[par], (n + 1) * 16)
                if not first:
                    pe.wait_ge(xT_out, t - 1)
                for k in range(KD):
                    ins = pe.transpose(pT[par][:, k, :], x[:, par, k * P:(k + 1) * P], c.ident[:, :])
                ins.then_inc(xT_done, 1)

            def second(t, par, e):
                for m in range(FC):
                    if m % 4 == 0:
                        pe.wait_ge(h_out, t * 2 + m // 4 + 1)
                    ins = pe.matmul(py[par][:, :], hT[:, par, m, :],
                                    w2[:, ds(e, 1), m, :].rearrange("p a d -> p (a d)"),
                                    start=(m == 0), stop=(m == FC - 1))
                ins.then_inc(y_done, 1)

            def body(t, par, n, first):
                if first and par == 0:
                    turn_x(0, 0, 0, True)
                pe.wait_ge(w_ready, t + 1)
                pe.wait_ge(xT_out, t + 1)
                if not first:
                    pe.wait_ge(h_out, t * 2 - 2)
                for m in range(FC):
                    if m == FC // 2 and not (first and par == 0):
                        e = expert(t - 1)
                    for k in range(KD):
                        ins = pe.matmul(ph[par * 2 + m // 4][:, m % 4, :], w1_now[:, par, k, m * P:(m + 1) * P],
                                        xT[:, par, k, :], start=(k == 0), stop=(k == KD - 1))
                    if m % 4 == 3:
                        ins.then_inc(h_done, 1)
                if not (isinstance(t, int) and t == XT - 1):
                    turn_x(t + 1, 1 - par, n if par == 0 else n + 1, first and par == 0)
                if first and par == 0:
                    pe.wait_ge(c.w2_in, 32 * NE)
                elif first:
                    second(0, 0, e)
                else:
                    pe.wait_ge(y_out[1 - par], n if par == 0 else n + 1)
                    second(t - 1, 1 - par, e)
            tiles(pe, body)
            pe.wait_ge(y_out[(XT - 1) % 2], (XT - 1) // 2 + 1)
            second(XT - 1, (XT - 1) % 2, expert(XT - 1))


def stage_output(nc, c):
    RING = 8
    with ExitStack() as ctx:
        sem = stage_semaphores(nc, ctx)
        y = ctx.enter_context(nc.sbuf_tensor("y12", [P, RING, D], F32))
        fetched = [sem(f"fetched{i}") for i in range(RING)]
        added, stored = sem("added12"), sem("stored12")
        block = ctx.enter_context(nc.Block())

        @block.gpsimd
        def _(pool):
            for t in range(NT):
                if t >= RING:
                    pool.wait_ge(added, t - RING + 1)
                pool.indirect_dma_start(
                    out=y[:, t % RING, :], out_offset=None, in_=c.sorted_y,
                    in_offset=bass.IndirectOffsetOnAxis(ap=c.slot[:, t:t + 1], axis=0))\
                    .then_inc(fetched[t % RING], 16)

        @block.vector
        def _(dve):
            for t in range(NT):
                dve.wait_ge(fetched[t % RING], 16 * (t // RING + 1))
                dve.scalar_tensor_tensor(out=c.h[:, t, :], in0=y[:, t % RING, :], scalar=c.gate[:, t:t + 1],
                                         in1=c.h[:, t, :], op0=ALU.mult, op1=ALU.add).then_inc(added, 1)

        @block.sync
        def _(sp):
            for b in range(NB):
                sp.wait_ge(added, b * 2 + 2)
                sp.dma_start(c.out[b].rearrange("(j p) d -> p j d", p=P), c.h[:, 2 * b:2 * b + 2, :])\
                    .then_inc(stored, 16)
            sp.wait_ge(stored, 16 * NB)


def expert_weights(nc, c):
    right = lambda name, shape, dt: c.ctx_all.enter_context(nc.sbuf_tensor(name, shape, dt, side="right"))
    c.ew1, c.eb1 = right("ew1", [P, NE, KD, FF], F32), right("eb1", [P, NE * FF // P], F32)
    c.w1_in, c.w2_in = (c.ctx_all.enter_context(nc.semaphore(n)) for n in ("w1_in11", "w2_in11"))


def second_layer_attention(nc, c):
    with ExitStack() as ctx:
        sb = lambda name, shape, dt: ctx.enter_context(nc.sbuf_tensor(name, shape, dt))
        dram = lambda name, shape, dt: nc.dram_tensor(name, shape, dt).ap()
        c.nv = sb("nv", [P, NT, D], BF16)
        c.qscale, c.vinv = sb("qscale", [P, 2 * NBLK + 1], F32), sb("vinv", [P, 1], F32)
        c.ex_dram = dram("ex_dram", (NB * PC, P, 1024), F32)
        c.sum_dram = dram("sum_dram", (NB, PC, 512), F32)
        with ExitStack() as proj:
            sb1 = lambda name, shape, dt: proj.enter_context(nc.sbuf_tensor(name, shape, dt))
            c.qk32, c.v32 = sb1("qk32", [P, 4, NB * S], F32), sb1("v32", [P, NT, D], F32)
            c.qs_row, c.qi_row = sb1("qs_row", [P, 2, S], F32), sb1("qi_row", [P, 2, S], F32)
            stage_l1_project(nc, c)
            stage_l1_quantise(nc, c)
        stage_l1_exponentials(nc, c)
        expert_weights(nc, c)
        c.inv_dram = dram("inv_dram", (3, NB, PC, 512), BF16)
        with ExitStack() as context:
            c.ctx = context.enter_context(nc.sbuf_tensor("ctx", [P, NT, D], F32))
            c.cmax = context.enter_context(nc.sbuf_tensor("cmax", [P, NB], F32))
            stage_l1_context(nc, c)
            stage_l1_output(nc, c)


def second_layer_ffn(nc, c):
    with ExitStack() as ctx:
        sb = lambda name, shape, dt: ctx.enter_context(nc.sbuf_tensor(name, shape, dt))
        c.gate, c.slot = sb("gate", [P, NT], F32), sb("slot", [P, NT], I32)
        c.tile_expert = sb("tile_expert", [P, XT], I32)
        right = lambda name, shape, dt: c.ctx_all.enter_context(nc.sbuf_tensor(name, shape, dt, side="right"))
        c.ew2, c.eb2 = right("ew2", [P, NE, FF // P, D], F32), right("eb2", [P, NE, D], F32)
        stage_router(nc, c)
        stage_experts(nc, c)
        stage_output(nc, c)


FIRST_LAYER = [stage_setup, stage_l0_project, stage_l0_attention, stage_l0_ffn]


def build(nc, ins, out):
    with ExitStack() as ctx:
        sb = lambda name, shape, dt: ctx.enter_context(nc.sbuf_tensor(name, shape, dt))
        dram = lambda name, shape, dt: nc.dram_tensor(name, shape, dt).ap()
        c = Core()
        c.ins, c.out, c.ctx_all = ins, out, ctx
        c.h = sb("h", [P, NT, D], F32)
        c.stats = sb("stats", [P, NT, 6], F32)
        c.mean, c.var, c.veps = (sb(n, [P, NT], F32) for n in ("mean", "var", "veps"))
        c.rstd, c.sd = sb("rstd", [P, NT], F32), sb("sd", [P, NT], F32)
        c.small = sb("small", [P, 2, NT], F32)
        c.ident, c.identb = sb("ident", [P, P], F32), sb("identb", [P, P], BF16)
        c.wr, c.br = sb("wr", [P, KD, NE], F32), sb("br", [P, NE], F32)
        c.ln_g, c.ln_b = sb("ln_g", [P, D], F32), sb("ln_b", [P, D], F32)
        c.qk_dram = dram("qk_dram", (NB, 3, 4 * P, S), BF16)
        c.sorted_x = dram("sorted_x", (XT * P, D), F32)
        c.sorted_y = dram("sorted_y", (XT * P, D), F32)
        with ExitStack() as attention:
            sb2 = lambda name, shape, dt: attention.enter_context(nc.sbuf_tensor(name, shape, dt))
            c.sel = sb2("sel", [3 * H, H, P], BF16)
            c.wT = sb2("wT", [P, 4, KD, D], BF16)
            c.wscale = sb2("wscale", [P, 8], F32)
            c.wvo = sb2("wvo", [P, 2, D], F32)
            c.bqk = sb2("bqk", [P, 4], F32)
            c.bv, c.bo = sb2("bv", [P, D], F32), sb2("bo", [P, D], F32)
            with ExitStack() as first:
                sb1 = lambda name, shape, dt: first.enter_context(nc.sbuf_tensor(name, shape, dt))
                c.wqkv, c.wo0 = sb1("wqkv", [P, KD, 3 * D], F32), sb1("wo0", [P, KD, D], F32)
                c.mask_qk, c.mask_kq = sb1("mask_qk", [P, 3, P], BF16), sb1("mask_kq", [P, 2, P], BF16)
                c.mask4 = sb1("mask4", [P, 4, 512], BF16)
                c.win = sb1("win", [P, KD, M_UNITS], F32)
                c.w1col, c.b1col, c.w2col = (sb1(n, [P, NBLK], F32) for n in ("w1col", "b1col", "w2col"))
                c.bin, c.b2u = sb1("bin", [M_UNITS, 1], F32), sb1("b2u", [M_UNITS, 1], F32)
                c.w2m, c.spread = sb1("w2m", [P, NBLK, M_UNITS], F32), sb1("spread", [M_UNITS, NBLK, P], F32)
                c.wout = sb1("wout", [M_UNITS + 1, D], F32)
                c.vaug = sb1("vaug", [P, NT, H, VA], F32)
                for stage in FIRST_LAYER:
                    stage(nc, c)
            second_layer_attention(nc, c)
        second_layer_ffn(nc, c)


COLUMNS = ("x", "L0_attn_g", "L0_ffn_W1", "L0_ffn_b1", "L0_ffn_W2", "L1_attn_bq", "L1_attn_bk", "L1_ffn_b1")


def kernel(**inputs):
    import concourse.bacc as bacc
    from concourse.bass_utils import run_bass_kernel_spmd

    nc = bacc.Bacc("TRN2", target_bir_lowering=False, num_devices=1)
    arrays, ins = {}, {}
    for name, value in inputs.items():
        a = np.asarray(value)
        if name == "L0_tok_weight":
            name, a = "table", a.T
        elif name in COLUMNS:
            a = a.reshape(-1, P).T
        a = np.ascontiguousarray(a)
        arrays["in_" + name] = a
        ins[name] = nc.dram_tensor("in_" + name, a.shape, mybir.dt.from_np(a.dtype), kind="ExternalInput").ap()
    out = nc.dram_tensor("out", (NB, S, D), F32, kind="ExternalOutput").ap()
    build(nc, ins, out)
    result = run_bass_kernel_spmd(nc, [arrays], core_ids=[0])
    return result.results[0]["out"]
```
